# Optimizing a Trainium2 kernel written in Bass

```python
import numpy as np
import jax
import jax.numpy as jnp

def _softmax(x, axis=-1):
    return jax.nn.softmax(x, axis=axis)

def _gelu(x):
    return jax.nn.gelu(x, approximate=True)

def _silu(x):
    return jax.nn.silu(x)

def _sigmoid(x):
    return jax.nn.sigmoid(x)

def _layernorm(x, axis=-1, eps=1e-05):
    m = jnp.mean(x, axis=axis, keepdims=True)
    v = jnp.var(x, axis=axis, keepdims=True)
    return (x - m) / jnp.sqrt(v + eps)

def _scatter_add(tgt, idx, src, axis=0):
    return tgt.at[idx].add(src)

def _segment_sum(src, seg, n):
    return jax.ops.segment_sum(src, seg, n)
kernel_name = 'mk_flamingo_gated_d2_seqx_r8_1a248c'

def setup_inputs(seed: int=0):
    np.random.seed(seed)
    _w = jnp.asarray

    def _rec_inputs():
        import jax
        import jax.numpy as jnp
        _rk = jax.random.key(seed)
        x = -0.0003929 + 0.9999 * jax.random.normal(jax.random.fold_in(_rk, 1), (64, 128, 128), jnp.float32)
        _lenS = 128 - jax.random.randint(jax.random.fold_in(_rk, 7), (64,), 0, max(1, 128 // 4) + 1, jnp.int32)
        _lenS2 = 77 - jax.random.randint(jax.random.fold_in(_rk, 8), (64,), 0, max(1, 77 // 4) + 1, jnp.int32)
        _ctx_1024P = jax.random.normal(jax.random.fold_in(_rk, 11), (64, 16, 128), jnp.float32)
        _ctx_1024c = jax.random.dirichlet(jax.random.fold_in(_rk, 511), 0.3 * jnp.ones((16,), jnp.float32), (64, 77))
        _ctx_1024t = jnp.einsum('bsk,bkd->bsd', _ctx_1024c, _ctx_1024P)
        _ctx_1024t = _ctx_1024t * jax.lax.rsqrt(jnp.mean(jnp.square(_ctx_1024t)) + 1e-12) * 0.953939
        ctx_1024 = 4.13588e-05 + 0.999923 * (_ctx_1024t + 0.3 * jax.random.normal(jax.random.fold_in(_rk, 611), (64, 77, 128), jnp.float32))
        _g = jax.random.normal(jax.random.fold_in(_rk, 9001), (2, 2), jnp.float32)
        _g = jnp.sign(_g) * jnp.maximum(jnp.abs(_g), 1.0) + (_g == 0) * 1.0
        g_xattn = _g[0]
        g_ffn = _g[1]
        return (x, ctx_1024, g_xattn, g_ffn)
    x, ctx_1024, g_xattn, g_ffn = _rec_inputs()

    def _L0_xattn_setup():
        import jax, jax.numpy as jnp
        import numpy as np
        DIM = 128
        HEADS = 8
        DIM_HEAD = 64
        INNER = HEADS * DIM_HEAD
        SCALE = DIM_HEAD ** (-0.5)
        EPS = 1e-05

        def _layernorm(x, gamma, beta):
            mu = jnp.mean(x, axis=-1, keepdims=True)
            var = jnp.var(x, axis=-1, keepdims=True)
            return (x - mu) * jax.lax.rsqrt(var + EPS) * gamma + beta
        key = jax.random.key(seed)
        ks = jax.random.split(key, 6)
        x = jax.random.normal(ks[0], (4, 512, DIM), dtype=jnp.float32)
        media = jax.random.normal(ks[1], (4, 256, DIM), dtype=jnp.float32)
        gamma = jnp.ones((DIM,), dtype=jnp.float32)
        beta = jnp.zeros((DIM,), dtype=jnp.float32)
        Wq = jax.random.normal(ks[2], (DIM, INNER), dtype=jnp.float32) * DIM ** (-0.5)
        Wkv = jax.random.normal(ks[3], (DIM, 2 * INNER), dtype=jnp.float32) * DIM ** (-0.5)
        Wout = jax.random.normal(ks[4], (INNER, DIM), dtype=jnp.float32) * INNER ** (-0.5)
        return {'x': x, 'media': media, 'gamma': gamma, 'beta': beta, 'Wq': Wq, 'Wkv': Wkv, 'Wout': Wout}
    _L0_xattn_all = _L0_xattn_setup()
    _L0_xattn_in = {k: v for k, v in _L0_xattn_all.items() if k in ('gamma', 'beta', 'Wq', 'Wkv', 'Wout')}
    del _L0_xattn_all

    def _L0_ffn_setup():
        import jax, jax.numpy as jnp
        import numpy as np
        D_MODEL, EXPERT_DIM, NUM_EXPERTS, TOP_K = (128, 256, 16, 2)
        SEQ_LEN, BATCH = (256, 2)
        key = jax.random.key(seed)
        ks = jax.random.split(key, 8)
        s_d = 1.0 / np.sqrt(D_MODEL)
        s_h = 1.0 / np.sqrt(EXPERT_DIM)
        return {'x': jax.random.normal(ks[0], (SEQ_LEN, BATCH, D_MODEL), jnp.float32), 'Wg': jax.random.uniform(ks[1], (D_MODEL, NUM_EXPERTS), jnp.float32, -s_d, s_d), 'bg': jax.random.uniform(ks[2], (NUM_EXPERTS,), jnp.float32, -s_d, s_d), 'bias': jnp.zeros((NUM_EXPERTS,), jnp.float32), 'W1': jax.random.uniform(ks[3], (NUM_EXPERTS, D_MODEL, EXPERT_DIM), jnp.float32, -s_d, s_d), 'b1': jax.random.uniform(ks[4], (NUM_EXPERTS, EXPERT_DIM), jnp.float32, -s_d, s_d), 'W2': jax.random.uniform(ks[5], (NUM_EXPERTS, EXPERT_DIM, D_MODEL), jnp.float32, -s_h, s_h), 'b2': jax.random.uniform(ks[6], (NUM_EXPERTS, D_MODEL), jnp.float32, -s_h, s_h)}
    _L0_ffn_all = _L0_ffn_setup()
    _L0_ffn_in = {k: v for k, v in _L0_ffn_all.items() if k in ('Wg', 'bg', 'bias', 'W1', 'b1', 'W2', 'b2')}
    del _L0_ffn_all

    def _L1_xattn_setup():
        import jax, jax.numpy as jnp
        import numpy as np
        D_MODEL = 128
        NUM_HEADS = 16
        D_K = D_MODEL // NUM_HEADS
        B, S = (4, 256)
        key = jax.random.key(seed)
        ks = jax.random.split(key, 11)
        scale = 1.0 / np.sqrt(D_MODEL)
        inp = {'query': jax.random.normal(ks[0], (B, S, D_MODEL), dtype=jnp.float32), 'key': jax.random.normal(ks[1], (B, S, D_MODEL), dtype=jnp.float32), 'value': jax.random.normal(ks[2], (B, S, D_MODEL), dtype=jnp.float32), 'Wq': jax.random.normal(ks[3], (D_MODEL, D_MODEL), dtype=jnp.float32) * scale, 'bq': jnp.zeros((D_MODEL,), dtype=jnp.float32), 'Wk': jax.random.normal(ks[4], (D_MODEL, D_MODEL), dtype=jnp.float32) * scale, 'bk': jnp.zeros((D_MODEL,), dtype=jnp.float32), 'Wv': jax.random.normal(ks[5], (D_MODEL, D_MODEL), dtype=jnp.float32) * scale, 'bv': jnp.zeros((D_MODEL,), dtype=jnp.float32), 'Wo': jax.random.normal(ks[6], (D_MODEL, D_MODEL), dtype=jnp.float32) * scale, 'bo': jnp.zeros((D_MODEL,), dtype=jnp.float32)}
        return inp
    _L1_xattn_all = _L1_xattn_setup()
    _L1_xattn_in = {k: v for k, v in _L1_xattn_all.items() if k in ('Wq', 'bq', 'Wk', 'bk', 'Wv', 'bv', 'Wo', 'bo')}
    del _L1_xattn_all

    def _L1_ffn_setup():
        import jax, jax.numpy as jnp
        import numpy as np
        FEATURES = 128
        D_IN = 128

        def fp8_gemm_optimized(x, input_scale, kernel, kernel_scale):
            s_in = input_scale[0]
            s_k = kernel_scale[0]
            x_q = (x.astype(jnp.float32) / s_in).astype(jnp.float8_e4m3fn)
            k_q = (kernel.astype(jnp.float32) / s_k).astype(jnp.float8_e4m3fn)
            y = jnp.dot(x_q.astype(jnp.float32), k_q.astype(jnp.float32), preferred_element_type=jnp.float32)
            return y * (s_in * s_k)
        key = jax.random.key(seed)
        kx, kk, kb = jax.random.split(key, 3)
        x = jax.random.normal(kx, (4, 1024, D_IN), dtype=jnp.float32)
        limit = np.sqrt(6.0 / (D_IN + FEATURES)).astype(np.float32)
        kernel = jax.random.uniform(kk, (D_IN, FEATURES), dtype=jnp.float32, minval=-limit, maxval=limit).astype(jnp.bfloat16)
        input_scale = jnp.ones((1,), dtype=jnp.float32)
        kernel_scale = jnp.ones((1,), dtype=jnp.float32)
        bias = jnp.zeros((FEATURES,), dtype=jnp.bfloat16)
        return {'x': x, 'kernel': kernel, 'input_scale': input_scale, 'kernel_scale': kernel_scale, 'bias': bias}
    _L1_ffn_all = _L1_ffn_setup()
    _L1_ffn_in = {k: v for k, v in _L1_ffn_all.items() if k in ('kernel', 'input_scale', 'kernel_scale', 'bias')}
    del _L1_ffn_all
    return {'x': x, 'ctx_1024': ctx_1024, 'g_xattn': g_xattn, 'g_ffn': g_ffn, 'L0_xattn_gamma': _L0_xattn_in['gamma'], 'L0_xattn_beta': _L0_xattn_in['beta'], 'L0_xattn_Wq': _L0_xattn_in['Wq'], 'L0_xattn_Wkv': _L0_xattn_in['Wkv'], 'L0_xattn_Wout': _L0_xattn_in['Wout'], 'L0_ffn_Wg': _L0_ffn_in['Wg'], 'L0_ffn_bg': _L0_ffn_in['bg'], 'L0_ffn_bias': _L0_ffn_in['bias'], 'L0_ffn_W1': _L0_ffn_in['W1'], 'L0_ffn_b1': _L0_ffn_in['b1'], 'L0_ffn_W2': _L0_ffn_in['W2'], 'L0_ffn_b2': _L0_ffn_in['b2'], 'L1_xattn_Wq': _L1_xattn_in['Wq'], 'L1_xattn_bq': _L1_xattn_in['bq'], 'L1_xattn_Wk': _L1_xattn_in['Wk'], 'L1_xattn_bk': _L1_xattn_in['bk'], 'L1_xattn_Wv': _L1_xattn_in['Wv'], 'L1_xattn_bv': _L1_xattn_in['bv'], 'L1_xattn_Wo': _L1_xattn_in['Wo'], 'L1_xattn_bo': _L1_xattn_in['bo'], 'L1_ffn_kernel': _L1_ffn_in['kernel'], 'L1_ffn_input_scale': _L1_ffn_in['input_scale'], 'L1_ffn_kernel_scale': _L1_ffn_in['kernel_scale'], 'L1_ffn_bias': _L1_ffn_in['bias']}

def reference(x, ctx_1024, g_xattn, g_ffn, L0_xattn_gamma, L0_xattn_beta, L0_xattn_Wq, L0_xattn_Wkv, L0_xattn_Wout, L0_ffn_Wg, L0_ffn_bg, L0_ffn_bias, L0_ffn_W1, L0_ffn_b1, L0_ffn_W2, L0_ffn_b2, L1_xattn_Wq, L1_xattn_bq, L1_xattn_Wk, L1_xattn_bk, L1_xattn_Wv, L1_xattn_bv, L1_xattn_Wo, L1_xattn_bo, L1_ffn_kernel, L1_ffn_input_scale, L1_ffn_kernel_scale, L1_ffn_bias):
    import jax
    import jax.numpy as jnp

    def _L0_xattn_ref(x, media, gamma, beta, Wq, Wkv, Wout):
        import jax, jax.numpy as jnp
        import numpy as np
        DIM = 128
        HEADS = 8
        DIM_HEAD = 64
        INNER = HEADS * DIM_HEAD
        SCALE = DIM_HEAD ** (-0.5)
        EPS = 1e-05

        def _layernorm(x, gamma, beta):
            mu = jnp.mean(x, axis=-1, keepdims=True)
            var = jnp.var(x, axis=-1, keepdims=True)
            return (x - mu) * jax.lax.rsqrt(var + EPS) * gamma + beta
        b, n, _ = x.shape
        j = media.shape[1]
        xn = _layernorm(x, gamma, beta)
        q = xn @ Wq
        kv = media @ Wkv
        k, v = jnp.split(kv, 2, axis=-1)
        q = q.reshape(b, n, HEADS, DIM_HEAD).transpose(0, 2, 1, 3) * SCALE
        k = k.reshape(b, j, HEADS, DIM_HEAD).transpose(0, 2, 1, 3)
        v = v.reshape(b, j, HEADS, DIM_HEAD).transpose(0, 2, 1, 3)
        sim = jnp.einsum('bhid,bhjd->bhij', q, k)
        sim = sim - jax.lax.stop_gradient(jnp.max(sim, axis=-1, keepdims=True))
        attn = jax.nn.softmax(sim, axis=-1)
        out = jnp.einsum('bhij,bhjd->bhid', attn, v)
        out = out.transpose(0, 2, 1, 3).reshape(b, n, INNER)
        return out @ Wout

    def _L0_ffn_ref(x, Wg, bg, bias, W1, b1, W2, b2):
        import jax, jax.numpy as jnp
        import numpy as np
        D_MODEL, EXPERT_DIM, NUM_EXPERTS, TOP_K = (128, 256, 16, 2)
        SEQ_LEN, BATCH = (256, 2)
        logits = jnp.einsum('sbd,de->sbe', x, Wg) + bg + bias
        vals, idx = jax.lax.top_k(logits, TOP_K)
        w = jax.nn.softmax(vals - jnp.max(vals, axis=-1, keepdims=True), axis=-1)
        cw = jnp.einsum('sbk,sbke->sbe', w, jax.nn.one_hot(idx, NUM_EXPERTS, dtype=x.dtype))
        h = jax.nn.relu(jnp.einsum('sbd,edh->esbh', x, W1) + b1[:, None, None, :])
        y = jnp.einsum('esbh,ehd->esbd', h, W2) + b2[:, None, None, :]
        out = jnp.einsum('esbd,sbe->sbd', y, cw)
        return out

    def _L1_xattn_ref(query, key, value, Wq, bq, Wk, bk, Wv, bv, Wo, bo):
        import jax, jax.numpy as jnp
        import numpy as np
        D_MODEL = 128
        NUM_HEADS = 16
        D_K = D_MODEL // NUM_HEADS
        B, S = (4, 256)
        b, sq, _ = query.shape
        sk = key.shape[1]
        Q = query @ Wq + bq
        K = key @ Wk + bk
        V = value @ Wv + bv
        Q = Q.reshape(b, sq, NUM_HEADS, D_K).transpose(0, 2, 1, 3)
        K = K.reshape(b, sk, NUM_HEADS, D_K).transpose(0, 2, 1, 3)
        V = V.reshape(b, sk, NUM_HEADS, D_K).transpose(0, 2, 1, 3)
        scores = jnp.einsum('bhqd,bhkd->bhqk', Q, K) / jnp.sqrt(jnp.float32(D_K))
        attn = jax.nn.softmax(scores, axis=-1)
        out = jnp.einsum('bhqk,bhkd->bhqd', attn, V)
        out = out.transpose(0, 2, 1, 3).reshape(b, sq, D_MODEL)
        return out @ Wo + bo

    def _L1_ffn_ref(x, kernel, input_scale, kernel_scale, bias):
        import jax, jax.numpy as jnp
        import numpy as np
        FEATURES = 128
        D_IN = 128

        def fp8_gemm_optimized(x, input_scale, kernel, kernel_scale):
            s_in = input_scale[0]
            s_k = kernel_scale[0]
            x_q = (x.astype(jnp.float32) / s_in).astype(jnp.float8_e4m3fn)
            k_q = (kernel.astype(jnp.float32) / s_k).astype(jnp.float8_e4m3fn)
            y = jnp.dot(x_q.astype(jnp.float32), k_q.astype(jnp.float32), preferred_element_type=jnp.float32)
            return y * (s_in * s_k)
        dtype = jnp.bfloat16
        x = x.astype(dtype)
        orig_shape = x.shape
        x2 = x.reshape(-1, x.shape[-1])
        y = fp8_gemm_optimized(x2, input_scale, kernel, kernel_scale)
        y = y.astype(dtype) + bias
        return y.reshape(orig_shape[:-1] + (FEATURES,))
    x = x + jnp.tanh(g_xattn[0]) * _L0_xattn_ref(_layernorm(x, axis=-1), ctx_1024, L0_xattn_gamma, L0_xattn_beta, L0_xattn_Wq, L0_xattn_Wkv, L0_xattn_Wout)
    x = x + jnp.tanh(g_ffn[0]) * _L0_ffn_ref(_layernorm(x, axis=-1), L0_ffn_Wg, L0_ffn_bg, L0_ffn_bias, L0_ffn_W1, L0_ffn_b1, L0_ffn_W2, L0_ffn_b2)
    x = x + jnp.tanh(g_xattn[1]) * _L1_xattn_ref(_layernorm(x, axis=-1), ctx_1024, ctx_1024, L1_xattn_Wq, L1_xattn_bq, L1_xattn_Wk, L1_xattn_bk, L1_xattn_Wv, L1_xattn_bv, L1_xattn_Wo, L1_xattn_bo)
    x = x + jnp.tanh(g_ffn[1]) * _L1_ffn_ref(_layernorm(x, axis=-1), L1_ffn_kernel, L1_ffn_input_scale, L1_ffn_kernel_scale, L1_ffn_bias)
    return x

_drawn_inputs = setup_inputs


def setup_inputs(seed=0):
    import zlib

    import numpy as np

    out = dict(_drawn_inputs(seed))
    spreads = {'g_ffn': (-1.0, 0.2),
     'L0_xattn_gamma': (1.0, 0.2),
     'L0_xattn_beta': (0.0, 0.297),
     'L0_ffn_bias': (0.0, 0.1),
     'L1_xattn_bq': (0.0, 0.333),
     'L1_xattn_bk': (0.0, 0.8),
     'L1_xattn_bv': (0.0, 0.1),
     'L1_xattn_bo': (0.0, 0.1),
     'L1_ffn_bias': (0.0, 0.1)}
    factors = {'L0_ffn_b1': 4.159, 'L0_ffn_b2': 2.741}
    for name, (base, spread) in spreads.items():
        noise = np.random.default_rng([zlib.crc32(name.encode()), seed]).standard_normal(out[name].shape)
        drawn = base * np.exp(spread * noise) if base else spread * noise
        out[name] = jnp.asarray(drawn.astype(out[name].dtype))
    for name, factor in factors.items():
        out[name] = (out[name] * factor).astype(out[name].dtype)
    return out
```

```python
import concourse.bass as bass
from concourse import mybir
from contextlib import ExitStack

F32 = mybir.dt.float32
BF16 = mybir.dt.bfloat16
I32 = mybir.dt.int32
ALU = mybir.AluOpType
ACT = mybir.ActivationFunctionType
X = mybir.AxisListType.X
P = 128


class Step:

    def __init__(self, value, parity, count):
        self.value, self.parity, self.count = value, parity, count

    def at(self, lag):
        if isinstance(self.value, int):
            b = self.value - lag
            return b if 0 <= b < self.count else None
        return self.value - lag

    def par(self, lag):
        return (self.parity - lag) % 2

    def seen(self, lag, now=0):
        n = self.value - lag + now
        return min(max(n, 0), self.count) if isinstance(n, int) else n


def run_steps(engine, count, first, last, peeled, body):
    if peeled:
        for t in range(first, last):
            body(Step(t, t % 2, count))
    else:
        assert first % 2 == 0 and last % 2 == 0
        with engine.Fori(first // 2, last // 2) as turn:
            for p in range(2):
                body(Step(turn * 2 + p, p, count))


def wait_free(engine, sem, value):
    if isinstance(value, int) and value <= 0:
        return
    engine.wait_ge(sem, value)


def flamingo_two_layers(nc, a, out, xs_dram, ys_dram):
    NB, N, D = a["x"].shape
    J = a["ctxT"].shape[2]
    H0 = 8
    DH0 = a["WqT"].shape[0]
    HD0 = H0 * DH0
    H1, DH1 = 16, D // 16
    NE, EH = a["b1"].shape
    EPS = 1e-5
    NCH = 2
    CB = NB // NCH
    NT = (2 * CB * N + NE * (P - 1)) // P
    NT += NT % 2
    HB0 = H0 // 2
    VW0 = DH0 + 1
    VW1 = DH1 + 1
    GH = 4
    NG = H1 // GH
    LOOP0 = 8
    LAST_LAG_A = 6
    LAST_LAG_B = 4
    LAST_LAG_C = 9
    LOOPC = 12
    ROUTE0 = CB + LAST_LAG_A
    assert ROUTE0 % 2 == 0

    ctx = ExitStack()
    with ctx:
        def sb(name, shape, dt=F32):
            return ctx.enter_context(nc.sbuf_tensor(name, shape, dt))

        def sem(name):
            return ctx.enter_context(nc.semaphore(name))

        XR = sb("residual", [P, NB, D])
        XN = sb("moe_in", [P, NB, D])
        W1s = sb("w1", [P, NE, EH])
        W2s = sb("w2", [P, NE, 2, D])
        b1s = sb("b1_rows", [P, NE, EH])
        b2s = sb("b2_rows", [P, NE, D])
        LG = sb("logits", [P, NB, NE])
        WT = [sb(f"gate_w{k}", [P, NB]) for k in range(2)]
        POS = [sb(f"slot{k}", [P, NB], I32) for k in range(2)]
        ETI = sb("tile_expert", [1, NCH, P], I32)
        ident = sb("ident", [P, P])
        identb = sb("identb", [P, P], BF16)
        ltri = sb("before", [P, P], BF16)
        onesb = sb("onesb", [P, P], BF16)
        iotaD = sb("rank_of_expert", [P, NE])
        tau = sb("tile_start", [P, 1])
        nfirst = sb("not_first", [P, NE, CB])
        mask4 = sb("head_of_row", [P, GH])
        mhalf = sb("minus_half", [P, 1])
        tg = sb("tanh_gates", [P, 4])
        gamma = sb("gamma", [P, 1])
        beta = sb("beta", [P, 1])
        wgs = sb("wg", [P, NE])
        lbias = sb("logit_bias", [P, 2, NE])
        T0 = sb("wk_wq", [P, H0, D])
        wv0 = sb("wv0", [P, HD0])
        wo0 = sb("wo0", [P, HD0 // P, D])
        wq1 = sb("wq1", [P, D])
        wk1 = sb("wk1", [P, D])
        wv1 = sb("wv1", [P, D])
        wo1 = sb("wo1", [P, D])
        bq1 = sb("bq1", [P, 1])
        bk1 = sb("bk1", [P, 1])
        bv1 = sb("bv1", [P, D])
        bo1 = sb("bo1", [P, D])
        kf = sb("ffn_kernel", [P, D], BF16)
        kq = sb("ffn_kernel_q", [P, D], BF16)
        sc = sb("ffn_scales", [P, 2])
        scr = sb("ffn_rscales", [P, 2])
        scm = sb("ffn_scale_product", [P, 1])
        fbias = sb("ffn_bias", [P, D], BF16)
        zt = sb("zeros", [P, 512])

        PS = ctx.enter_context(nc.psum_tensor("PS", [P, 8, 512], F32))

        AW = 14400
        arena = sb("arena", [P, AW])

        class Carver:
            def __init__(self):
                self.at = 0

            def __call__(self, width, parts=P):
                v = arena[0:parts, self.at:self.at + width]
                self.at += width
                assert self.at <= AW, self.at
                return v

        ca = Carver()
        one16 = ca(NE)
        scat = [ca(D) for _ in range(2)]
        si = [ca(1).bitcast(I32) for _ in range(4)]
        after_scatter = ca.at
        ctxa = [ca(J) for _ in range(2)]
        mv1 = [ca(2) for _ in range(2)]
        st1 = ca(6)
        rs1 = [ca(2) for _ in range(2)]
        xn1 = [ca(D) for _ in range(2)]
        xT1 = [ca(D) for _ in range(2)]
        KA = [ca(H0 * J) for _ in range(2)]
        V0 = [ca(H0 * VW0, J) for _ in range(2)]
        S0 = [ca(H0 * J) for _ in range(2)]
        P0 = [ca(H0 * J) for _ in range(2)]
        mx0 = ca(H0)
        PT0 = [ca(H0 * P, J) for _ in range(2)]
        rd0 = ca(H0)
        O0 = [ca(HD0) for _ in range(2)]
        OT0 = [ca(HD0) for _ in range(2)]
        mv2 = [ca(2) for _ in range(2)]
        st2 = ca(6)
        rs2 = [ca(2) for _ in range(2)]
        xn2 = [ca(D) for _ in range(2)]
        xT2 = [ca(D) for _ in range(2)]
        after_a = ca.at
        rt = {}
        for name, width in (("v0", CB), ("v1", CB), ("eq", CB * NE), ("m", CB), ("oh0", CB * NE),
                            ("oh1", CB * NE), ("lg2", CB * NE), ("e", CB), ("s", CB), ("cum", NE * CB),
                            ("pos", NE * CB), ("tot", NE), ("pad", NE), ("inc", NE), ("base", NE),
                            ("et", 1), ("le", NE)):
            rt[name] = ca(width)
        rtM = ca(NE * CB // 2).bitcast(BF16)
        rti = ca(NE).bitcast(I32)
        cb = Carver()
        cb.at = after_scatter
        xsb = [cb(D) for _ in range(2)]
        xsT = [cb(D) for _ in range(2)]
        hb = [cb(EH) for _ in range(2)]
        hT = [cb(EH) for _ in range(2)]
        yb = [cb(D) for _ in range(2)]
        cc = Carver()
        gy = [[cc(D) for _ in range(2)] for _ in range(2)]
        gi = [[cc(1).bitcast(I32) for _ in range(2)] for _ in range(2)]
        ctxc = [cc(J) for _ in range(2)]
        uc = cc(D)
        mv3 = [cc(2) for _ in range(2)]
        st3 = cc(6)
        rs3 = [cc(2) for _ in range(2)]
        xn3 = [cc(D) for _ in range(2)]
        xT3 = [cc(D) for _ in range(2)]
        QT1 = [cc(D) for _ in range(2)]
        KB1 = [cc(GH * J) for _ in range(2)]
        V1 = [cc(H1 * VW1, J) for _ in range(2)]
        S1 = cc(H1 * J)
        P1 = [cc(H1 * J) for _ in range(2)]
        mx1 = cc(H1)
        PT1 = cc(H1 * P, J)
        rd1 = cc(H1)
        O1 = [cc(D) for _ in range(2)]
        OT1 = [cc(D) for _ in range(2)]
        mv4 = [cc(2) for _ in range(2)]
        st4 = cc(6)
        rs4 = [cc(2) for _ in range(2)]
        xb4 = cc(D // 2).bitcast(BF16)
        z4 = [cc(D) for _ in range(2)]
        c4 = [cc(D) for _ in range(2)]
        q4 = cc(D)
        n4 = cc(D)
        t4 = cc(D)
        xq4 = [cc(D // 2).bitcast(BF16) for _ in range(2)]
        xqT4 = [cc(D // 2).bitcast(BF16) for _ in range(2)]
        y4 = [cc(D // 2).bitcast(BF16) for _ in range(2)]
        y4b = [cc(D // 2).bitcast(BF16) for _ in range(2)]
        ob = [cc(D) for _ in range(2)]
        cs = Carver()
        cs.at = after_a
        wqT = cs(H0 * D, DH0)
        wkT = cs(H0 * D, DH0)
        ksz = cs(D)
        ksc = cs(D)
        ksq = cs(D)

        names = """w_loaded moe_loaded ms consts ident_made tau_made mask_made
            t0_mm t0_cp tanh_made kq_step kq_made zero_made xs_zeroed setup_dve
            x_loaded ctx_loaded stats1 agg1 rst1 rs1_made xn1_made xT1_mm xT1_cp KA_mm KA_cp V0_mm V0_cp S0_mm mx0_made
            S0_sub exp0 PT0_mm PT0_cpa PT0_cpb O0_mm rd0_made O0_cp OT0_mm OT0_cp Y0_mm x1_made
            stats2 agg2 rst2 rs2_made xn2_made XN_kept xT2_mm xT2_cp lg_mm lg_made
            ro ro_M ro_e ro_cnt ro_et ro_done ro_exp idx_made scat_made0 scat_made1
            xs_loaded0 xs_loaded1 xsT_mm xsT_cp h_mm h_made hT_mm hT_cp y_mm y_made ys_stored0 ys_stored1
            gi_made gy_made0 gy_made1 ctxc_loaded u_made x2_made x2b_made stats3 agg3 rst3 rs3_made xn3_made xT3_mm xT3_cp
            QT_mm QT_cp KT_mm KB_made V1_mm V1_cp S1_mm mx1_made S1_sub exp1
            PT1_mm PT1_cpa PT1_cpb O1_mm rd1_made O1_cp OT1_mm OT1_cp Y1_mm x3_made stats4 agg4 rst4 rs4_made xb4_made
            z4_made m4_made c4_made t4_made q4_made n4_made xq4_made xqT_mm xqT_cp y4_mm y4_made y4b_made ob_made out_stored0 out_stored1""".split()
        s = {n: sem(n) for n in names}

        block = ctx.enter_context(nc.Block())

        xs_flat = [xs_dram[c] for c in range(NCH)]
        ys_flat = [ys_dram[c] for c in range(NCH)]
        x_rows = a["x"].rearrange("b n d -> (b n) d")
        out_rows = out.rearrange("b n d -> (b n) d")
        ctx_rows = a["ctxT"].rearrange("b d j -> (b d) j")

        def apart(engine):
            engine.nop(nofuse=True)

        def row(ap, parts=P):
            return ap.rearrange("(o n) -> o n", o=1).to_broadcast([parts, ap.shape[0]])

        def col(ap):
            return ap.rearrange("(n o) -> n o", o=1)

        def route_spans():
            return [(0, LOOP0, True), (LOOP0, ROUTE0, False), None,
                    (ROUTE0, ROUTE0 + 2, True), (ROUTE0 + 2, NB, False),
                    (NB, NB + LAST_LAG_A, True)]

        def spans(count, lead, lag):
            return [(0, lead, True), (lead, count, False), (count, count + lag, True)]

        def c_spans():
            return [(0, LOOPC, True), (LOOPC, CB, False), (CB, NB, False), (NB, NB + LAST_LAG_C, True)]

        loads = [(wqT, a["WqT"]), (wkT, a["WkT"]), (gamma[:, :], col(a["gamma"])), (beta[:, :], col(a["beta"])),
                 (wv0[:, :], a["Wv"]), (wo0[:, :, :], a["Wout"].rearrange("(c p) n -> p c n", p=P)),
                 (tg[:, 0:2], row(a["g_xattn"])), (tg[:, 2:4], row(a["g_ffn"])),
                 (wgs[:, :], a["Wg"]), (lbias[:, 0, :], row(a["bg"])), (lbias[:, 1, :], row(a["bias"])),
                 (wq1[:, :], a["Wq1"]), (wk1[:, :], a["Wk1"]), (wv1[:, :], a["Wv1"]), (wo1[:, :], a["Wo1"]),
                 (bq1[:, :], col(a["bq1"])), (bk1[:, :], col(a["bk1"])), (bv1[:, :], row(a["bv1"])),
                 (bo1[:, :], row(a["bo1"])), (kf[:, :], a["kernel"]), (sc[:, 0:1], row(a["input_scale"])),
                 (sc[:, 1:2], row(a["kernel_scale"])), (fbias[:, :], row(a["ffn_bias"]))]

        @block.sync
        def _(sp):
            def load_x(b):
                wait_free(sp, s["x_loaded"], b * 16)
                sp.dma_start(XR[:, bass.ds(b, 1), :].rearrange("p o d -> p (o d)"),
                             x_rows[bass.ds(b * N, N), :]).then_inc(s["x_loaded"], 16)

            def load_ctx(b, dst, loaded, free):
                wait_free(sp, s[loaded], b * 16)
                apart(sp)
                wait_free(sp, s[free], b - 1)
                sp.dma_start(dst, ctx_rows[bass.ds(b * D, D), :]).then_inc(s[loaded], 16)

            load_x(0)
            load_x(1)
            load_ctx(0, ctxa[0], "ctx_loaded", "V0_mm")
            for dst, src in loads:
                sp.dma_start(dst, src).then_inc(s["w_loaded"], 16)
            load_ctx(1, ctxa[1], "ctx_loaded", "V0_mm")
            with sp.Fori(1, NB // 2) as turn:
                for p in range(2):
                    load_x(turn * 2 + p)
                    load_ctx(turn * 2 + p, ctxa[p], "ctx_loaded", "V0_mm")
            for c in range(NCH):
                sp.wait_ge(s["xs_zeroed"], 16 * NCH)
                for p in range(2):
                    sp.wait_ge(s[f"scat_made{p}"], 16 * CB * (c + 1))

                def load_tile(t, p):
                    tt = t + c * NT
                    wait_free(sp, s[f"xs_loaded{p}"], (tt - p) * 8)
                    apart(sp)
                    wait_free(sp, s["xsT_mm"], tt - 1)
                    sp.dma_start(xsb[p], xs_flat[c][bass.ds(t * P, P), :]).then_inc(s[f"xs_loaded{p}"], 16)

                def store_tile(t, p):
                    tt = t + c * NT
                    sp.wait_ge(s["y_made"], tt + 1)
                    wait_free(sp, s[f"ys_stored{p}"], (tt - p) * 8)
                    sp.dma_start(ys_flat[c][bass.ds(t * P, P), :], yb[p]).then_inc(s[f"ys_stored{p}"], 16)

                for t in range(4):
                    load_tile(t, t % 2)
                for t in range(4, 6):
                    load_tile(t, t % 2)
                    store_tile(t - 4, t % 2)
                with sp.Fori(3, NT // 2) as turn:
                    for p in range(2):
                        load_tile(turn * 2 + p, p)
                        store_tile(turn * 2 + (p - 4), p)
                for t in range(NT - 4, NT):
                    store_tile(t, t % 2)
            sp.wait_ge(s["lg_made"], NB)
            load_ctx(0, ctxc[0], "ctxc_loaded", "V1_mm")
            load_ctx(1, ctxc[1], "ctxc_loaded", "V1_mm")

            def store_out(b, p):
                sp.wait_ge(s["ob_made"], b + 1)
                wait_free(sp, s[f"out_stored{p}"], (b - p) * 8)
                sp.dma_start(out_rows[bass.ds(b * N, N), :], ob[p]).then_inc(s[f"out_stored{p}"], 16)

            for b in range(2, 8):
                load_ctx(b, ctxc[b % 2], "ctxc_loaded", "V1_mm")
            for b in range(8, 10):
                load_ctx(b, ctxc[b % 2], "ctxc_loaded", "V1_mm")
                store_out(b - 8, b % 2)
            with sp.Fori(5, NB // 2) as turn:
                for p in range(2):
                    load_ctx(turn * 2 + p, ctxc[p], "ctxc_loaded", "V1_mm")
                    store_out(turn * 2 + (p - 8), p)
            for b in range(NB - 8, NB):
                store_out(b, b % 2)
            for p in range(2):
                sp.wait_ge(s[f"out_stored{p}"], NB // 2 * 16)

        @block.gpsimd
        def _(pool):
            g = nc.gpsimd
            g.memset(ident[:, :], 0.0).then_inc(s["ms"], 1)
            g.memset(identb[:, :], 0.0).then_inc(s["ms"], 1)
            g.memset(onesb[:, :], 1.0).then_inc(s["ms"], 1)
            g.memset(nfirst[:, :, :], 1.0).then_inc(s["ms"], 1)
            g.memset(mask4[:, :], 1.0).then_inc(s["ms"], 1)
            g.memset(zt[:, :], 0.0).then_inc(s["ms"], 1)
            g.memset(one16, 1.0).then_inc(s["ms"], 1)
            g.memset(mhalf[:, :], -0.5).then_inc(s["ms"], 1)
            pool.wait_ge(s["ms"], 8)
            for p in range(2):
                vv = V0[p].rearrange("j (h w) -> j h w", h=H0)
                g.memset(vv[:, :, VW0 - 1:VW0], 1.0).then_inc(s["ms"], 1)
            pool.wait_ge(s["ms"], 10)
            for m in (ident, identb):
                g.affine_select(out=m[:, :], in_=m[:, :], compare_op=ALU.not_equal, fill=1.0, base=0,
                                pattern=[[-1, P]], channel_multiplier=1).then_inc(s["consts"], 1)
            g.affine_select(out=ltri[:, :], in_=onesb[:, :], compare_op=ALU.is_ge, fill=0.0, base=-1,
                            pattern=[[1, P]], channel_multiplier=-1).then_inc(s["consts"], 1)
            g.iota(iotaD[:, :], pattern=[[-1, NE]], base=NE, channel_multiplier=0,
                   allow_small_or_imprecise_dtypes=True).then_inc(s["consts"], 1)
            g.iota(tau[:, :], pattern=[[0, 1]], base=0, channel_multiplier=P,
                   allow_small_or_imprecise_dtypes=True).then_inc(s["consts"], 1)
            g.memset(nfirst[:, :, 0:1], 0.0).then_inc(s["consts"], 1)
            for q in range(P // 32):
                m = mask4[32 * q:32 * q + 32, :]
                wait_free(pool, s["mask_made"], 2 * q)
                g.affine_select(out=m, in_=m, compare_op=ALU.is_ge, fill=0.0, base=0,
                                pattern=[[-DH1, GH]], channel_multiplier=1).then_inc(s["mask_made"], 1)
                pool.wait_ge(s["mask_made"], 2 * q + 1)
                g.affine_select(out=m, in_=m, compare_op=ALU.is_ge, fill=0.0, base=DH1 - 1,
                                pattern=[[DH1, GH]], channel_multiplier=-1).then_inc(s["mask_made"], 1)
            pool.wait_ge(s["mask_made"], 2 * P // 32)
            for c in range(NCH):
                rows = NT * P // P
                pool.dma_start(xs_flat[c].rearrange("(p r) d -> p (r d)", p=P)[:, 0:rows * D].rearrange(
                    "p (k w) -> p k w", w=512), zt[:, :].rearrange("p (o w) -> p o w", o=1).to_broadcast(
                        [P, rows * D // 512, 512])).then_inc(s["xs_zeroed"], 16)
            pool.dma_start(W1s[:, :, :], a["W1"].rearrange("e d h -> d e h")).then_inc(s["moe_loaded"], 16)
            pool.dma_start(W2s[:, :, :, :].rearrange("p e c d -> p (e c) d"),
                           a["W2"].rearrange("e (c p) d -> p (e c) d", p=P)).then_inc(s["moe_loaded"], 16)
            pool.dma_start(b1s[:, :, :].rearrange("p e h -> p (e h)"),
                           row(a["b1"].rearrange("e h -> (e h)"))).then_inc(s["moe_loaded"], 16)
            pool.dma_start(b2s[:, :, :].rearrange("p e h -> p (e h)"),
                           row(a["b2"].rearrange("e h -> (e h)"))).then_inc(s["moe_loaded"], 16)
            pool.wait_ge(s["xs_zeroed"], 16 * NCH)

            def rstd(mv, rs, agg, mid, made, b, scale, shift, last_use):
                pool.wait_ge(s[agg], b + 1)
                wait_free(pool, s[last_use], b - 1)
                apart(pool)
                g.tensor_scalar(rs[:, 0:1], mv[:, 1:2], scale, shift, ALU.mult, ALU.add).then_inc(s[mid], 1)
                pool.wait_ge(s[mid], b + 1)
                g.tensor_tensor(rs[:, 1:2], rs[:, 0:1], mhalf[:, :], ALU.pow).then_inc(s[made], 1)

            def scatter(c, b, p):
                bb = b + c * CB
                wait_free(pool, s[f"scat_made{p}"], (bb - p) * 16)
                g.tensor_copy(scat[p], XN[:, bass.ds(bb, 1), :].rearrange("q o d -> q (o d)")).then_inc(s["idx_made"], 1)
                for k in range(2):
                    g.tensor_copy(si[2 * p + k], POS[k][:, bass.ds(bb, 1)]).then_inc(s["idx_made"], 1)
                pool.wait_ge(s["idx_made"], bb * 3 + 3)
                apart(pool)
                for k in range(2):
                    g.indirect_dma_start(out=xs_flat[c][:, :], out_offset=bass.IndirectOffsetOnAxis(ap=si[2 * p + k], axis=0),
                                         in_=scat[p], in_offset=None).then_inc(s[f"scat_made{p}"], 16)

            def step_a(t):
                if (b := t.at(4)) is not None:
                    p = t.par(4)
                    rstd(mv2[p], rs2[p], "agg2", "rst2", "rs2_made", b, 1.0, EPS, "xn2_made")
                if (b := t.at(0)) is not None:
                    p = t.par(0)
                    rstd(mv1[p], rs1[p], "agg1", "rst1", "rs1_made", b, 1.0 + EPS, EPS * EPS, "xn1_made")
                if (b := t.at(5)) is not None:
                    pool.wait_ge(s["xn2_made"], b + 1)
                    g.tensor_copy(XN[:, bass.ds(b, 1), :].rearrange("q o d -> q (o d)"), xn2[t.par(5)]).then_inc(s["XN_kept"], 1)

            for span in route_spans():
                if span is None:
                    pool.wait_ge(s["ro_done"], 1)
                    continue
                first, last, peeled = span

                def step(t):
                    step_a(t)
                    if first >= ROUTE0:
                        v = t.value - ROUTE0
                        scatter(0, v, t.parity)
                run_steps(pool, NB, first, last, peeled, step)
            pool.wait_ge(s["ro_done"], 2)
            pool.wait_ge(s["XN_kept"], NB)
            with pool.Fori(0, CB // 2) as turn:
                for p in range(2):
                    scatter(1, turn * 2 + p, p)
            for p in range(2):
                pool.wait_ge(s[f"ys_stored{p}"], NCH * NT // 2 * 16)
                vv = V1[p].rearrange("j (h w) -> j h w", h=H1)
                g.memset(vv[:, :, VW1 - 1:VW1], 1.0).then_inc(s["ms"], 1)
            pool.wait_ge(s["ms"], 12)

            def gather(b, p, c):
                wait_free(pool, s["x2_made"], b - 1)
                for k in range(2):
                    g.tensor_copy(gi[k][p], POS[k][:, bass.ds(b, 1)]).then_inc(s["gi_made"], 1)
                pool.wait_ge(s["gi_made"], b * 2 + 2)
                apart(pool)
                for k in range(2):
                    g.indirect_dma_start(out=gy[k][p], out_offset=None, in_=ys_flat[c][:, :],
                                         in_offset=bass.IndirectOffsetOnAxis(ap=gi[k][p], axis=0)).then_inc(s[f"gy_made{p}"], 16)

            def step_c(t):
                if (b := t.at(1)) is not None:
                    p = t.par(1)
                    rstd(mv3[p], rs3[p], "agg3", "rst3", "rs3_made", b, 1.0, EPS, "xn3_made")
                    g.tensor_tensor(XR[:, bass.ds(b, 1), :].rearrange("q o d -> q (o d)"),
                                    XR[:, bass.ds(b, 1), :].rearrange("q o d -> q (o d)"), bo1[:, :], ALU.add).then_inc(s["x2b_made"], 1)
                if (b := t.at(6)) is not None:
                    p = t.par(6)
                    rstd(mv4[p], rs4[p], "agg4", "rst4", "rs4_made", b, 1.0, EPS, "xb4_made")
                if (b := t.at(0)) is not None:
                    gather(b, t.par(0), t.chunk)
                if (b := t.at(7)) is not None:
                    p = t.par(7)
                    pool.wait_ge(s["c4_made"], b + 1)
                    wait_free(pool, s["xq4_made"], b)
                    g.tensor_tensor(t4, z4[p], c4[p], ALU.add).then_inc(s["t4_made"], 1)
                    apart(pool)
                    g.tensor_scalar(n4, z4[p], FP8_TOP, 0.0, ALU.mult, ALU.mult).then_inc(s["n4_made"], 1)
                    pool.wait_ge(s["t4_made"], b + 1)
                    g.tensor_tensor(q4, t4, c4[p], ALU.subtract).then_inc(s["q4_made"], 1)
                    pool.wait_ge(s["n4_made"], b + 1)
                    pool.wait_ge(s["q4_made"], b + 1)
                    wait_free(pool, s["xqT_mm"], b - 1)
                    g.tensor_tensor(xq4[p], q4, n4, ALU.add).then_inc(s["xq4_made"], 1)
                if (b := t.at(8)) is not None:
                    p = t.par(8)
                    pool.wait_ge(s["y4_made"], b + 1)
                    wait_free(pool, s["ob_made"], b - 1)
                    g.tensor_tensor(y4b[p], y4[p], fbias[:, :], ALU.add).then_inc(s["y4b_made"], 1)

            for first, last, peeled in c_spans():
                def step(t):
                    t.chunk = 0 if first < CB else 1
                    step_c(t)
                run_steps(pool, NB, first, last, peeled, step)

        @block.scalar
        def _(act):
            A = nc.scalar

            def cp(o, i, done):
                A.activation(o, i, ACT.Copy).then_inc(s[done], 1)

            act.wait_ge(s["w_loaded"], 16 * len(loads))
            A.activation(tg[:, :], tg[:, :], ACT.Tanh).then_inc(s["tanh_made"], 1)
            for k in range(2):
                act.wait_ge(s["t0_mm"], k + 1)
                cp(T0[:, 4 * k:4 * k + 4, :].rearrange("p h d -> p (h d)"), PS[:, k, :], "t0_cp")

            def step_a(t):
                if (b := t.at(3)) is not None:
                    act.wait_ge(s["PT0_mm"], 2 * b + 1)
                    cp(PT0[t.par(3)][:, 0:HB0 * P], PS[0:J, 2, :], "PT0_cpa")
                if (b := t.at(2)) is not None:
                    act.wait_ge(s["S0_sub"], b + 1)
                    A.activation(P0[t.par(2)], S0[t.par(2)], ACT.Exp, scale=DH0 ** -0.5).then_inc(s["exp0"], 1)
                if (b := t.at(3)) is not None:
                    act.wait_ge(s["OT0_mm"], b + 1)
                    wait_free(act, s["Y0_mm"], b - 1)
                    cp(OT0[t.par(3)], PS[:, 3, :], "OT0_cp")
                if (b := t.at(1)) is not None:
                    p = t.par(1)
                    act.wait_ge(s["KA_mm"], b + 1)
                    wait_free(act, s["S0_mm"], b - 1)
                    cp(KA[p].rearrange("p (k w) -> p k w", k=2), PS[:, 6:8, 0:HB0 * J], "KA_cp")
                    act.wait_ge(s["V0_mm"], b + 1)
                    wait_free(act, s["O0_mm"], b - 1)
                    cp(V0[p].rearrange("j (h w) -> j h w", h=H0)[:, :, 0:DH0],
                       PS[0:J, 2, :].rearrange("j (h w) -> j h w", h=H0), "V0_cp")
                    act.wait_ge(s["xT1_mm"], b + 1)
                    A.activation(xT1[p], PS[:, 5, 0:D], ACT.Identity, bias=beta[:, 0:1],
                                 scale=gamma[:, 0:1]).then_inc(s["xT1_cp"], 1)
                if (b := t.at(5)) is not None:
                    act.wait_ge(s["xT2_mm"], b + 1)
                    wait_free(act, s["lg_mm"], b - 1)
                    cp(xT2[t.par(5)], PS[:, 6, 0:D], "xT2_cp")

            def route(c):
                act.wait_ge(s["ro_e"], c + 1)
                A.activation(rt["e"], rt["s"], ACT.Exp).then_inc(s["ro_exp"], 1)

            for span in route_spans():
                if span is None:
                    route(0)
                else:
                    run_steps(act, NB, *span, step_a)
            route(1)

            def step_b(t):
                if (b := t.at(0)) is not None:
                    act.wait_ge(s["xsT_mm"], b + t.base + 1)
                    wait_free(act, s["h_mm"], b + t.base - 1)
                    cp(xsT[t.par(0)], PS[:, t.par(0), 0:D], "xsT_cp")
                if (b := t.at(2)) is not None:
                    p = t.par(2)
                    act.wait_ge(s["hT_mm"], b + t.base + 1)
                    wait_free(act, s["y_mm"], b + t.base - 1)
                    A.activation(hT[p], PS[:, 4 + p, 0:EH], ACT.Relu).then_inc(s["hT_cp"], 1)

            for c in range(NCH):
                for span in spans(NT, LOOP0, LAST_LAG_B):
                    def step(t):
                        t.base = c * NT
                        step_b(t)
                    run_steps(act, NT, *span, step)

            def step_c(t):
                if (b := t.at(5)) is not None:
                    for q in (0, 2):
                        act.wait_ge(s["PT1_mm"], 4 * b + q + 1)
                        if q == 0:
                            wait_free(act, s["O1_mm"], b)
                        cp(PT1[:, q * 512:q * 512 + 512], PS[0:J, 4 + q % 3, :], "PT1_cpa")
                if (b := t.at(2)) is not None:
                    act.wait_ge(s["xT3_mm"], b + 1)
                    wait_free(act, s["QT_mm"], b - 1)
                    cp(xT3[t.par(2)], PS[:, 4, 0:D], "xT3_cp")
                if (b := t.at(3)) is not None:
                    act.wait_ge(s["QT_mm"], b + 1)
                    wait_free(act, s["S1_mm"], b - 1)
                    A.activation(QT1[t.par(3)], PS[:, 5, 0:D], ACT.Identity, bias=bq1[:, 0:1]).then_inc(s["QT_cp"], 1)
                if (b := t.at(4)) is not None:
                    act.wait_ge(s["S1_sub"], b + 1)
                    A.activation(P1[t.par(4)], S1, ACT.Exp, scale=DH1 ** -0.5).then_inc(s["exp1"], 1)
                if (b := t.at(5)) is not None:
                    act.wait_ge(s["OT1_mm"], b + 1)
                    wait_free(act, s["Y1_mm"], b - 1)
                    cp(OT1[t.par(5)], PS[:, 7, 0:D], "OT1_cp")
                if (b := t.at(8)) is not None:
                    act.wait_ge(s["xqT_mm"], b + 1)
                    wait_free(act, s["y4_mm"], b - 1)
                    cp(xqT4[t.par(8)], PS[:, 5, 0:D // 2].bitcast(BF16), "xqT_cp")

            for span in c_spans():
                run_steps(act, NB, *span, step_c)

        @block.vector
        def _(dve):
            V = nc.vector
            chain = {"kq_step": 0, "ro": 0}

            def link(ins, name):
                chain[name] += 1
                ins.then_inc(s[name], 1)
                dve.wait_ge(s[name], chain[name])

            def res(b):
                return XR[:, bass.ds(b, 1), :].rearrange("q o d -> q (o d)")

            dve.wait_ge(s["w_loaded"], 16 * len(loads))
            link(V.reciprocal(scr[:, :], sc[:, :]), "kq_step")
            link(V.tensor_tensor(scm[:, :], sc[:, 0:1], sc[:, 1:2], ALU.mult), "kq_step")
            link(V.tensor_scalar(ksz, kf[:, :], scr[:, 1:2], None, ALU.mult), "kq_step")
            link(V.tensor_scalar(ksc.bitcast(I32), ksz.bitcast(I32), EXP_BITS, None, ALU.bitwise_and), "kq_step")
            link(V.tensor_scalar(ksc, ksc, FP8_LEAST, FP8_ROUND, ALU.max, ALU.mult), "kq_step")
            link(V.tensor_tensor(ksq, ksz, ksc, ALU.add), "kq_step")
            link(V.tensor_tensor(ksq, ksq, ksc, ALU.subtract), "kq_step")
            link(V.tensor_scalar(ksz, ksz, FP8_TOP, 0.0, ALU.mult, ALU.mult), "kq_step")
            link(V.tensor_tensor(kq[:, :], ksq, ksz, ALU.add), "kq_step")
            dve.wait_ge(s["tanh_made"], 1)
            link(V.tensor_scalar(bo1[:, :], bo1[:, :], tg[:, 1:2], None, ALU.mult), "kq_step")
            link(V.tensor_tensor(lbias[:, 0, :], lbias[:, 0, :], lbias[:, 1, :], ALU.add), "kq_step")

            def stats(src, st, mv, sname, aname, b, last_use):
                wait_free(dve, s[aname], b)
                apart(dve)
                V.bn_stats(st, src).then_inc(s[sname], 1)
                dve.wait_ge(s[sname], b + 1)
                wait_free(dve, s[last_use], b - 1)
                apart(dve)
                V.bn_aggr(mv, st).then_inc(s[aname], 1)

            def normed(o, src, mv, rs, done):
                V.tensor_scalar(o, src, mv[:, 0:1], rs[:, 1:2], ALU.subtract, ALU.mult).then_inc(s[done], 1)

            def step_a(t):
                if (b := t.at(4)) is not None:
                    dve.wait_ge(s["Y0_mm"], b + 1)
                    V.scalar_tensor_tensor(res(b), PS[:, 4, 0:D], tg[:, 0:1], res(b), ALU.mult,
                                           ALU.add).then_inc(s["x1_made"], 1)
                    dve.wait_ge(s["x1_made"], b + 1)
                    stats(res(b), st2, mv2[t.par(4)], "stats2", "agg2", b, "xn2_made")
                if (b := t.at(3)) is not None:
                    dve.wait_ge(s["PT0_mm"], 2 * b + 2)
                    V.tensor_copy(PT0[t.par(3)][:, HB0 * P:], PS[0:J, 3, :]).then_inc(s["PT0_cpb"], 1)
                if (b := t.at(0)) is not None:
                    dve.wait_ge(s["x_loaded"], b * 16 + 16)
                    stats(res(b), st1, mv1[t.par(0)], "stats1", "agg1", b, "xn1_made")
                if (b := t.at(5)) is not None:
                    p = t.par(5)
                    dve.wait_ge(s["rs2_made"], b + 1)
                    wait_free(dve, s["xT2_mm"], b - 1)
                    wait_free(dve, s["XN_kept"], b - 1)
                    normed(xn2[p], res(b), mv2[p], rs2[p], "xn2_made")
                if (b := t.at(2)) is not None:
                    p = t.par(2)
                    sv = PS[:, 0:2, 0:HB0 * J].rearrange("q k (h j) -> q k h j", j=J)
                    dve.wait_ge(s["S0_mm"], b + 1)
                    wait_free(dve, s["S0_sub"], b)
                    V.tensor_reduce(mx0.rearrange("q (k h) -> q k h", k=2), sv, X, ALU.max).then_inc(s["mx0_made"], 1)
                    dve.wait_ge(s["mx0_made"], b + 1)
                    wait_free(dve, s["exp0"], b - 1)
                    V.tensor_tensor(S0[p].rearrange("q (k h j) -> q k h j", k=2, j=J), sv,
                                    mx0.rearrange("q (k h o) -> q k h o", k=2, o=1).to_broadcast([P, 2, HB0, J]),
                                    ALU.subtract).then_inc(s["S0_sub"], 1)
                if (b := t.at(3)) is not None:
                    p = t.par(3)
                    ov = PS[:, 4:6, 0:HB0 * VW0].rearrange("q k (h w) -> q k h w", w=VW0)
                    dve.wait_ge(s["O0_mm"], b + 1)
                    wait_free(dve, s["O0_cp"], b)
                    V.reciprocal(rd0.rearrange("q (k h o) -> q k h o", k=2, o=1), ov[:, :, :, DH0:VW0]).then_inc(s["rd0_made"], 1)
                    dve.wait_ge(s["rd0_made"], b + 1)
                    wait_free(dve, s["OT0_mm"], b - 1)
                    V.tensor_tensor(O0[p].rearrange("q (k h w) -> q k h w", k=2, w=DH0), ov[:, :, :, 0:DH0],
                                    rd0.rearrange("q (k h o) -> q k h o", k=2, o=1).to_broadcast([P, 2, HB0, DH0]),
                                    ALU.mult).then_inc(s["O0_cp"], 1)
                if (b := t.at(1)) is not None:
                    p = t.par(1)
                    dve.wait_ge(s["rs1_made"], b + 1)
                    wait_free(dve, s["xT1_mm"], b - 1)
                    normed(xn1[p], res(b), mv1[p], rs1[p], "xn1_made")
                if (b := t.at(6)) is not None:
                    dve.wait_ge(s["lg_mm"], b + 1)
                    V.tensor_tensor(LG[:, bass.ds(b, 1), :].rearrange("q o e -> q (o e)"), PS[:, 7, 0:NE],
                                    lbias[:, 0, :], ALU.add).then_inc(s["lg_made"], 1)

            def route(c):
                lo = c * CB
                be = lambda v: v.rearrange("q (b e) -> q b e", e=NE)
                eb = lambda v: v.rearrange("q (e b) -> q e b", e=NE)
                per_b = lambda v: v.rearrange("q (b o) -> q b o", o=1).to_broadcast([P, CB, NE])
                lg = LG[:, lo:lo + CB, :]
                ranks = iotaD[:, :].rearrange("q (o e) -> q o e", o=1).to_broadcast([P, CB, NE])
                dve.wait_ge(s["lg_made"], lo + CB)

                def choose(logits, v, oh):
                    link(V.tensor_reduce(v, logits, X, ALU.max), "ro")
                    link(V.tensor_tensor(be(rt["eq"]), logits, per_b(v), ALU.is_equal), "ro")
                    link(V.tensor_tensor(be(rt["eq"]), be(rt["eq"]), ranks, ALU.mult), "ro")
                    link(V.tensor_reduce(rt["m"], be(rt["eq"]), X, ALU.max), "ro")
                    link(V.tensor_tensor(be(oh), ranks, per_b(rt["m"]), ALU.is_equal), "ro")

                choose(lg, rt["v0"], rt["oh0"])
                link(V.scalar_tensor_tensor(be(rt["lg2"]), be(rt["oh0"]), -3.0e38, lg, ALU.mult, ALU.add), "ro")
                choose(be(rt["lg2"]), rt["v1"], rt["oh1"])
                V.tensor_tensor(rt["s"], rt["v1"], rt["v0"], ALU.subtract).then_inc(s["ro_e"], 1)
                V.tensor_tensor(eb(rtM), rt["oh0"].rearrange("q (b e) -> q e b", e=NE),
                                rt["oh1"].rearrange("q (b e) -> q e b", e=NE), ALU.add).then_inc(s["ro_M"], 1)
                dve.wait_ge(s["ro_cnt"], c + 1)
                link(V.tensor_tensor_scan(rt["cum"], nfirst[:, :, :].rearrange("q e b -> q (e b)"), PS[:, 1, :],
                                          0.0, ALU.mult, ALU.add), "ro")
                link(V.tensor_scalar(rti, eb(rt["cum"])[:, :, CB - 1], float(P - 1), None, ALU.add), "ro")
                link(V.tensor_scalar(rti, rti, -P, None, ALU.bitwise_and), "ro")
                link(V.tensor_copy(rt["pad"], rti), "ro")
                link(V.tensor_tensor_scan(rt["inc"], one16, rt["pad"], 0.0, ALU.mult, ALU.add), "ro")
                link(V.tensor_tensor(rt["base"], rt["inc"], rt["pad"], ALU.subtract), "ro")
                link(V.tensor_scalar(rt["le"], rt["inc"], tau[:, 0:1], None, ALU.is_le), "ro")
                link(V.tensor_reduce(rt["et"], rt["le"], X, ALU.add), "ro")
                V.tensor_scalar(rt["et"], rt["et"], float(NE - 1), None, ALU.min).then_inc(s["ro_et"], 1)
                link(V.tensor_tensor(rt["pos"], rt["cum"], PS[:, 1, :], ALU.subtract), "ro")
                link(V.tensor_tensor(rt["pos"], rt["pos"], PS[:, 0, :], ALU.add), "ro")
                link(V.tensor_tensor(eb(rt["pos"]), eb(rt["pos"]),
                                     rt["base"].rearrange("q (e o) -> q e o", o=1).to_broadcast([P, NE, CB]), ALU.add), "ro")
                for k in range(2):
                    link(V.tensor_tensor(be(rt["eq"]), be(rt[f"oh{k}"]), rt["pos"].rearrange("q (e b) -> q b e", e=NE),
                                         ALU.mult), "ro")
                    link(V.tensor_reduce(rt["m"], be(rt["eq"]), X, ALU.add), "ro")
                    link(V.tensor_copy(POS[k][:, lo:lo + CB], rt["m"]), "ro")
                dve.wait_ge(s["ro_exp"], c + 1)
                link(V.tensor_scalar(rt["s"], rt["e"], 1.0, None, ALU.add), "ro")
                link(V.reciprocal(rt["s"], rt["s"]), "ro")
                link(V.tensor_scalar(WT[0][:, lo:lo + CB], rt["s"], tg[:, 2:3], None, ALU.mult), "ro")
                link(V.tensor_tensor(WT[1][:, lo:lo + CB], WT[0][:, lo:lo + CB], rt["e"], ALU.mult), "ro")
                dve.wait_ge(s["ro_et"], 2 * c + 2)
                V.tensor_copy(ETI[:, c, :], PS[0:1, 2, 0:P]).then_inc(s["ro_done"], 1)

            for span in route_spans():
                if span is None:
                    route(0)
                else:
                    run_steps(dve, NB, *span, step_a)
            route(1)

            dve.wait_ge(s["moe_loaded"], 64)
            dve.wait_ge(s["ro_done"], NCH)

            def step_b(t, c):
                base = c * NT
                if (b := t.at(1)) is not None:
                    p = t.par(1)
                    e = dve.value_load(ETI[0:1, c, bass.ds(b, 1)], min_val=0, max_val=NE - 1)
                    dve.wait_ge(s["h_mm"], b + base + 1)
                    wait_free(dve, s["hT_mm"], b + base - 1)
                    V.tensor_tensor(hb[p], PS[:, 2 + p, 0:EH],
                                    b1s[:, bass.ds(e, 1), :].rearrange("q o h -> q (o h)"), ALU.add).then_inc(s["h_made"], 1)
                if (b := t.at(3)) is not None:
                    p = t.par(3)
                    e = dve.value_load(ETI[0:1, c, bass.ds(b, 1)], min_val=0, max_val=NE - 1)
                    dve.wait_ge(s["y_mm"], b + base + 1)
                    wait_free(dve, s[f"ys_stored{p}"], (b + base - p) * 8)
                    V.tensor_tensor(yb[p], PS[:, 6 + p, 0:D],
                                    b2s[:, bass.ds(e, 1), :].rearrange("q o h -> q (o h)"), ALU.add).then_inc(s["y_made"], 1)

            for c in range(NCH):
                for span in spans(NT, LOOP0, LAST_LAG_B):
                    run_steps(dve, NT, *span, lambda t: step_b(t, c))

            def step_c(t):
                if (b := t.at(6)) is not None:
                    dve.wait_ge(s["Y1_mm"], b + 1)
                    dve.wait_ge(s["x2b_made"], b + 1)
                    V.scalar_tensor_tensor(res(b), PS[:, 6, 0:D], tg[:, 1:2], res(b), ALU.mult,
                                           ALU.add).then_inc(s["x3_made"], 1)
                    dve.wait_ge(s["x3_made"], b + 1)
                    stats(res(b), st4, mv4[t.par(6)], "stats4", "agg4", b, "xb4_made")
                if (b := t.at(5)) is not None:
                    for q in (1, 3):
                        dve.wait_ge(s["PT1_mm"], 4 * b + q + 1)
                        if q == 1:
                            wait_free(dve, s["O1_mm"], b)
                        V.tensor_copy(PT1[:, q * 512:q * 512 + 512], PS[0:J, 4 + q % 3, :]).then_inc(s["PT1_cpb"], 1)
                if (b := t.at(1)) is not None:
                    p = t.par(1)
                    dve.wait_ge(s[f"gy_made{p}"], (b - p) * 16 + 32)
                    wait_free(dve, s["x2_made"], b)
                    V.scalar_tensor_tensor(uc, gy[0][p], WT[0][:, bass.ds(b, 1)], res(b), ALU.mult, ALU.add).then_inc(s["u_made"], 1)
                    dve.wait_ge(s["u_made"], b + 1)
                    V.scalar_tensor_tensor(res(b), gy[1][p], WT[1][:, bass.ds(b, 1)], uc, ALU.mult, ALU.add).then_inc(s["x2_made"], 1)
                    dve.wait_ge(s["x2_made"], b + 1)
                    wait_free(dve, s["agg3"], b)
                    apart(dve)
                    V.bn_stats(st3, res(b)).then_inc(s["stats3"], 1)
                    wait_free(dve, s["xT3_mm"], b - 1)
                    apart(dve)
                    V.tensor_copy(xn3[p], res(b)).then_inc(s["z4_made"], 1)
                    dve.wait_ge(s["stats3"], b + 1)
                    apart(dve)
                    V.bn_aggr(mv3[p], st3).then_inc(s["agg3"], 1)
                if (b := t.at(2)) is not None:
                    p = t.par(2)
                    dve.wait_ge(s["rs3_made"], b + 1)
                    normed(xn3[p], xn3[p], mv3[p], rs3[p], "xn3_made")
                if (b := t.at(4)) is not None:
                    sv = PS[:, 0:NG, 0:GH * J].rearrange("q g (h j) -> q g h j", j=J)
                    dve.wait_ge(s["S1_mm"], b + 1)
                    wait_free(dve, s["S1_sub"], b)
                    V.tensor_reduce(mx1.rearrange("q (g h) -> q g h", g=NG), sv, X, ALU.max).then_inc(s["mx1_made"], 1)
                    dve.wait_ge(s["mx1_made"], b + 1)
                    wait_free(dve, s["exp1"], b)
                    V.tensor_tensor(S1.rearrange("q (g h j) -> q g h j", g=NG, j=J), sv,
                                    mx1.rearrange("q (g h o) -> q g h o", g=NG, o=1).to_broadcast([P, NG, GH, J]),
                                    ALU.subtract).then_inc(s["S1_sub"], 1)
                if (b := t.at(3)) is not None:
                    p = t.par(3)
                    dve.wait_ge(s["KT_mm"], b + 1)
                    wait_free(dve, s["S1_mm"], b - 1)
                    V.scalar_tensor_tensor(KB1[p].rearrange("q (h j) -> q h j", h=GH),
                                           PS[:, 6, 0:J].rearrange("q (o j) -> q o j", o=1).to_broadcast([P, GH, J]),
                                           bk1[:, 0:1],
                                           mask4[:, :].rearrange("q (h o) -> q h o", o=1).to_broadcast([P, GH, J]),
                                           ALU.add, ALU.mult).then_inc(s["KB_made"], 1)
                    dve.wait_ge(s["V1_mm"], b + 1)
                    wait_free(dve, s["O1_mm"], b - 1)
                    V.tensor_tensor(V1[p].rearrange("j (h w) -> j h w", h=H1)[:, :, 0:DH1],
                                    PS[0:J, 4, 0:D].rearrange("j (h w) -> j h w", h=H1),
                                    bv1[0:J, :].rearrange("j (h w) -> j h w", h=H1), ALU.add).then_inc(s["V1_cp"], 1)
                if (b := t.at(5)) is not None:
                    p = t.par(5)
                    ov = PS[:, 7, 0:H1 * VW1].rearrange("q (h w) -> q h w", w=VW1)
                    dve.wait_ge(s["O1_mm"], b + 1)
                    wait_free(dve, s["O1_cp"], b)
                    V.reciprocal(rd1.rearrange("q (h o) -> q h o", o=1), ov[:, :, DH1:VW1]).then_inc(s["rd1_made"], 1)
                    dve.wait_ge(s["rd1_made"], b + 1)
                    wait_free(dve, s["OT1_mm"], b - 1)
                    V.tensor_tensor(O1[p].rearrange("q (h w) -> q h w", w=DH1), ov[:, :, 0:DH1],
                                    rd1.rearrange("q (h o) -> q h o", o=1).to_broadcast([P, H1, DH1]),
                                    ALU.mult).then_inc(s["O1_cp"], 1)
                if (b := t.at(7)) is not None:
                    p = t.par(7)
                    dve.wait_ge(s["rs4_made"], b + 1)
                    wait_free(dve, s["m4_made"], 2 * b)
                    normed(xb4, res(b), mv4[p], rs4[p], "xb4_made")
                    dve.wait_ge(s["xb4_made"], b + 1)
                    wait_free(dve, s["xq4_made"], b - 1)
                    V.tensor_scalar(z4[p], xb4, scr[:, 0:1], None, ALU.mult).then_inc(s["m4_made"], 1)
                    dve.wait_ge(s["m4_made"], 2 * b + 1)
                    V.tensor_scalar(c4[p].bitcast(I32), z4[p].bitcast(I32), EXP_BITS, None, ALU.bitwise_and).then_inc(s["m4_made"], 1)
                    dve.wait_ge(s["m4_made"], 2 * b + 2)
                    V.tensor_scalar(c4[p], c4[p], FP8_LEAST, FP8_ROUND, ALU.max, ALU.mult).then_inc(s["c4_made"], 1)
                if (b := t.at(8)) is not None:
                    p = t.par(8)
                    dve.wait_ge(s["y4_mm"], b + 1)
                    wait_free(dve, s["y4b_made"], b - 1)
                    V.tensor_scalar(y4[p], PS[:, 7, 0:D], scm[:, 0:1], None, ALU.mult).then_inc(s["y4_made"], 1)
                if (b := t.at(9)) is not None:
                    p = t.par(9)
                    dve.wait_ge(s["y4b_made"], b + 1)
                    wait_free(dve, s[f"out_stored{p}"], (b - p) * 8)
                    V.scalar_tensor_tensor(ob[p], y4b[p], tg[:, 3:4], res(b), ALU.mult, ALU.add).then_inc(s["ob_made"], 1)

            for span in c_spans():
                run_steps(dve, NB, *span, step_c)

        @block.tensor
        def _(pe):
            T = nc.tensor

            def mm(o, l, r, start=True, stop=True):
                return T.matmul(o, l, r, start=start, stop=stop)

            pe.wait_ge(s["w_loaded"], 16 * len(loads))
            for h in range(H0):
                last = mm(PS[:, h // 4, (h % 4) * D:(h % 4 + 1) * D], wkT[:, h * D:(h + 1) * D], wqT[:, h * D:(h + 1) * D])
                if h % 4 == 3:
                    last.then_inc(s["t0_mm"], 1)
            pe.wait_ge(s["t0_cp"], 2)
            pe.wait_ge(s["consts"], 6)

            def step_a(t):
                if (b := t.at(3)) is not None:
                    p = t.par(3)
                    pe.wait_ge(s["exp0"], b + 1)
                    pe.wait_ge(s["V0_cp"], b + 1)
                    wait_free(pe, s["V0_cp"], t.seen(1))
                    wait_free(pe, s["OT0_cp"], t.seen(3))
                    for h in range(H0):
                        last = T.transpose(PS[0:J, 2 + h // 4, (h % 4) * P:(h % 4 + 1) * P],
                                           P0[p][:, h * J:(h + 1) * J], ident[:, :])
                        if h % 4 == 3:
                            last.then_inc(s["PT0_mm"], 1)
                if (b := t.at(2)) is not None:
                    p = t.par(2)
                    pe.wait_ge(s["xT1_cp"], b + 1)
                    pe.wait_ge(s["KA_cp"], b + 1)
                    wait_free(pe, s["S0_sub"], b)
                    for k in range(2):
                        last = mm(PS[:, k, 0:HB0 * J], xT1[p], KA[p][:, k * HB0 * J:(k + 1) * HB0 * J])
                    last.then_inc(s["S0_mm"], 1)
                if (b := t.at(3)) is not None:
                    p = t.par(3)
                    pe.wait_ge(s["PT0_cpa"], b + 1)
                    pe.wait_ge(s["PT0_cpb"], b + 1)
                    wait_free(pe, s["x1_made"], t.seen(3))
                    wait_free(pe, s["xT1_cp"], t.seen(1))
                    for h in range(H0):
                        last = mm(PS[:, 4 + h // 4, (h % 4) * VW0:(h % 4 + 1) * VW0],
                                  PT0[p][:, h * P:(h + 1) * P], V0[p][:, h * VW0:(h + 1) * VW0])
                    last.then_inc(s["O0_mm"], 1)
                if (b := t.at(1)) is not None:
                    p = t.par(1)
                    pe.wait_ge(s["ctx_loaded"], b * 16 + 16)
                    wait_free(pe, s["KA_cp"], b)
                    wait_free(pe, s["xT2_cp"], t.seen(5))
                    wait_free(pe, s["lg_made"], t.seen(6))
                    for h in range(H0):
                        last = mm(PS[:, 6 + h // 4, (h % 4) * J:(h % 4 + 1) * J], T0[:, h, :], ctxa[p])
                    last.then_inc(s["KA_mm"], 1)
                if (b := t.at(3)) is not None:
                    p = t.par(3)
                    pe.wait_ge(s["O0_cp"], b + 1)
                    pe.wait_ge(s["PT0_cpb"], b + 1)
                    for q in range(HD0 // P):
                        last = T.transpose(PS[:, 3, q * P:(q + 1) * P], O0[p][:, q * P:(q + 1) * P], ident[:, :])
                    last.then_inc(s["OT0_mm"], 1)
                if (b := t.at(1)) is not None:
                    p = t.par(1)
                    wait_free(pe, s["V0_cp"], b)
                    wait_free(pe, s["PT0_cpa"], t.seen(3, 1))
                    mm(PS[0:J, 2, :], ctxa[p], wv0[:, :]).then_inc(s["V0_mm"], 1)
                    pe.wait_ge(s["xn1_made"], b + 1)
                    wait_free(pe, s["xT1_cp"], b)
                    wait_free(pe, s["O0_cp"], t.seen(3, 1))
                    T.transpose(PS[:, 5, 0:D], xn1[p], ident[:, :]).then_inc(s["xT1_mm"], 1)
                if (b := t.at(3)) is not None:
                    p = t.par(3)
                    pe.wait_ge(s["OT0_cp"], b + 1)
                    for q in range(HD0 // P):
                        last = mm(PS[:, 4, 0:D], OT0[p][:, q * P:(q + 1) * P], wo0[:, q, :],
                                  start=(q == 0), stop=(q == HD0 // P - 1))
                    last.then_inc(s["Y0_mm"], 1)
                if (b := t.at(5)) is not None:
                    p = t.par(5)
                    pe.wait_ge(s["xn2_made"], b + 1)
                    wait_free(pe, s["xT2_cp"], b)
                    wait_free(pe, s["KA_cp"], t.seen(1, 1))
                    T.transpose(PS[:, 6, 0:D], xn2[p], ident[:, :]).then_inc(s["xT2_mm"], 1)
                if (b := t.at(6)) is not None:
                    p = t.par(6)
                    pe.wait_ge(s["xT2_cp"], b + 1)
                    wait_free(pe, s["lg_made"], b)
                    wait_free(pe, s["KA_cp"], t.seen(1, 1))
                    mm(PS[:, 7, 0:NE], xT2[p], wgs[:, :]).then_inc(s["lg_mm"], 1)

            def route(c):
                pe.wait_ge(s["ro_M"], c + 1)
                pe.wait_ge(s["S0_sub"], min(ROUTE0 - 2, NB) if c == 0 else NB)
                pe.wait_ge(s["xT2_cp"], CB + 1 if c == 0 else NB)
                pe.wait_ge(s["lg_made"], CB * (c + 1))
                pe.wait_ge(s["V0_cp"], ROUTE0 - 1 if c == 0 else NB)
                pe.wait_ge(s["PT0_cpa"], ROUTE0 - 3 if c == 0 else NB)
                mm(PS[:, 0, :], ltri[:, :], rtM)
                mm(PS[:, 1, :], onesb[:, :], rtM).then_inc(s["ro_cnt"], 1)
                pe.wait_ge(s["ro_et"], 2 * c + 1)
                mm(PS[0:1, 2, 0:P], rt["et"], ident[:, :]).then_inc(s["ro_et"], 1)
                pe.wait_ge(s["ro_done"], c + 1)

            for span in route_spans():
                if span is None:
                    route(0)
                else:
                    run_steps(pe, NB, *span, step_a)
            route(1)

            pe.wait_ge(s["moe_loaded"], 64)
            for last in ("OT0_cp", "PT0_cpb", "KA_cp", "xT1_cp", "O0_cp", "x1_made", "xT2_cp", "lg_made"):
                pe.wait_ge(s[last], NB)

            def step_b(t, c):
                base = c * NT
                if (b := t.at(0)) is not None:
                    p = t.par(0)
                    pe.wait_ge(s[f"xs_loaded{p}"], (b + base - p) * 8 + 16)
                    wait_free(pe, s["xsT_cp"], b + base - 1)
                    T.transpose(PS[:, p, 0:D], xsb[p], ident[:, :]).then_inc(s["xsT_mm"], 1)
                if (b := t.at(1)) is not None:
                    p = t.par(1)
                    e = pe.value_load(ETI[0:1, c, bass.ds(b, 1)], min_val=0, max_val=NE - 1)
                    pe.wait_ge(s["xsT_cp"], b + base + 1)
                    wait_free(pe, s["h_made"], b + base - 1)
                    mm(PS[:, 2 + p, 0:EH], xsT[p], W1s[:, bass.ds(e, 1), :].rearrange("q o h -> q (o h)")).then_inc(s["h_mm"], 1)
                if (b := t.at(2)) is not None:
                    p = t.par(2)
                    pe.wait_ge(s["h_made"], b + base + 1)
                    wait_free(pe, s["hT_cp"], b + base - 1)
                    for q in range(2):
                        last = T.transpose(PS[:, 4 + p, q * P:(q + 1) * P], hb[p][:, q * P:(q + 1) * P], ident[:, :])
                    last.then_inc(s["hT_mm"], 1)
                if (b := t.at(3)) is not None:
                    p = t.par(3)
                    e = pe.value_load(ETI[0:1, c, bass.ds(b, 1)], min_val=0, max_val=NE - 1)
                    pe.wait_ge(s["hT_cp"], b + base + 1)
                    wait_free(pe, s["y_made"], b + base - 1)
                    for q in range(2):
                        last = mm(PS[:, 6 + p, 0:D], hT[p][:, q * P:(q + 1) * P],
                                  W2s[:, bass.ds(e, 1), q, :].rearrange("q o d -> q (o d)"), start=(q == 0), stop=(q == 1))
                    last.then_inc(s["y_mm"], 1)

            for c in range(NCH):
                for span in spans(NT, LOOP0, LAST_LAG_B):
                    run_steps(pe, NT, *span, lambda t: step_b(t, c))
            pe.wait_ge(s["y_made"], NCH * NT)
            pe.wait_ge(s["ms"], 12)
            pe.wait_ge(s["kq_step"], 11)

            def step_c(t):
                def transpose_p(b, p, q):
                    for h in range(4 * q, 4 * q + 4):
                        last = T.transpose(PS[0:J, 4 + q % 3, (h % 4) * P:(h % 4 + 1) * P],
                                           P1[p][:, h * J:(h + 1) * J], ident[:, :])
                    last.then_inc(s["PT1_mm"], 1)

                if (b := t.at(5)) is not None:
                    p = t.par(5)
                    pe.wait_ge(s["exp1"], b + 1)
                    wait_free(pe, s["xT3_cp"], t.seen(2))
                    wait_free(pe, s["V1_cp"], t.seen(3))
                    wait_free(pe, s["xqT_cp"], t.seen(8))
                    wait_free(pe, s["QT_cp"], t.seen(3))
                    wait_free(pe, s["x3_made"], t.seen(5))
                    wait_free(pe, s["KB_made"], t.seen(3))
                    for q in range(3):
                        transpose_p(b, p, q)
                if (b := t.at(4)) is not None:
                    p = t.par(4)
                    pe.wait_ge(s["QT_cp"], b + 1)
                    pe.wait_ge(s["KB_made"], b + 1)
                    wait_free(pe, s["S1_sub"], b)
                    for q in range(NG):
                        last = mm(PS[:, q, 0:GH * J], QT1[p][32 * q:32 * q + 32, :], KB1[p][32 * q:32 * q + 32, :])
                    last.then_inc(s["S1_mm"], 1)
                if (b := t.at(5)) is not None:
                    p = t.par(5)
                    pe.wait_ge(s["PT1_cpa"], 2 * b + 1)
                    transpose_p(b, p, 3)
                    pe.wait_ge(s["PT1_cpb"], 2 * b + 1)
                    wait_free(pe, s["y4_made"], t.seen(8))
                    wait_free(pe, s["OT1_cp"], b)
                    for h in range(H1):
                        if h == 8:
                            pe.wait_ge(s["PT1_cpa"], 2 * b + 2)
                        if h == 12:
                            pe.wait_ge(s["PT1_cpb"], 2 * b + 2)
                        last = mm(PS[:, 7, h * VW1:(h + 1) * VW1], PT1[:, h * P:(h + 1) * P],
                                  V1[p][:, h * VW1:(h + 1) * VW1])
                    last.then_inc(s["O1_mm"], 1)
                if (b := t.at(3)) is not None:
                    p = t.par(3)
                    pe.wait_ge(s["ctxc_loaded"], b * 16 + 16)
                    wait_free(pe, s["PT1_cpa"], 2 * t.seen(5, 1))
                    wait_free(pe, s["PT1_cpb"], 2 * t.seen(5, 1))
                    wait_free(pe, s["xT3_cp"], t.seen(2))
                    wait_free(pe, s["x3_made"], t.seen(5))
                    wait_free(pe, s["xqT_cp"], t.seen(8))
                    mm(PS[:, 6, 0:J], wk1[:, :], ctxc[p]).then_inc(s["KT_mm"], 1)
                    mm(PS[0:J, 4, 0:D], ctxc[p], wv1[:, :]).then_inc(s["V1_mm"], 1)
                    pe.wait_ge(s["xT3_cp"], b + 1)
                    mm(PS[:, 5, 0:D], wq1[:, :], xT3[p]).then_inc(s["QT_mm"], 1)
                if (b := t.at(2)) is not None:
                    p = t.par(2)
                    pe.wait_ge(s["xn3_made"], b + 1)
                    wait_free(pe, s["xT3_cp"], b)
                    wait_free(pe, s["V1_cp"], t.seen(3, 1))
                    wait_free(pe, s["PT1_cpb"], 2 * t.seen(5, 1))
                    T.transpose(PS[:, 4, 0:D], xn3[p], ident[:, :]).then_inc(s["xT3_mm"], 1)
                if (b := t.at(5)) is not None:
                    p = t.par(5)
                    pe.wait_ge(s["O1_cp"], b + 1)
                    T.transpose(PS[:, 7, 0:D], O1[p], ident[:, :]).then_inc(s["OT1_mm"], 1)
                if (b := t.at(8)) is not None:
                    p = t.par(8)
                    pe.wait_ge(s["xq4_made"], b + 1)
                    wait_free(pe, s["xqT_cp"], b)
                    wait_free(pe, s["QT_cp"], t.seen(3, 1))
                    wait_free(pe, s["PT1_cpb"], 2 * t.seen(5, 1))
                    T.transpose(PS[:, 5, 0:D // 2].bitcast(BF16), xq4[p], identb[:, :]).then_inc(s["xqT_mm"], 1)
                if (b := t.at(5)) is not None:
                    p = t.par(5)
                    pe.wait_ge(s["OT1_cp"], b + 1)
                    wait_free(pe, s["x3_made"], b)
                    wait_free(pe, s["KB_made"], t.seen(3, 1))
                    wait_free(pe, s["PT1_cpa"], 2 * t.seen(5, 1))
                    mm(PS[:, 6, 0:D], OT1[p], wo1[:, :]).then_inc(s["Y1_mm"], 1)
                if (b := t.at(8)) is not None:
                    p = t.par(8)
                    pe.wait_ge(s["xqT_cp"], b + 1)
                    wait_free(pe, s["OT1_cp"], t.seen(5, 1))
                    wait_free(pe, s["y4_made"], b)
                    mm(PS[:, 7, 0:D], xqT4[p], kq[:, :]).then_inc(s["y4_mm"], 1)

            for span in c_spans():
                run_steps(pe, NB, *span, step_c)


EXP_BITS = 0x7F800000
FP8_LEAST = 2.0 ** -6
FP8_ROUND = 1.5 * 2.0 ** 20
FP8_TOP = 3.4028234e38 / 464.5


_INS = {"x": "x", "g_xattn": "g_xattn", "g_ffn": "g_ffn", "gamma": "L0_xattn_gamma", "beta": "L0_xattn_beta",
        "Wout": "L0_xattn_Wout", "Wg": "L0_ffn_Wg", "bg": "L0_ffn_bg", "bias": "L0_ffn_bias",
        "W1": "L0_ffn_W1", "b1": "L0_ffn_b1", "W2": "L0_ffn_W2", "b2": "L0_ffn_b2",
        "Wq1": "L1_xattn_Wq", "bq1": "L1_xattn_bq", "Wk1": "L1_xattn_Wk", "bk1": "L1_xattn_bk",
        "Wv1": "L1_xattn_Wv", "bv1": "L1_xattn_bv", "Wo1": "L1_xattn_Wo", "bo1": "L1_xattn_bo",
        "kernel": "L1_ffn_kernel", "input_scale": "L1_ffn_input_scale", "kernel_scale": "L1_ffn_kernel_scale",
        "ffn_bias": "L1_ffn_bias"}


def kernel(**inputs):
    import numpy as np
    import concourse.bacc as bacc
    from concourse.bass_utils import run_bass_kernel_spmd

    data = {name: np.ascontiguousarray(inputs[full]) for name, full in _INS.items()}
    heads, dh = 8, 64
    wq, wkv = np.asarray(inputs["L0_xattn_Wq"]), np.asarray(inputs["L0_xattn_Wkv"])
    d, inner = wq.shape
    data["WqT"] = np.ascontiguousarray(wq.reshape(d, heads, dh).transpose(2, 1, 0)).reshape(dh, heads * d)
    data["WkT"] = np.ascontiguousarray(wkv[:, :inner].reshape(d, heads, dh).transpose(2, 1, 0)).reshape(dh, heads * d)
    data["Wv"] = np.ascontiguousarray(wkv[:, inner:])
    data["ctxT"] = np.ascontiguousarray(np.asarray(inputs["ctx_1024"]).transpose(0, 2, 1))

    nc = bacc.Bacc("TRN2", target_bir_lowering=False, num_devices=1)
    aps, arrays = {}, {}
    for name, v in data.items():
        arrays[f"in_{name}"] = v
        aps[name] = nc.dram_tensor(f"in_{name}", v.shape, mybir.dt.from_np(v.dtype), kind="ExternalInput").ap()
    out = nc.dram_tensor("out", data["x"].shape, F32, kind="ExternalOutput").ap()
    nb, n, dd = data["x"].shape
    nt = (nb * n + 16 * 127) // 128
    nt += nt % 2
    xs = [nc.dram_tensor(f"moe_rows{c}", (nt * 128, dd), F32, kind="Internal").ap() for c in range(2)]
    ys = [nc.dram_tensor(f"moe_results{c}", (nt * 128, dd), F32, kind="Internal").ap() for c in range(2)]
    flamingo_two_layers(nc, aps, out, xs, ys)
    r = run_bass_kernel_spmd(nc, [arrays], core_ids=[0])
    return r.results[0]["out"]
```

```python
import concourse.bass as bass
from concourse import mybir
from contextlib import ExitStack

F32 = mybir.dt.float32
BF16 = mybir.dt.bfloat16
I32 = mybir.dt.int32
ALU = mybir.AluOpType
ACT = mybir.ActivationFunctionType
X = mybir.AxisListType.X
P = 128


class Step:

    def __init__(self, value, place, count, turn=None, per_turn=2):
        self.value, self.place, self.count, self.turn, self.per_turn = value, place, count, turn, per_turn

    def at(self, lag):
        if isinstance(self.value, int):
            b = self.value - lag
            return b if 0 <= b < self.count else None
        return self.value - lag

    def par(self, lag):
        return (self.place - lag) % 2

    def ring(self, lag, size):
        return (self.place - lag) % size

    def seen(self, lag, now=0):
        n = self.value - lag + now
        return min(max(n, 0), self.count) if isinstance(n, int) else n


def run_steps(engine, count, first, last, peeled, body, per_turn=2):
    if peeled:
        for t in range(first, last):
            body(Step(t, t % per_turn, count))
    else:
        assert first % per_turn == 0 and last % per_turn == 0
        with engine.Fori(first // per_turn, last // per_turn) as turn:
            for p in range(per_turn):
                body(Step(turn * per_turn + p, p, count, turn, per_turn))


def wait_free(engine, sem, value):
    if isinstance(value, int) and value <= 0:
        return
    engine.wait_ge(sem, value)


class Experts:

    def __init__(self, engine, table):
        self.engine, self.table, self.words = engine, table, {}

    def of(self, t, c, lag):
        if isinstance(t.value, int):
            word, k = divmod(t.at(lag), 4)
            key = (c, word)
        else:
            group, k = divmod(t.place - lag, 4)
            word = t.turn * (t.per_turn // 4) + group
            key = (c, "turn", group)
            if t.place == 0:
                self.words = {}
        if key not in self.words:
            self.words[key] = self.engine.value_load(self.table[0:1, c, bass.ds(word, 1)], min_val=0, max_val=0xFFFF)
        return (self.words[key] >> (4 * k)) & 15


def wait_edge(engine, t, sem, value):
    if isinstance(t.value, int):
        wait_free(engine, sem, value)


def flamingo_two_layers(nc, a, out, xs_dram, ys_dram):
    NB, N, D = a["x"].shape
    J = a["ctxT"].shape[2]
    H0 = 8
    DH0 = a["WqT"].shape[0]
    HD0 = H0 * DH0
    H1, DH1 = 16, D // 16
    NE, EH = a["b1"].shape
    EPS = 1e-5
    NCH = 2
    CB = NB // NCH
    NT = (2 * CB * N + NE * (P - 1)) // P
    GT = 4
    NT += -NT % (2 * GT)
    NG_B = NT // GT
    HB0 = H0 // 2
    VW0 = DH0 + 1
    VW1 = DH1 + 1
    GH = 4
    NG = H1 // GH
    HH = H1 // 2
    PT_BANK = (4, 5, 6, 4)
    LOOP0 = 8
    LAST_LAG_A = 6
    LAST_LAG_B = 6
    LAST_LAG_C = 11
    LOOPC = 12
    ROUTE0 = CB + LAST_LAG_A
    assert ROUTE0 % 2 == 0

    ctx = ExitStack()
    with ctx:
        def sb(name, shape, dt=F32):
            return ctx.enter_context(nc.sbuf_tensor(name, shape, dt))

        def sem(name):
            return ctx.enter_context(nc.semaphore(name))

        XR = sb("residual", [P, NB, D])
        XN = sb("moe_in", [P, NB, D])
        W1s = sb("w1", [P, NE, EH])
        W2s = sb("w2", [P, NE, 2, D])
        b1s = sb("b1_rows", [P, NE, EH])
        b2s = sb("b2_rows", [P, NE, D])
        LG = sb("logits", [P, NB, NE])
        WT = [sb(f"gate_w{k}", [P, NB]) for k in range(2)]
        POS = [sb(f"slot{k}", [P, NB], I32) for k in range(2)]
        ETI = sb("tile_experts", [1, NCH, P // 4], I32)
        ident = sb("ident", [P, P])
        identb = sb("identb", [P, P], BF16)
        ltri = sb("before", [P, P], BF16)
        onesb = sb("onesb", [P, P], BF16)
        iotaD = sb("rank_of_expert", [P, NE])
        tau = sb("tile_start", [P, 1])
        nfirst = sb("not_first", [P, NE, CB])
        mask4 = sb("head_of_row", [P, GH])
        mhalf = sb("minus_half", [P, 1])
        tg = sb("tanh_gates", [P, 4])
        gamma = sb("gamma", [P, 1])
        beta = sb("beta", [P, 1])
        wgs = sb("wg", [P, NE])
        lbias = sb("logit_bias", [P, 2, NE])
        T0 = sb("wk_wq", [P, H0, D])
        wv0 = sb("wv0", [P, HD0])
        wo0 = sb("wo0", [P, HD0 // P, D])
        wq1 = sb("wq1", [P, D])
        wk1 = sb("wk1", [P, D])
        wv1 = sb("wv1", [P, D])
        wo1 = sb("wo1", [P, D])
        bq1 = sb("bq1", [P, 1])
        bk1 = sb("bk1", [P, 1])
        bv1 = sb("bv1", [P, D])
        bo1 = sb("bo1", [P, D])
        kf = sb("ffn_kernel", [P, D], BF16)
        kq = sb("ffn_kernel_q", [P, D], BF16)
        sc = sb("ffn_scales", [P, 2])
        scr = sb("ffn_rscales", [P, 2])
        scm = sb("ffn_scale_product", [P, 1])
        fbias = sb("ffn_bias", [P, D], BF16)
        ZR, ZP = NT * P // CB, P // 2
        zt = sb("zeros", [ZP, ZR // ZP * D])

        PS = ctx.enter_context(nc.psum_tensor("PS", [P, 8, 512], F32))

        AW = 14400
        arena = sb("arena", [P, AW])

        class Carver:
            def __init__(self):
                self.at = 0

            def __call__(self, width, parts=P):
                v = arena[0:parts, self.at:self.at + width]
                self.at += width
                assert self.at <= AW, self.at
                return v

        ca = Carver()
        one16 = ca(NE)
        scat = [ca(D) for _ in range(2)]
        si = [ca(1).bitcast(I32) for _ in range(4)]
        after_scatter = ca.at
        ctxa = [ca(J) for _ in range(2)]
        mv1 = [ca(2) for _ in range(2)]
        st1 = ca(6)
        rs1 = [ca(2) for _ in range(2)]
        xn1 = [ca(D) for _ in range(2)]
        xT1 = [ca(D) for _ in range(2)]
        KA = [ca(H0 * J) for _ in range(2)]
        V0 = [ca(H0 * VW0, J) for _ in range(2)]
        S0 = [ca(H0 * J) for _ in range(2)]
        P0 = [ca(H0 * J) for _ in range(2)]
        mx0 = ca(H0)
        PT0 = [ca(H0 * P, J) for _ in range(2)]
        rd0 = ca(H0)
        O0 = [ca(HD0) for _ in range(2)]
        OT0 = [ca(HD0) for _ in range(2)]
        mv2 = [ca(2) for _ in range(2)]
        st2 = ca(6)
        rs2 = [ca(2) for _ in range(2)]
        xn2 = [ca(D) for _ in range(2)]
        xT2 = [ca(D) for _ in range(2)]
        after_a = ca.at
        rt = {}
        for name, width in (("v0", CB), ("v1", CB), ("eq", CB * NE), ("m", CB), ("oh0", CB * NE),
                            ("oh1", CB * NE), ("lg2", CB * NE), ("e", CB), ("s", CB), ("cum", NE * CB),
                            ("pos", NE * CB), ("tot", NE), ("pad", NE), ("inc", NE), ("base", NE),
                            ("et", 1), ("le", NE), ("pk", P), ("pk2", P // 2)):
            rt[name] = ca(width)
        rtM = ca(NE * CB // 2).bitcast(BF16)
        rti = ca(NE).bitcast(I32)
        cb = Carver()
        cb.at = after_scatter
        xsb = [cb(GT * D).rearrange("p (k d) -> p k d", d=D) for _ in range(2)]
        xsT = [cb(D) for _ in range(2)]
        hb = [cb(EH) for _ in range(2)]
        hT = [cb(EH) for _ in range(2)]
        yb = [cb(GT * D).rearrange("p (k d) -> p k d", d=D) for _ in range(2)]
        cc = Carver()
        gy = [[cc(D) for _ in range(2)] for _ in range(2)]
        gi = [[cc(1).bitcast(I32) for _ in range(2)] for _ in range(2)]
        ctxc = [cc(J) for _ in range(2)]
        uc = cc(D)
        mv3 = [cc(2) for _ in range(2)]
        st3 = cc(6)
        rs3 = [cc(2) for _ in range(2)]
        xn3 = [cc(D) for _ in range(2)]
        xT3 = [cc(D) for _ in range(2)]
        QT1 = [cc(NG * D) for _ in range(2)]
        KB1 = [cc(GH * J) for _ in range(2)]
        V1 = [cc(H1 * VW1, J) for _ in range(2)]
        S1 = cc(H1 * J)
        P1 = [cc(H1 * J) for _ in range(2)]
        mx1 = cc(H1)
        PT1 = cc(H1 * P, J)
        rd1 = cc(H1)
        O1 = [cc(D) for _ in range(2)]
        OT1 = [cc(D) for _ in range(2)]
        mv4 = [cc(2) for _ in range(2)]
        st4 = cc(6)
        rs4 = [cc(2) for _ in range(2)]
        xb4 = cc(D // 2).bitcast(BF16)
        z4 = [cc(D) for _ in range(2)]
        c4 = [cc(D) for _ in range(2)]
        q4 = cc(D)
        n4 = cc(D)
        t4 = cc(D)
        xq4 = [cc(D // 2).bitcast(BF16) for _ in range(2)]
        xqT4 = [cc(D // 2).bitcast(BF16) for _ in range(2)]
        y4 = [cc(D // 2).bitcast(BF16) for _ in range(2)]
        y4b = [cc(D // 2).bitcast(BF16) for _ in range(2)]
        ob = [cc(D) for _ in range(2)]
        cs = Carver()
        cs.at = after_a
        wqT = cs(H0 * D, DH0)
        wkT = cs(H0 * D, DH0)
        ksz = cs(D)
        ksc = cs(D)
        ksq = cs(D)

        names = """w_loaded w1_loaded moe_loaded ms consts ident_made tau_made mask_made
            t0_mm t0_cp tanh_made kq_step lb_made zero_made xs_zeroed0 xs_zeroed1
            x_loaded ctx_loaded stats1 agg1 rst1 rs1_made xn1_made xT1_mm xT1_cp KA_mm KA_cp V0_mm V0_cp S0_mm mx0_made
            S0_sub exp0 PT0_mm PT0_cpa PT0_cpb O0_mm rd0_made O0_cp OT0_mm OT0_cp Y0_mm x1_made
            stats2 agg2 rst2 rs2_made xn2_made XN_kept xT2_mm xT2_cp lg_mm lg_made
            ro ro_M ro_e ro_cnt ro_et ro_done ro_exp idx_made scat_made0 scat_made1
            xs_loaded0 xs_loaded1 xsT_mm xsT_cp h_mm h_made hT_mm hT_cp y_mm y_made ys_stored0 ys_stored1
            gi_made gy_made0 gy_made1 ctxc_loaded u_made x2_made x2b_made stats3 agg3 rst3 rs3_made xn3_made xT3_mm xT3_cp
            QT_mm QT_cp KT_mm KB_made V1_mm V1_cp S1_mm mx1_made S1_sub exp1
            PT1_mm PT1_cp O1_mm rd1_made O1_cp OT1_mm OT1_cp Y1_mm x3_made stats4 agg4 rst4 rs4_made xb4_made
            z4_made m4_made c4_made t4_made q4_made n4_made xq4_made xqT_mm xqT_cp y4_mm y4_made y4b_made ob_made out_stored0 out_stored1""".split()
        s = {n: sem(n) for n in names}

        block = ctx.enter_context(nc.Block())

        xs_flat = [xs_dram[c] for c in range(NCH)]
        ys_flat = [ys_dram[c] for c in range(NCH)]
        x_rows = a["x"].rearrange("b n d -> (b n) d")
        out_rows = out.rearrange("b n d -> (b n) d")
        w1_rows = a["W1"].rearrange("e d h -> (e d) h")
        w2_rows = a["W2"].rearrange("e h d -> (e h) d")
        ctx_rows = a["ctxT"].rearrange("b d j -> (b d) j")

        def apart(engine):
            engine.nop(nofuse=True)

        def row(ap, parts=P):
            return ap.rearrange("(o n) -> o n", o=1).to_broadcast([parts, ap.shape[0]])

        def col(ap):
            return ap.rearrange("(n o) -> n o", o=1)

        def route_spans():
            return [(0, LOOP0, True), (LOOP0, ROUTE0, False), None,
                    (ROUTE0, ROUTE0 + 2, True), (ROUTE0 + 2, NB, False),
                    (NB, NB + LAST_LAG_A, True)]

        def spans(count, lead, lag):
            return [(0, lead, True), (lead, count, False), (count, count + lag, True)]

        def c_spans():
            return [(0, LOOPC, True), (LOOPC, CB, False), (CB, NB, False), (NB, NB + LAST_LAG_C, True)]

        loads = [(wqT, a["WqT"]), (wkT, a["WkT"]), (gamma[:, :], col(a["gamma"])), (beta[:, :], col(a["beta"])),
                 (wv0[:, :], a["Wv"]), (wo0[:, :, :], a["Wout"].rearrange("(c p) n -> p c n", p=P)),
                 (tg[:, 0:2], row(a["g_xattn"])), (tg[:, 2:4], row(a["g_ffn"])),
                 (wgs[:, :], a["Wg"]), (lbias[:, 0, :], row(a["bg"])), (lbias[:, 1, :], row(a["bias"])),
                 ]
        loads1 = [(wq1[:, :], a["Wq1"]), (wk1[:, :], a["Wk1"]), (wv1[:, :], a["Wv1"]), (wo1[:, :], a["Wo1"]),
                 (bq1[:, :], col(a["bq1"])), (bk1[:, :], col(a["bk1"])), (bv1[:, :], row(a["bv1"])),
                 (bo1[:, :], row(a["bo1"])), (kf[:, :], a["kernel"]), (sc[:, 0:1], row(a["input_scale"])),
                 (sc[:, 1:2], row(a["kernel_scale"])), (fbias[:, :], row(a["ffn_bias"]))]

        @block.sync
        def _(sp):
            def load_x(b):
                wait_free(sp, s["x_loaded"], b * 16)
                sp.dma_start(XR[:, bass.ds(b, 1), :].rearrange("p o d -> p (o d)"),
                             x_rows[bass.ds(b * N, N), :]).then_inc(s["x_loaded"], 16)

            def load_ctx(b, dst, loaded, free):
                wait_free(sp, s[loaded], b * 16)
                apart(sp)
                wait_free(sp, s[free], b - 1)
                sp.dma_start(dst, ctx_rows[bass.ds(b * D, D), :]).then_inc(s[loaded], 16)

            load_x(0)
            load_x(1)
            load_ctx(0, ctxa[0], "ctx_loaded", "V0_mm")
            for dst, src in loads:
                sp.dma_start(dst, src).then_inc(s["w_loaded"], 16)
            load_ctx(1, ctxa[1], "ctx_loaded", "V0_mm")

            def clear(c, b):
                sp.dma_start(xs_flat[c][bass.ds(b * ZR, ZR), :].rearrange("(p r) d -> p (r d)", p=ZP),
                             zt[:, :]).then_inc(s[f"xs_zeroed{c}"], 16)

            sp.wait_ge(s["ms"], 10)
            for dst, src in loads1:
                sp.dma_start(dst, src).then_inc(s["w1_loaded"], 16)
            clear(0, 0)
            clear(0, 1)
            with sp.Fori(1, CB // 2) as turn:
                for p in range(2):
                    load_x(turn * 2 + p)
                    load_ctx(turn * 2 + p, ctxa[p], "ctx_loaded", "V0_mm")
                    clear(0, turn * 2 + p)
            with sp.Fori(CB // 2, NB // 2) as turn:
                for p in range(2):
                    load_x(turn * 2 + p)
                    load_ctx(turn * 2 + p, ctxa[p], "ctx_loaded", "V0_mm")
                    clear(1, turn * 2 + (p - CB))
                    e = turn - CB // 2
                    if p == 0:
                        sp.dma_start(W1s[:, bass.ds(e, 1), :].rearrange("p o h -> p (o h)"),
                                     w1_rows[bass.ds(e * D, D), :]).then_inc(s["moe_loaded"], 16)
                        sp.dma_start(W2s[:, bass.ds(e, 1), :, :].rearrange("p o c d -> p (o c) d"),
                                     w2_rows[bass.ds(e * EH, EH), :].rearrange("(c p) d -> p c d", p=P)).then_inc(s["moe_loaded"], 16)
                    else:
                        sp.dma_start(b1s[:, bass.ds(e, 1), :].rearrange("p o h -> p (o h)"),
                                     a["b1"][bass.ds(e, 1), :].to_broadcast([P, EH])).then_inc(s["moe_loaded"], 16)
                        sp.dma_start(b2s[:, bass.ds(e, 1), :].rearrange("p o h -> p (o h)"),
                                     a["b2"][bass.ds(e, 1), :].to_broadcast([P, D])).then_inc(s["moe_loaded"], 16)
            for c in range(NCH):
                sp.wait_ge(s[f"xs_zeroed{c}"], 16 * CB)
                for p in range(2):
                    sp.wait_ge(s[f"scat_made{p}"], 16 * CB * (c + 1))

                def load_group(g, p):
                    gg = g + c * NG_B
                    wait_free(sp, s[f"xs_loaded{p}"], (gg - p) * 8)
                    apart(sp)
                    wait_free(sp, s["xsT_mm"], (gg - 1) * GT)
                    sp.dma_start(xsb[p], xs_flat[c][bass.ds(g * GT * P, GT * P), :].rearrange(
                        "(k p) d -> p k d", p=P)).then_inc(s[f"xs_loaded{p}"], 16)

                def store_group(g, p):
                    gg = g + c * NG_B
                    sp.wait_ge(s["y_made"], gg * GT + GT)
                    apart(sp)
                    wait_free(sp, s[f"ys_stored{p}"], (gg - p) * 8)
                    sp.dma_start(ys_flat[c][bass.ds(g * GT * P, GT * P), :].rearrange("(k p) d -> p k d", p=P),
                                 yb[p]).then_inc(s[f"ys_stored{p}"], 16)

                load_group(0, 0)
                load_group(1, 1)
                for g in range(2, 4):
                    load_group(g, g % 2)
                    store_group(g - 2, g % 2)
                with sp.Fori(2, NG_B // 2) as turn:
                    for p in range(2):
                        load_group(turn * 2 + p, p)
                        store_group(turn * 2 + (p - 2), p)
                for g in range(NG_B - 2, NG_B):
                    store_group(g, g % 2)
            sp.wait_ge(s["lg_made"], NB)
            load_ctx(0, ctxc[0], "ctxc_loaded", "V1_mm")
            load_ctx(1, ctxc[1], "ctxc_loaded", "V1_mm")

            def store_out(b, p):
                sp.wait_ge(s["ob_made"], b + 1)
                wait_free(sp, s[f"out_stored{p}"], (b - p) * 8)
                sp.dma_start(out_rows[bass.ds(b * N, N), :], ob[p]).then_inc(s[f"out_stored{p}"], 16)

            for b in range(2, 10):
                load_ctx(b, ctxc[b % 2], "ctxc_loaded", "V1_mm")
            with sp.Fori(5, NB // 2) as turn:
                for p in range(2):
                    load_ctx(turn * 2 + p, ctxc[p], "ctxc_loaded", "V1_mm")
                    store_out(turn * 2 + (p - 10), p)
            for b in range(NB - 10, NB):
                store_out(b, b % 2)
            for p in range(2):
                sp.wait_ge(s[f"out_stored{p}"], NB // 2 * 16)

        @block.gpsimd
        def _(pool):
            g = nc.gpsimd
            g.memset(ident[:, :], 0.0).then_inc(s["ms"], 1)
            g.memset(identb[:, :], 0.0).then_inc(s["ms"], 1)
            g.memset(onesb[:, :], 1.0).then_inc(s["ms"], 1)
            g.memset(nfirst[:, :, :], 1.0).then_inc(s["ms"], 1)
            g.memset(mask4[:, :], 1.0).then_inc(s["ms"], 1)
            g.memset(zt[:, :], 0.0).then_inc(s["ms"], 1)
            g.memset(one16, 1.0).then_inc(s["ms"], 1)
            g.memset(mhalf[:, :], -0.5).then_inc(s["ms"], 1)
            pool.wait_ge(s["ms"], 8)
            for p in range(2):
                vv = V0[p].rearrange("j (h w) -> j h w", h=H0)
                g.memset(vv[:, :, VW0 - 1:VW0], 1.0).then_inc(s["ms"], 1)
            pool.wait_ge(s["ms"], 10)
            for m in (ident, identb):
                g.affine_select(out=m[:, :], in_=m[:, :], compare_op=ALU.not_equal, fill=1.0, base=0,
                                pattern=[[-1, P]], channel_multiplier=1).then_inc(s["consts"], 1)
            g.affine_select(out=ltri[:, :], in_=onesb[:, :], compare_op=ALU.is_ge, fill=0.0, base=-1,
                            pattern=[[1, P]], channel_multiplier=-1).then_inc(s["consts"], 1)
            g.iota(iotaD[:, :], pattern=[[-1, NE]], base=NE, channel_multiplier=0,
                   allow_small_or_imprecise_dtypes=True).then_inc(s["consts"], 1)
            g.iota(tau[:, :], pattern=[[0, 1]], base=0, channel_multiplier=P,
                   allow_small_or_imprecise_dtypes=True).then_inc(s["consts"], 1)
            g.memset(nfirst[:, :, 0:1], 0.0).then_inc(s["consts"], 1)
            for q in range(P // 32):
                m = mask4[32 * q:32 * q + 32, :]
                wait_free(pool, s["mask_made"], 2 * q)
                g.affine_select(out=m, in_=m, compare_op=ALU.is_ge, fill=0.0, base=0,
                                pattern=[[-DH1, GH]], channel_multiplier=1).then_inc(s["mask_made"], 1)
                pool.wait_ge(s["mask_made"], 2 * q + 1)
                g.affine_select(out=m, in_=m, compare_op=ALU.is_ge, fill=0.0, base=DH1 - 1,
                                pattern=[[DH1, GH]], channel_multiplier=-1).then_inc(s["mask_made"], 1)
            pool.wait_ge(s["mask_made"], 2 * P // 32)
            def rstd(mv, rs, agg, mid, made, b, scale, shift, last_use):
                pool.wait_ge(s[agg], b + 1)
                wait_free(pool, s[last_use], b - 1)
                apart(pool)
                g.tensor_scalar(rs[:, 0:1], mv[:, 1:2], scale, shift, ALU.mult, ALU.add).then_inc(s[mid], 1)
                pool.wait_ge(s[mid], b + 1)
                g.tensor_tensor(rs[:, 1:2], rs[:, 0:1], mhalf[:, :], ALU.pow).then_inc(s[made], 1)

            def scatter(c, b, p):
                bb = b + c * CB
                wait_free(pool, s[f"scat_made{p}"], (bb - p) * 16)
                g.tensor_copy(scat[p], XN[:, bass.ds(bb, 1), :].rearrange("q o d -> q (o d)")).then_inc(s["idx_made"], 1)
                for k in range(2):
                    g.tensor_copy(si[2 * p + k], POS[k][:, bass.ds(bb, 1)]).then_inc(s["idx_made"], 1)
                pool.wait_ge(s["idx_made"], bb * 3 + 3)
                apart(pool)
                for k in range(2):
                    g.indirect_dma_start(out=xs_flat[c][:, :], out_offset=bass.IndirectOffsetOnAxis(ap=si[2 * p + k], axis=0),
                                         in_=scat[p], in_offset=None).then_inc(s[f"scat_made{p}"], 16)

            def step_a(t):
                if (b := t.at(4)) is not None:
                    p = t.par(4)
                    rstd(mv2[p], rs2[p], "agg2", "rst2", "rs2_made", b, 1.0, EPS, "xn2_made")
                if (b := t.at(0)) is not None:
                    p = t.par(0)
                    rstd(mv1[p], rs1[p], "agg1", "rst1", "rs1_made", b, 1.0 + EPS, EPS * EPS, "xn1_made")
                if (b := t.at(5)) is not None:
                    pool.wait_ge(s["xn2_made"], b + 1)
                    g.tensor_copy(XN[:, bass.ds(b, 1), :].rearrange("q o d -> q (o d)"), xn2[t.par(5)]).then_inc(s["XN_kept"], 1)

            for span in route_spans():
                if span is None:
                    pool.wait_ge(s["ro_done"], 1)
                    pool.wait_ge(s["xs_zeroed0"], 16 * CB)
                    continue
                first, last, peeled = span

                def step(t):
                    step_a(t)
                    if first >= ROUTE0:
                        v = t.value - ROUTE0
                        scatter(0, v, t.par(ROUTE0))
                run_steps(pool, NB, first, last, peeled, step)
            pool.wait_ge(s["ro_done"], 2)
            pool.wait_ge(s["xs_zeroed1"], 16 * CB)
            pool.wait_ge(s["XN_kept"], NB)
            with pool.Fori(0, CB // 2) as turn:
                for p in range(2):
                    scatter(1, turn * 2 + p, p)
            pool.wait_ge(s["w1_loaded"], 16 * len(loads1))
            for p in range(2):
                pool.wait_ge(s[f"ys_stored{p}"], NCH * NG_B // 2 * 16)
            for p in range(2):
                vv = V1[p].rearrange("j (h w) -> j h w", h=H1)
                g.memset(vv[:, :, VW1 - 1:VW1], 1.0).then_inc(s["ms"], 1)
                g.memset(QT1[p], 0.0).then_inc(s["ms"], 1)
            pool.wait_ge(s["ms"], 14)

            def gather(b, p, c):
                wait_free(pool, s["x2_made"], b - 1)
                for k in range(2):
                    g.tensor_copy(gi[k][p], POS[k][:, bass.ds(b, 1)]).then_inc(s["gi_made"], 1)
                pool.wait_ge(s["gi_made"], b * 2 + 2)
                apart(pool)
                for k in range(2):
                    g.indirect_dma_start(out=gy[k][p], out_offset=None, in_=ys_flat[c][:, :],
                                         in_offset=bass.IndirectOffsetOnAxis(ap=gi[k][p], axis=0)).then_inc(s[f"gy_made{p}"], 16)

            def step_c(t):
                if (b := t.at(3)) is not None:
                    pool.wait_ge(s["xn3_made"], b + 1)
                    g.tensor_tensor(XR[:, bass.ds(b, 1), :].rearrange("q o d -> q (o d)"),
                                    XR[:, bass.ds(b, 1), :].rearrange("q o d -> q (o d)"), bo1[:, :], ALU.add).then_inc(s["x2b_made"], 1)
                if (b := t.at(10)) is not None:
                    p = t.par(10)
                    pool.wait_ge(s["y4_made"], b + 1)
                    wait_free(pool, s["ob_made"], b - 1)
                    g.tensor_tensor(y4b[p], y4[p], fbias[:, :], ALU.add).then_inc(s["y4b_made"], 1)
                if (b := t.at(7)) is not None:
                    p = t.par(7)
                    rstd(mv4[p], rs4[p], "agg4", "rst4", "rs4_made", b, 1.0, EPS, "xb4_made")
                if (b := t.at(0)) is not None:
                    gather(b, t.par(0), t.chunk)
                if (b := t.at(8)) is not None:
                    p = t.par(8)
                    pool.wait_ge(s["c4_made"], b + 1)
                    wait_free(pool, s["xq4_made"], b)
                    g.tensor_tensor(t4, z4[p], c4[p], ALU.add).then_inc(s["t4_made"], 1)
                    apart(pool)
                    g.tensor_scalar(n4, z4[p], FP8_TOP, 0.0, ALU.mult, ALU.mult).then_inc(s["n4_made"], 1)
                    pool.wait_ge(s["t4_made"], b + 1)
                    g.tensor_tensor(q4, t4, c4[p], ALU.subtract).then_inc(s["q4_made"], 1)
                    pool.wait_ge(s["n4_made"], b + 1)
                    pool.wait_ge(s["q4_made"], b + 1)
                    wait_free(pool, s["xqT_mm"], b - 1)
                    g.tensor_tensor(xq4[p], q4, n4, ALU.add).then_inc(s["xq4_made"], 1)
                if (b := t.at(1)) is not None:
                    p = t.par(1)
                    rstd(mv3[p], rs3[p], "agg3", "rst3", "rs3_made", b, 1.0, EPS, "xn3_made")

            for first, last, peeled in c_spans():
                def step(t):
                    t.chunk = 0 if first < CB else 1
                    step_c(t)
                run_steps(pool, NB, first, last, peeled, step)

        @block.scalar
        def _(act):
            A = nc.scalar

            def cp(o, i, done):
                A.activation(o, i, ACT.Copy).then_inc(s[done], 1)

            act.wait_ge(s["w_loaded"], 16 * len(loads))
            A.activation(tg[:, :], tg[:, :], ACT.Tanh).then_inc(s["tanh_made"], 1)
            for k in range(2):
                act.wait_ge(s["t0_mm"], k + 1)
                cp(T0[:, 4 * k:4 * k + 4, :].rearrange("p h d -> p (h d)"), PS[:, k, :], "t0_cp")

            def step_a(t):
                if (b := t.at(3)) is not None:
                    act.wait_ge(s["PT0_mm"], 2 * b + 1)
                    cp(PT0[t.par(3)][:, 0:HB0 * P], PS[0:J, 2, :], "PT0_cpa")
                if (b := t.at(2)) is not None:
                    act.wait_ge(s["S0_sub"], b + 1)
                    A.activation(P0[t.par(2)], S0[t.par(2)], ACT.Exp, scale=DH0 ** -0.5).then_inc(s["exp0"], 1)
                if (b := t.at(3)) is not None:
                    act.wait_ge(s["OT0_mm"], b + 1)
                    wait_free(act, s["Y0_mm"], b - 1)
                    cp(OT0[t.par(3)], PS[:, 3, :], "OT0_cp")
                if (b := t.at(1)) is not None:
                    p = t.par(1)
                    act.wait_ge(s["KA_mm"], b + 1)
                    wait_free(act, s["S0_mm"], b - 1)
                    cp(KA[p].rearrange("p (k w) -> p k w", k=2), PS[:, 6:8, 0:HB0 * J], "KA_cp")
                    act.wait_ge(s["V0_mm"], b + 1)
                    wait_free(act, s["O0_mm"], b - 1)
                    cp(V0[p].rearrange("j (h w) -> j h w", h=H0)[:, :, 0:DH0],
                       PS[0:J, 2, :].rearrange("j (h w) -> j h w", h=H0), "V0_cp")
                    act.wait_ge(s["xT1_mm"], b + 1)
                    A.activation(xT1[p], PS[:, 5, 0:D], ACT.Identity, bias=beta[:, 0:1],
                                 scale=gamma[:, 0:1]).then_inc(s["xT1_cp"], 1)
                if (b := t.at(5)) is not None:
                    act.wait_ge(s["xT2_mm"], b + 1)
                    wait_free(act, s["lg_mm"], b - 1)
                    cp(xT2[t.par(5)], PS[:, 6, 0:D], "xT2_cp")

            def route(c):
                act.wait_ge(s["ro_e"], c + 1)
                A.activation(rt["e"], rt["s"], ACT.Exp).then_inc(s["ro_exp"], 1)

            for span in route_spans():
                if span is None:
                    route(0)
                else:
                    run_steps(act, NB, *span, step_a)
            route(1)

            def step_b(t):
                if (b := t.at(4)) is not None:
                    p = t.par(4)
                    act.wait_ge(s["hT_mm"], b + t.base + 1)
                    wait_edge(act, t, s["y_mm"], b + t.base - 1)
                    A.activation(hT[p], PS[:, 4 + p, 0:EH], ACT.Relu).then_inc(s["hT_cp"], 1)
                if (b := t.at(0)) is not None:
                    act.wait_ge(s["xsT_mm"], b + t.base + 1)
                    wait_edge(act, t, s["h_mm"], b + t.base - 1)
                    cp(xsT[t.par(0)], PS[:, t.par(0), 0:D], "xsT_cp")

            for c in range(NCH):
                for span in spans(NT, LOOP0, LAST_LAG_B):
                    def step(t):
                        t.base = c * NT
                        step_b(t)
                    run_steps(act, NT, *span, step, 2 * GT)
            act.wait_ge(s["w1_loaded"], 16 * len(loads1))
            act.wait_ge(s["ms"], 14)

            def step_c(t):
                def take_p(b, q):
                    act.wait_ge(s["PT1_mm"], NG * b + q + 1)
                    cp(PT1[:, q * 512:q * 512 + 512], PS[0:J, PT_BANK[q], :], "PT1_cp")

                def take_exp(b, p, i):
                    half = slice(i * HH * J, (i + 1) * HH * J)
                    act.wait_ge(s["S1_sub"], 2 * b + i + 1)
                    A.activation(P1[p][:, half], S1[:, half], ACT.Exp, scale=DH1 ** -0.5).then_inc(s["exp1"], 1)

                if (b := t.at(5)) is not None:
                    wait_free(act, s["O1_mm"], b)
                    take_p(b, 0)
                if (b := t.at(6)) is not None:
                    act.wait_ge(s["OT1_mm"], b + 1)
                    wait_free(act, s["xqT_mm"], t.seen(9, 1))
                    wait_free(act, s["Y1_mm"], b - 1)
                    cp(OT1[t.par(6)], PS[:, 6, 0:D], "OT1_cp")
                if (b := t.at(9)) is not None:
                    act.wait_ge(s["xqT_mm"], b + 1)
                    wait_free(act, s["y4_mm"], b - 1)
                    cp(xqT4[t.par(9)], PS[:, 6, D:D + D // 2].bitcast(BF16), "xqT_cp")
                if (b := t.at(5)) is not None:
                    take_p(b, 1)
                    take_p(b, 2)
                if (b := t.at(4)) is not None:
                    take_exp(b, t.par(4), 0)
                if (b := t.at(5)) is not None:
                    take_p(b, 3)
                if (b := t.at(3)) is not None:
                    act.wait_ge(s["QT_mm"], b + 1)
                    wait_free(act, s["S1_mm"], 2 * (b - 1))
                    for q in range(NG):
                        strip = slice(32 * q, 32 * q + 32)
                        A.activation(QT1[t.par(3)][strip, q * D:(q + 1) * D], PS[strip, 6, 0:D], ACT.Identity,
                                     bias=bq1[strip, 0:1]).then_inc(s["QT_cp"], 1)
                if (b := t.at(4)) is not None:
                    take_exp(b, t.par(4), 1)
                if (b := t.at(2)) is not None:
                    act.wait_ge(s["xT3_mm"], b + 1)
                    wait_free(act, s["QT_mm"], b - 1)
                    cp(xT3[t.par(2)], PS[:, 6, 0:D], "xT3_cp")

            for span in c_spans():
                run_steps(act, NB, *span, step_c)

        @block.vector
        def _(dve):
            V = nc.vector
            chain = {"kq_step": 0, "ro": 0}

            def link(ins, name):
                chain[name] += 1
                ins.then_inc(s[name], 1)
                dve.wait_ge(s[name], chain[name])

            def res(b):
                return XR[:, bass.ds(b, 1), :].rearrange("q o d -> q (o d)")

            dve.wait_ge(s["w_loaded"], 16 * len(loads))
            V.tensor_tensor(lbias[:, 0, :], lbias[:, 0, :], lbias[:, 1, :], ALU.add).then_inc(s["lb_made"], 1)
            dve.wait_ge(s["lb_made"], 1)
            dve.wait_ge(s["tanh_made"], 1)

            def stats(src, st, mv, sname, aname, b, last_use):
                wait_free(dve, s[aname], b)
                apart(dve)
                V.bn_stats(st, src).then_inc(s[sname], 1)
                dve.wait_ge(s[sname], b + 1)
                wait_free(dve, s[last_use], b - 1)
                apart(dve)
                V.bn_aggr(mv, st).then_inc(s[aname], 1)

            def normed(o, src, mv, rs, done):
                V.tensor_scalar(o, src, mv[:, 0:1], rs[:, 1:2], ALU.subtract, ALU.mult).then_inc(s[done], 1)

            def step_a(t):
                if (b := t.at(4)) is not None:
                    dve.wait_ge(s["Y0_mm"], b + 1)
                    V.scalar_tensor_tensor(res(b), PS[:, 4, 0:D], tg[:, 0:1], res(b), ALU.mult,
                                           ALU.add).then_inc(s["x1_made"], 1)
                    dve.wait_ge(s["x1_made"], b + 1)
                    stats(res(b), st2, mv2[t.par(4)], "stats2", "agg2", b, "xn2_made")
                if (b := t.at(3)) is not None:
                    dve.wait_ge(s["PT0_mm"], 2 * b + 2)
                    V.tensor_copy(PT0[t.par(3)][:, HB0 * P:], PS[0:J, 3, :]).then_inc(s["PT0_cpb"], 1)
                if (b := t.at(0)) is not None:
                    dve.wait_ge(s["x_loaded"], b * 16 + 16)
                    stats(res(b), st1, mv1[t.par(0)], "stats1", "agg1", b, "xn1_made")
                if (b := t.at(5)) is not None:
                    p = t.par(5)
                    dve.wait_ge(s["rs2_made"], b + 1)
                    wait_free(dve, s["xT2_mm"], b - 1)
                    wait_free(dve, s["XN_kept"], b - 1)
                    normed(xn2[p], res(b), mv2[p], rs2[p], "xn2_made")
                if (b := t.at(2)) is not None:
                    p = t.par(2)
                    sv = PS[:, 0:2, 0:HB0 * J].rearrange("q k (h j) -> q k h j", j=J)
                    dve.wait_ge(s["S0_mm"], b + 1)
                    wait_free(dve, s["S0_sub"], b)
                    V.tensor_reduce(mx0.rearrange("q (k h) -> q k h", k=2), sv, X, ALU.max).then_inc(s["mx0_made"], 1)
                    dve.wait_ge(s["mx0_made"], b + 1)
                    wait_free(dve, s["exp0"], b - 1)
                    V.tensor_tensor(S0[p].rearrange("q (k h j) -> q k h j", k=2, j=J), sv,
                                    mx0.rearrange("q (k h o) -> q k h o", k=2, o=1).to_broadcast([P, 2, HB0, J]),
                                    ALU.subtract).then_inc(s["S0_sub"], 1)
                if (b := t.at(3)) is not None:
                    p = t.par(3)
                    ov = PS[:, 4:6, 0:HB0 * VW0].rearrange("q k (h w) -> q k h w", w=VW0)
                    dve.wait_ge(s["O0_mm"], b + 1)
                    wait_free(dve, s["O0_cp"], b)
                    V.reciprocal(rd0.rearrange("q (k h o) -> q k h o", k=2, o=1), ov[:, :, :, DH0:VW0]).then_inc(s["rd0_made"], 1)
                    dve.wait_ge(s["rd0_made"], b + 1)
                    wait_free(dve, s["OT0_mm"], b - 1)
                    V.tensor_tensor(O0[p].rearrange("q (k h w) -> q k h w", k=2, w=DH0), ov[:, :, :, 0:DH0],
                                    rd0.rearrange("q (k h o) -> q k h o", k=2, o=1).to_broadcast([P, 2, HB0, DH0]),
                                    ALU.mult).then_inc(s["O0_cp"], 1)
                if (b := t.at(1)) is not None:
                    p = t.par(1)
                    dve.wait_ge(s["rs1_made"], b + 1)
                    wait_free(dve, s["xT1_mm"], b - 1)
                    normed(xn1[p], res(b), mv1[p], rs1[p], "xn1_made")
                if (b := t.at(6)) is not None:
                    dve.wait_ge(s["lg_mm"], b + 1)
                    V.tensor_tensor(LG[:, bass.ds(b, 1), :].rearrange("q o e -> q (o e)"), PS[:, 7, 0:NE],
                                    lbias[:, 0, :], ALU.add).then_inc(s["lg_made"], 1)

            def route(c):
                lo = c * CB
                be = lambda v: v.rearrange("q (b e) -> q b e", e=NE)
                eb = lambda v: v.rearrange("q (e b) -> q e b", e=NE)
                per_b = lambda v: v.rearrange("q (b o) -> q b o", o=1).to_broadcast([P, CB, NE])
                lg = LG[:, lo:lo + CB, :]
                ranks = iotaD[:, :].rearrange("q (o e) -> q o e", o=1).to_broadcast([P, CB, NE])
                dve.wait_ge(s["lg_made"], lo + CB)

                def choose(logits, v, oh):
                    link(V.tensor_reduce(v, logits, X, ALU.max), "ro")
                    link(V.tensor_tensor(be(rt["eq"]), logits, per_b(v), ALU.is_equal), "ro")
                    link(V.tensor_tensor(be(rt["eq"]), be(rt["eq"]), ranks, ALU.mult), "ro")
                    link(V.tensor_reduce(rt["m"], be(rt["eq"]), X, ALU.max), "ro")
                    link(V.tensor_tensor(be(oh), ranks, per_b(rt["m"]), ALU.is_equal), "ro")

                choose(lg, rt["v0"], rt["oh0"])
                link(V.scalar_tensor_tensor(be(rt["lg2"]), be(rt["oh0"]), -3.0e38, lg, ALU.mult, ALU.add), "ro")
                choose(be(rt["lg2"]), rt["v1"], rt["oh1"])
                V.tensor_tensor(rt["s"], rt["v1"], rt["v0"], ALU.subtract).then_inc(s["ro_e"], 1)
                V.tensor_tensor(eb(rtM), rt["oh0"].rearrange("q (b e) -> q e b", e=NE),
                                rt["oh1"].rearrange("q (b e) -> q e b", e=NE), ALU.add).then_inc(s["ro_M"], 1)
                dve.wait_ge(s["ro_cnt"], c + 1)
                link(V.tensor_tensor_scan(rt["cum"], nfirst[:, :, :].rearrange("q e b -> q (e b)"), PS[:, 1, :],
                                          0.0, ALU.mult, ALU.add), "ro")
                link(V.tensor_scalar(rti, eb(rt["cum"])[:, :, CB - 1], float(P - 1), None, ALU.add), "ro")
                link(V.tensor_scalar(rti, rti, -P, None, ALU.bitwise_and), "ro")
                link(V.tensor_copy(rt["pad"], rti), "ro")
                link(V.tensor_tensor_scan(rt["inc"], one16, rt["pad"], 0.0, ALU.mult, ALU.add), "ro")
                link(V.tensor_tensor(rt["base"], rt["inc"], rt["pad"], ALU.subtract), "ro")
                link(V.tensor_scalar(rt["le"], rt["inc"], tau[:, 0:1], None, ALU.is_le), "ro")
                link(V.tensor_reduce(rt["et"], rt["le"], X, ALU.add), "ro")
                V.tensor_scalar(rt["et"], rt["et"], float(NE - 1), None, ALU.min).then_inc(s["ro_et"], 1)
                link(V.tensor_tensor(rt["pos"], rt["cum"], PS[:, 1, :], ALU.subtract), "ro")
                link(V.tensor_tensor(rt["pos"], rt["pos"], PS[:, 0, :], ALU.add), "ro")
                link(V.tensor_tensor(eb(rt["pos"]), eb(rt["pos"]),
                                     rt["base"].rearrange("q (e o) -> q e o", o=1).to_broadcast([P, NE, CB]), ALU.add), "ro")
                for k in range(2):
                    link(V.tensor_tensor(be(rt["eq"]), be(rt[f"oh{k}"]), rt["pos"].rearrange("q (e b) -> q b e", e=NE),
                                         ALU.mult), "ro")
                    link(V.tensor_reduce(rt["m"], be(rt["eq"]), X, ALU.add), "ro")
                    link(V.tensor_copy(POS[k][:, lo:lo + CB], rt["m"]), "ro")
                dve.wait_ge(s["ro_exp"], c + 1)
                link(V.tensor_scalar(rt["s"], rt["e"], 1.0, None, ALU.add), "ro")
                link(V.reciprocal(rt["s"], rt["s"]), "ro")
                link(V.tensor_scalar(WT[0][:, lo:lo + CB], rt["s"], tg[:, 2:3], None, ALU.mult), "ro")
                link(V.tensor_tensor(WT[1][:, lo:lo + CB], WT[0][:, lo:lo + CB], rt["e"], ALU.mult), "ro")
                dve.wait_ge(s["ro_et"], 2 * c + 2)
                e4 = PS[0:1, 2, 0:P].rearrange("o (w k) -> o w k", k=4)
                link(V.tensor_copy(rt["pk"][0:1, :].rearrange("o (w k) -> o w k", k=4), e4), "ro")
                pk = rt["pk"][0:1, :].rearrange("o (w h k) -> o (w h) k", h=2, k=2)
                pairs = rt["pk2"][0:1, :]
                link(V.scalar_tensor_tensor(pairs, pk[:, :, 1], 16.0, pk[:, :, 0], ALU.mult, ALU.add), "ro")
                pq = pairs.rearrange("o (w h) -> o w h", h=2)
                V.scalar_tensor_tensor(ETI[:, c, :], pq[:, :, 1], 256.0, pq[:, :, 0], ALU.mult, ALU.add).then_inc(s["ro_done"], 1)

            for span in route_spans():
                if span is None:
                    route(0)
                else:
                    run_steps(dve, NB, *span, step_a)
            route(1)

            dve.wait_ge(s["w1_loaded"], 16 * len(loads1))
            link(V.reciprocal(scr[:, :], sc[:, :]), "kq_step")
            link(V.tensor_tensor(scm[:, :], sc[:, 0:1], sc[:, 1:2], ALU.mult), "kq_step")
            link(V.tensor_scalar(ksz, kf[:, :], scr[:, 1:2], None, ALU.mult), "kq_step")
            link(V.tensor_scalar(ksc.bitcast(I32), ksz.bitcast(I32), EXP_BITS, None, ALU.bitwise_and), "kq_step")
            link(V.tensor_scalar(ksc, ksc, FP8_LEAST, FP8_ROUND, ALU.max, ALU.mult), "kq_step")
            link(V.tensor_tensor(ksq, ksz, ksc, ALU.add), "kq_step")
            link(V.tensor_tensor(ksq, ksq, ksc, ALU.subtract), "kq_step")
            link(V.tensor_scalar(ksz, ksz, FP8_TOP, 0.0, ALU.mult, ALU.mult), "kq_step")
            link(V.tensor_tensor(kq[:, :], ksq, ksz, ALU.add), "kq_step")
            link(V.tensor_scalar(bo1[:, :], bo1[:, :], tg[:, 1:2], None, ALU.mult), "kq_step")

            dve.wait_ge(s["moe_loaded"], 4 * 16 * NE)
            dve.wait_ge(s["ro_done"], NCH)

            experts = Experts(dve, ETI)

            def step_b(t, c):
                base = c * NT
                if (b := t.at(6)) is not None:
                    p = t.par(6)
                    e = experts.of(t, c, 6)
                    dve.wait_ge(s["y_mm"], b + base + 1)
                    k = t.ring(6, 2 * GT)
                    if k % GT == 0:
                        wait_free(dve, s[f"ys_stored{k // GT}"], (b + base - k) * 2)
                        apart(dve)
                    V.tensor_tensor(yb[k // GT][:, k % GT, :], PS[:, 6 + p, 0:D],
                                    b2s[:, bass.ds(e, 1), :].rearrange("q o h -> q (o h)"), ALU.add).then_inc(s["y_made"], 1)
                if (b := t.at(2)) is not None:
                    p = t.par(2)
                    e = experts.of(t, c, 2)
                    dve.wait_ge(s["h_mm"], b + base + 1)
                    wait_edge(dve, t, s["hT_mm"], b + base - 1)
                    V.tensor_tensor(hb[p], PS[:, 2 + p, 0:EH],
                                    b1s[:, bass.ds(e, 1), :].rearrange("q o h -> q (o h)"), ALU.add).then_inc(s["h_made"], 1)

            for c in range(NCH):
                for span in spans(NT, LOOP0, LAST_LAG_B):
                    run_steps(dve, NT, *span, lambda t: step_b(t, c), 2 * GT)

            def step_c(t):
                def less_max(b, i):
                    gh = NG // 2
                    sv = PS[:, gh * i:gh * (i + 1), 0:GH * J].rearrange("q g (h j) -> q g h j", j=J)
                    mx = mx1[:, HH * i:HH * (i + 1)]
                    dve.wait_ge(s["S1_mm"], 2 * b + i + 1)
                    wait_free(dve, s["S1_sub"], 2 * b + i - 1)
                    V.tensor_reduce(mx.rearrange("q (g h) -> q g h", g=gh), sv, X, ALU.max).then_inc(s["mx1_made"], 1)
                    dve.wait_ge(s["mx1_made"], 2 * b + i + 1)
                    wait_free(dve, s["exp1"], 2 * b + i - 1)
                    V.tensor_tensor(S1[:, HH * J * i:HH * J * (i + 1)].rearrange("q (g h j) -> q g h j", g=gh, j=J), sv,
                                    mx.rearrange("q (g h o) -> q g h o", g=gh, o=1).to_broadcast([P, gh, GH, J]),
                                    ALU.subtract).then_inc(s["S1_sub"], 1)

                if (b := t.at(6)) is not None:
                    p = t.par(6)
                    ov = PS[:, 7, 0:H1 * VW1].rearrange("q (h w) -> q h w", w=VW1)
                    dve.wait_ge(s["O1_mm"], b + 1)
                    wait_free(dve, s["O1_cp"], b)
                    V.reciprocal(rd1.rearrange("q (h o) -> q h o", o=1), ov[:, :, DH1:VW1]).then_inc(s["rd1_made"], 1)
                    dve.wait_ge(s["rd1_made"], b + 1)
                    wait_free(dve, s["OT1_mm"], b - 1)
                    V.tensor_tensor(O1[p].rearrange("q (h w) -> q h w", w=DH1), ov[:, :, 0:DH1],
                                    rd1.rearrange("q (h o) -> q h o", o=1).to_broadcast([P, H1, DH1]),
                                    ALU.mult).then_inc(s["O1_cp"], 1)
                if (b := t.at(7)) is not None:
                    dve.wait_ge(s["Y1_mm"], b + 1)
                    wait_free(dve, s["y4_mm"], t.seen(9))
                    dve.wait_ge(s["x2b_made"], b + 1)
                    V.scalar_tensor_tensor(res(b), PS[:, 5, 0:D], tg[:, 1:2], res(b), ALU.mult,
                                           ALU.add).then_inc(s["x3_made"], 1)
                if (b := t.at(10)) is not None:
                    p = t.par(10)
                    dve.wait_ge(s["y4_mm"], b + 1)
                    wait_free(dve, s["y4b_made"], b - 1)
                    V.tensor_scalar(y4[p], PS[:, 5, D:2 * D], scm[:, 0:1], None, ALU.mult).then_inc(s["y4_made"], 1)
                if (b := t.at(7)) is not None:
                    dve.wait_ge(s["x3_made"], b + 1)
                    stats(res(b), st4, mv4[t.par(7)], "stats4", "agg4", b, "xb4_made")
                if (b := t.at(4)) is not None:
                    less_max(b, 0)
                if (b := t.at(8)) is not None:
                    p = t.par(8)
                    dve.wait_ge(s["rs4_made"], b + 1)
                    wait_free(dve, s["m4_made"], 2 * b)
                    normed(xb4, res(b), mv4[p], rs4[p], "xb4_made")
                if (b := t.at(2)) is not None:
                    p = t.par(2)
                    dve.wait_ge(s["rs3_made"], b + 1)
                    wait_free(dve, s["xT3_mm"], b - 1)
                    normed(xn3[p], res(b), mv3[p], rs3[p], "xn3_made")
                if (b := t.at(8)) is not None:
                    p = t.par(8)
                    dve.wait_ge(s["xb4_made"], b + 1)
                    wait_free(dve, s["xq4_made"], b - 1)
                    V.tensor_scalar(z4[p], xb4, scr[:, 0:1], None, ALU.mult).then_inc(s["m4_made"], 1)
                    dve.wait_ge(s["m4_made"], 2 * b + 1)
                    V.tensor_scalar(c4[p].bitcast(I32), z4[p].bitcast(I32), EXP_BITS, None, ALU.bitwise_and).then_inc(s["m4_made"], 1)
                    dve.wait_ge(s["m4_made"], 2 * b + 2)
                    V.tensor_scalar(c4[p], c4[p], FP8_LEAST, FP8_ROUND, ALU.max, ALU.mult).then_inc(s["c4_made"], 1)
                if (b := t.at(4)) is not None:
                    less_max(b, 1)
                if (b := t.at(3)) is not None:
                    p = t.par(3)
                    dve.wait_ge(s["KT_mm"], b + 1)
                    wait_free(dve, s["V1_mm"], t.seen(4, 1))
                    wait_free(dve, s["S1_mm"], 2 * (b - 1))
                    V.scalar_tensor_tensor(KB1[p].rearrange("q (h j) -> q h j", h=GH),
                                           PS[:, 5, D:D + J].rearrange("q (o j) -> q o j", o=1).to_broadcast([P, GH, J]),
                                           bk1[:, 0:1],
                                           mask4[:, :].rearrange("q (h o) -> q h o", o=1).to_broadcast([P, GH, J]),
                                           ALU.add, ALU.mult).then_inc(s["KB_made"], 1)
                if (b := t.at(4)) is not None:
                    p = t.par(4)
                    dve.wait_ge(s["V1_mm"], b + 1)
                    wait_free(dve, s["O1_mm"], b - 1)
                    V.tensor_tensor(V1[p].rearrange("j (h w) -> j h w", h=H1)[:, :, 0:DH1],
                                    PS[0:J, 5, 0:D].rearrange("j (h w) -> j h w", h=H1),
                                    bv1[0:J, :].rearrange("j (h w) -> j h w", h=H1), ALU.add).then_inc(s["V1_cp"], 1)
                if (b := t.at(1)) is not None:
                    p = t.par(1)
                    dve.wait_ge(s[f"gy_made{p}"], (b - p) * 16 + 32)
                    wait_free(dve, s["x2_made"], b)
                    V.scalar_tensor_tensor(uc, gy[0][p], WT[0][:, bass.ds(b, 1)], res(b), ALU.mult, ALU.add).then_inc(s["u_made"], 1)
                    dve.wait_ge(s["u_made"], b + 1)
                    V.scalar_tensor_tensor(res(b), gy[1][p], WT[1][:, bass.ds(b, 1)], uc, ALU.mult, ALU.add).then_inc(s["x2_made"], 1)
                if (b := t.at(11)) is not None:
                    p = t.par(11)
                    dve.wait_ge(s["y4b_made"], b + 1)
                    wait_free(dve, s[f"out_stored{p}"], (b - p) * 8)
                    V.scalar_tensor_tensor(ob[p], y4b[p], tg[:, 3:4], res(b), ALU.mult, ALU.add).then_inc(s["ob_made"], 1)
                if (b := t.at(1)) is not None:
                    dve.wait_ge(s["x2_made"], b + 1)
                    stats(res(b), st3, mv3[t.par(1)], "stats3", "agg3", b, "xn3_made")

            for span in c_spans():
                run_steps(dve, NB, *span, step_c)

        @block.tensor
        def _(pe):
            T = nc.tensor

            def mm(o, l, r, start=True, stop=True):
                return T.matmul(o, l, r, start=start, stop=stop)

            pe.wait_ge(s["w_loaded"], 16 * len(loads))
            for h in range(H0):
                last = mm(PS[:, h // 4, (h % 4) * D:(h % 4 + 1) * D], wkT[:, h * D:(h + 1) * D], wqT[:, h * D:(h + 1) * D])
                if h % 4 == 3:
                    last.then_inc(s["t0_mm"], 1)
            pe.wait_ge(s["t0_cp"], 2)
            pe.wait_ge(s["consts"], 6)

            def step_a(t):
                if (b := t.at(3)) is not None:
                    p = t.par(3)
                    pe.wait_ge(s["exp0"], b + 1)
                    pe.wait_ge(s["V0_cp"], b + 1)
                    wait_free(pe, s["V0_cp"], t.seen(1))
                    wait_free(pe, s["OT0_cp"], t.seen(3))
                    for h in range(H0):
                        last = T.transpose(PS[0:J, 2 + h // 4, (h % 4) * P:(h % 4 + 1) * P],
                                           P0[p][:, h * J:(h + 1) * J], ident[:, :])
                        if h % 4 == 3:
                            last.then_inc(s["PT0_mm"], 1)
                if (b := t.at(2)) is not None:
                    p = t.par(2)
                    pe.wait_ge(s["xT1_cp"], b + 1)
                    pe.wait_ge(s["KA_cp"], b + 1)
                    wait_free(pe, s["S0_sub"], b)
                    for k in range(2):
                        last = mm(PS[:, k, 0:HB0 * J], xT1[p], KA[p][:, k * HB0 * J:(k + 1) * HB0 * J])
                    last.then_inc(s["S0_mm"], 1)
                if (b := t.at(3)) is not None:
                    p = t.par(3)
                    pe.wait_ge(s["PT0_cpa"], b + 1)
                    pe.wait_ge(s["PT0_cpb"], b + 1)
                    wait_free(pe, s["x1_made"], t.seen(3))
                    wait_free(pe, s["xT1_cp"], t.seen(1))
                    for h in range(H0):
                        last = mm(PS[:, 4 + h // 4, (h % 4) * VW0:(h % 4 + 1) * VW0],
                                  PT0[p][:, h * P:(h + 1) * P], V0[p][:, h * VW0:(h + 1) * VW0])
                    last.then_inc(s["O0_mm"], 1)
                if (b := t.at(1)) is not None:
                    p = t.par(1)
                    pe.wait_ge(s["ctx_loaded"], b * 16 + 16)
                    wait_free(pe, s["KA_cp"], b)
                    wait_free(pe, s["xT2_cp"], t.seen(5))
                    wait_free(pe, s["lg_made"], t.seen(6))
                    for h in range(H0):
                        last = mm(PS[:, 6 + h // 4, (h % 4) * J:(h % 4 + 1) * J], T0[:, h, :], ctxa[p])
                    last.then_inc(s["KA_mm"], 1)
                if (b := t.at(3)) is not None:
                    p = t.par(3)
                    pe.wait_ge(s["O0_cp"], b + 1)
                    pe.wait_ge(s["PT0_cpb"], b + 1)
                    for q in range(HD0 // P):
                        last = T.transpose(PS[:, 3, q * P:(q + 1) * P], O0[p][:, q * P:(q + 1) * P], ident[:, :])
                    last.then_inc(s["OT0_mm"], 1)
                if (b := t.at(1)) is not None:
                    p = t.par(1)
                    wait_free(pe, s["V0_cp"], b)
                    wait_free(pe, s["PT0_cpa"], t.seen(3, 1))
                    mm(PS[0:J, 2, :], ctxa[p], wv0[:, :]).then_inc(s["V0_mm"], 1)
                    pe.wait_ge(s["xn1_made"], b + 1)
                    wait_free(pe, s["xT1_cp"], b)
                    wait_free(pe, s["O0_cp"], t.seen(3, 1))
                    T.transpose(PS[:, 5, 0:D], xn1[p], ident[:, :]).then_inc(s["xT1_mm"], 1)
                if (b := t.at(3)) is not None:
                    p = t.par(3)
                    pe.wait_ge(s["OT0_cp"], b + 1)
                    for q in range(HD0 // P):
                        last = mm(PS[:, 4, 0:D], OT0[p][:, q * P:(q + 1) * P], wo0[:, q, :],
                                  start=(q == 0), stop=(q == HD0 // P - 1))
                    last.then_inc(s["Y0_mm"], 1)
                if (b := t.at(5)) is not None:
                    p = t.par(5)
                    pe.wait_ge(s["xn2_made"], b + 1)
                    wait_free(pe, s["xT2_cp"], b)
                    wait_free(pe, s["KA_cp"], t.seen(1, 1))
                    T.transpose(PS[:, 6, 0:D], xn2[p], ident[:, :]).then_inc(s["xT2_mm"], 1)
                if (b := t.at(6)) is not None:
                    p = t.par(6)
                    pe.wait_ge(s["xT2_cp"], b + 1)
                    wait_free(pe, s["lg_made"], b)
                    wait_free(pe, s["KA_cp"], t.seen(1, 1))
                    mm(PS[:, 7, 0:NE], xT2[p], wgs[:, :]).then_inc(s["lg_mm"], 1)

            def route(c):
                pe.wait_ge(s["ro_M"], c + 1)
                pe.wait_ge(s["S0_sub"], min(ROUTE0 - 2, NB) if c == 0 else NB)
                pe.wait_ge(s["xT2_cp"], CB + 1 if c == 0 else NB)
                pe.wait_ge(s["lg_made"], CB * (c + 1))
                pe.wait_ge(s["V0_cp"], ROUTE0 - 1 if c == 0 else NB)
                pe.wait_ge(s["PT0_cpa"], ROUTE0 - 3 if c == 0 else NB)
                mm(PS[:, 0, :], ltri[:, :], rtM)
                mm(PS[:, 1, :], onesb[:, :], rtM).then_inc(s["ro_cnt"], 1)
                pe.wait_ge(s["ro_et"], 2 * c + 1)
                mm(PS[0:1, 2, 0:P], rt["et"], ident[:, :]).then_inc(s["ro_et"], 1)
                pe.wait_ge(s["ro_done"], c + 1)

            for span in route_spans():
                if span is None:
                    route(0)
                else:
                    run_steps(pe, NB, *span, step_a)
            route(1)

            pe.wait_ge(s["moe_loaded"], 4 * 16 * NE)
            for last in ("OT0_cp", "PT0_cpb", "KA_cp", "xT1_cp", "O0_cp", "x1_made", "xT2_cp", "lg_made"):
                pe.wait_ge(s[last], NB)

            experts = Experts(pe, ETI)

            def step_b(t, c):
                base = c * NT
                if (b := t.at(6)) is not None:
                    p = t.par(6)
                    e = experts.of(t, c, 6)
                    pe.wait_ge(s["hT_cp"], b + base + 1)
                    wait_free(pe, s["y_made"], b + base - 1)
                    for q in range(2):
                        last = mm(PS[:, 6 + p, 0:D], hT[p][:, q * P:(q + 1) * P],
                                  W2s[:, bass.ds(e, 1), q, :].rearrange("q o d -> q (o d)"), start=(q == 0), stop=(q == 1))
                    last.then_inc(s["y_mm"], 1)
                if (b := t.at(4)) is not None:
                    p = t.par(4)
                    pe.wait_ge(s["h_made"], b + base + 1)
                    wait_edge(pe, t, s["hT_cp"], b + base - 1)
                    for q in range(2):
                        last = T.transpose(PS[:, 4 + p, q * P:(q + 1) * P], hb[p][:, q * P:(q + 1) * P], ident[:, :])
                    last.then_inc(s["hT_mm"], 1)
                if (b := t.at(2)) is not None:
                    p = t.par(2)
                    e = experts.of(t, c, 2)
                    pe.wait_ge(s["xsT_cp"], b + base + 1)
                    wait_edge(pe, t, s["h_made"], b + base - 1)
                    mm(PS[:, 2 + p, 0:EH], xsT[p], W1s[:, bass.ds(e, 1), :].rearrange("q o h -> q (o h)")).then_inc(s["h_mm"], 1)
                if (b := t.at(0)) is not None:
                    p = t.par(0)
                    k = t.ring(0, 2 * GT)
                    if k % GT == 0:
                        pe.wait_ge(s[f"xs_loaded{k // GT}"], (b + base - k) * 2 + 16)
                    wait_edge(pe, t, s["xsT_cp"], b + base - 1)
                    T.transpose(PS[:, p, 0:D], xsb[k // GT][:, k % GT, :], ident[:, :]).then_inc(s["xsT_mm"], 1)

            for c in range(NCH):
                for span in spans(NT, LOOP0, LAST_LAG_B):
                    run_steps(pe, NT, *span, lambda t: step_b(t, c), 2 * GT)
            pe.wait_ge(s["y_made"], NCH * NT)
            pe.wait_ge(s["ms"], 14)
            pe.wait_ge(s["kq_step"], 10)
            pe.wait_ge(s["w1_loaded"], 16 * len(loads1))

            def step_c(t):
                def scores(q):
                    if (b := t.at(4)) is not None:
                        p = t.par(4)
                        if q == 0:
                            pe.wait_ge(s["QT_cp"], NG * b + NG)
                            pe.wait_ge(s["KB_made"], b + 1)
                        if q % 2 == 0:
                            wait_edge(pe, t, s["S1_sub"], 2 * b + q // 2 - 1)
                        ins = mm(PS[:, q, 0:GH * J], QT1[p][:, q * D:(q + 1) * D], KB1[p])
                        if q % 2 == 1:
                            ins.then_inc(s["S1_mm"], 1)

                def transpose_p(q):
                    if (b := t.at(5)) is not None:
                        if q == 0:
                            pe.wait_ge(s["exp1"], 2 * b + 1)
                        if q == 2:
                            wait_edge(pe, t, s["exp1"], 2 * b + 2)
                        for h in range(GH * q, GH * q + GH):
                            last = T.transpose(PS[0:J, PT_BANK[q], (h % GH) * P:(h % GH + 1) * P],
                                               P1[t.par(5)][:, h * J:(h + 1) * J], ident[:, :])
                        last.then_inc(s["PT1_mm"], 1)

                def attend(q):
                    if (b := t.at(5)) is not None:
                        if q == 2:
                            wait_edge(pe, t, s["PT1_cp"], NG * b + q + 1)
                        else:
                            pe.wait_ge(s["PT1_cp"], NG * b + q + 1)
                        for h in range(GH * q, GH * q + GH):
                            last = mm(PS[:, 7, h * VW1:(h + 1) * VW1], PT1[:, h * P:(h + 1) * P],
                                      V1[t.par(5)][:, h * VW1:(h + 1) * VW1])
                        if q == NG - 1:
                            last.then_inc(s["O1_mm"], 1)

                def bank5_free(now):
                    wait_edge(pe, t, s["x3_made"], t.seen(6))
                    wait_edge(pe, t, s["y4_made"], t.seen(9))
                    wait_edge(pe, t, s["KB_made"], t.seen(3, now))
                    if now:
                        wait_free(pe, s["V1_cp"], t.seen(4, 1))
                    else:
                        wait_edge(pe, t, s["V1_cp"], t.seen(4))

                def bank6_free(now):
                    wait_edge(pe, t, s["OT1_cp"], t.seen(6, now))
                    wait_edge(pe, t, s["xqT_cp"], t.seen(9, now))

                scores(0)
                wait_edge(pe, t, s["PT1_cp"], NG * t.seen(5))
                transpose_p(0)
                scores(1)
                if t.at(6) is not None or t.at(9) is not None:
                    bank6_free(0)
                    wait_edge(pe, t, s["QT_cp"], NG * t.seen(3))
                    wait_free(pe, s["xT3_cp"], t.seen(2))
                if (b := t.at(6)) is not None:
                    pe.wait_ge(s["O1_cp"], b + 1)
                    T.transpose(PS[:, 6, 0:D], O1[t.par(6)], ident[:, :]).then_inc(s["OT1_mm"], 1)
                if (b := t.at(9)) is not None:
                    pe.wait_ge(s["xq4_made"], b + 1)
                    T.transpose(PS[:, 6, D:D + D // 2].bitcast(BF16), xq4[t.par(9)], identb[:, :]).then_inc(s["xqT_mm"], 1)
                if t.at(5) is not None:
                    bank5_free(0)
                    wait_free(pe, s["y4_made"], t.seen(9))
                transpose_p(1)
                if t.at(5) is not None:
                    wait_edge(pe, t, s["O1_cp"], t.seen(5))
                attend(0)
                scores(2)
                if t.at(5) is not None:
                    bank6_free(1)
                    wait_free(pe, s["xqT_cp"], t.seen(9, 1))
                    wait_edge(pe, t, s["QT_cp"], NG * t.seen(3))
                    wait_edge(pe, t, s["xT3_cp"], t.seen(2))
                transpose_p(2)
                scores(3)
                attend(1)
                if t.at(4) is not None or t.at(3) is not None:
                    wait_edge(pe, t, s["PT1_cp"], NG * t.seen(5, 1) - 2)
                    bank5_free(0)
                if (b := t.at(4)) is not None:
                    wait_edge(pe, t, s["ctxc_loaded"], b * 16 + 16)
                    mm(PS[0:J, 5, 0:D], ctxc[t.par(4)], wv1[:, :]).then_inc(s["V1_mm"], 1)
                if (b := t.at(3)) is not None:
                    pe.wait_ge(s["ctxc_loaded"], b * 16 + 16)
                    mm(PS[:, 5, D:D + J], wk1[:, :], ctxc[t.par(3)]).then_inc(s["KT_mm"], 1)
                transpose_p(3)
                if (b := t.at(3)) is not None:
                    wait_edge(pe, t, s["xT3_cp"], b + 1)
                    wait_free(pe, s["PT1_cp"], NG * t.seen(5, 1) - 1)
                    bank6_free(1)
                    mm(PS[:, 6, 0:D], wq1[:, :], xT3[t.par(3)]).then_inc(s["QT_mm"], 1)
                attend(2)
                if t.at(6) is not None or t.at(9) is not None:
                    wait_edge(pe, t, s["PT1_cp"], NG * t.seen(5, 1) - 2)
                    bank5_free(1)
                if (b := t.at(6)) is not None:
                    wait_edge(pe, t, s["OT1_cp"], b + 1)
                    mm(PS[:, 5, 0:D], OT1[t.par(6)], wo1[:, :]).then_inc(s["Y1_mm"], 1)
                if (b := t.at(9)) is not None:
                    wait_edge(pe, t, s["xqT_cp"], b + 1)
                    mm(PS[:, 5, D:2 * D], xqT4[t.par(9)], kq[:, :]).then_inc(s["y4_mm"], 1)
                attend(3)
                if (b := t.at(2)) is not None:
                    pe.wait_ge(s["xn3_made"], b + 1)
                    wait_edge(pe, t, s["PT1_cp"], NG * t.seen(5, 1) - 1)
                    bank6_free(1)
                    wait_free(pe, s["QT_cp"], NG * t.seen(3, 1))
                    wait_edge(pe, t, s["xT3_cp"], b)
                    T.transpose(PS[:, 6, 0:D], xn3[t.par(2)], ident[:, :]).then_inc(s["xT3_mm"], 1)

            def warm_up(first):
                wait_free(pe, s["PT1_cp"], NG * (first - 5))
                with pe.Fori(0, 12):
                    for _ in range(4):
                        T.transpose(PS[:, 4, 0:P], ident[:, :], ident[:, :])

            for span in c_spans():
                if not span[2]:
                    warm_up(span[0])
                run_steps(pe, NB, *span, step_c)


EXP_BITS = 0x7F800000
FP8_LEAST = 2.0 ** -6
FP8_ROUND = 1.5 * 2.0 ** 20
FP8_TOP = 3.4028234e38 / 464.5


_INS = {"x": "x", "g_xattn": "g_xattn", "g_ffn": "g_ffn", "gamma": "L0_xattn_gamma", "beta": "L0_xattn_beta",
        "Wout": "L0_xattn_Wout", "Wg": "L0_ffn_Wg", "bg": "L0_ffn_bg", "bias": "L0_ffn_bias",
        "W1": "L0_ffn_W1", "b1": "L0_ffn_b1", "W2": "L0_ffn_W2", "b2": "L0_ffn_b2",
        "Wq1": "L1_xattn_Wq", "bq1": "L1_xattn_bq", "Wk1": "L1_xattn_Wk", "bk1": "L1_xattn_bk",
        "Wv1": "L1_xattn_Wv", "bv1": "L1_xattn_bv", "Wo1": "L1_xattn_Wo", "bo1": "L1_xattn_bo",
        "kernel": "L1_ffn_kernel", "input_scale": "L1_ffn_input_scale", "kernel_scale": "L1_ffn_kernel_scale",
        "ffn_bias": "L1_ffn_bias"}


def kernel(**inputs):
    import numpy as np
    import concourse.bacc as bacc
    from concourse.bass_utils import run_bass_kernel_spmd

    data = {name: np.ascontiguousarray(inputs[full]) for name, full in _INS.items()}
    heads, dh = 8, 64
    wq, wkv = np.asarray(inputs["L0_xattn_Wq"]), np.asarray(inputs["L0_xattn_Wkv"])
    d, inner = wq.shape
    data["WqT"] = np.ascontiguousarray(wq.reshape(d, heads, dh).transpose(2, 1, 0)).reshape(dh, heads * d)
    data["WkT"] = np.ascontiguousarray(wkv[:, :inner].reshape(d, heads, dh).transpose(2, 1, 0)).reshape(dh, heads * d)
    data["Wv"] = np.ascontiguousarray(wkv[:, inner:])
    data["ctxT"] = np.ascontiguousarray(np.asarray(inputs["ctx_1024"]).transpose(0, 2, 1))

    nc = bacc.Bacc("TRN2", target_bir_lowering=False, num_devices=1)
    aps, arrays = {}, {}
    for name, v in data.items():
        arrays[f"in_{name}"] = v
        aps[name] = nc.dram_tensor(f"in_{name}", v.shape, mybir.dt.from_np(v.dtype), kind="ExternalInput").ap()
    out = nc.dram_tensor("out", data["x"].shape, F32, kind="ExternalOutput").ap()
    nb, n, dd = data["x"].shape
    nt = (nb * n + 16 * 127) // 128
    nt += -nt % 8
    xs = [nc.dram_tensor(f"moe_rows{c}", (nt * 128, dd), F32, kind="Internal").ap() for c in range(2)]
    ys = [nc.dram_tensor(f"moe_results{c}", (nt * 128, dd), F32, kind="Internal").ap() for c in range(2)]
    flamingo_two_layers(nc, aps, out, xs, ys)
    r = run_bass_kernel_spmd(nc, [arrays], core_ids=[0])
    return r.results[0]["out"]
```

```python
import concourse.bass as bass
from concourse import mybir
from contextlib import ExitStack

F32 = mybir.dt.float32
BF16 = mybir.dt.bfloat16
I32 = mybir.dt.int32
ALU = mybir.AluOpType
ACT = mybir.ActivationFunctionType
X = mybir.AxisListType.X
P = 128


class Step:

    def __init__(self, value, place, count, turn=None, per_turn=2):
        self.value, self.place, self.count, self.turn, self.per_turn = value, place, count, turn, per_turn

    def at(self, lag):
        if isinstance(self.value, int):
            b = self.value - lag
            return b if 0 <= b < self.count else None
        return self.value - lag

    def par(self, lag):
        return (self.place - lag) % 2

    def ring(self, lag, size):
        return (self.place - lag) % size

    def seen(self, lag, now=0):
        n = self.value - lag + now
        return min(max(n, 0), self.count) if isinstance(n, int) else n


def run_steps(engine, count, first, last, peeled, body, per_turn=2):
    if peeled:
        for t in range(first, last):
            body(Step(t, t % per_turn, count))
    else:
        assert first % per_turn == 0 and last % per_turn == 0
        with engine.Fori(first // per_turn, last // per_turn) as turn:
            for p in range(per_turn):
                body(Step(turn * per_turn + p, p, count, turn, per_turn))


def wait_free(engine, sem, value):
    if isinstance(value, int) and value <= 0:
        return
    engine.wait_ge(sem, value)


class Experts:

    def __init__(self, engine, table):
        self.engine, self.table, self.words = engine, table, {}

    def of(self, t, lag):
        if isinstance(t.value, int):
            word, k = divmod(t.at(lag), 4)
            key = word
        else:
            group, k = divmod(t.place - lag, 4)
            word = t.turn * (t.per_turn // 4) + group
            key = ("turn", group)
            if t.place == 0:
                self.words = {}
        if key not in self.words:
            self.words[key] = self.engine.value_load(self.table[0:1, bass.ds(word, 1)], min_val=0, max_val=0xFFFF)
        return (self.words[key] >> (4 * k)) & 15


def wait_edge(engine, t, sem, value):
    if isinstance(t.value, int):
        wait_free(engine, sem, value)


def flamingo_two_layers(nc, a, out, xs_dram, ys_dram):
    NB, N, D = a["x"].shape
    J = a["ctxT"].shape[2]
    H0 = 8
    DH0 = a["WqT"].shape[0]
    HD0 = H0 * DH0
    H1, DH1 = 16, D // 16
    NE, EH = a["b1"].shape
    EPS = 1e-5
    NCH = 2
    CB = NB // NCH
    NT = (2 * CB * N + NE * (P - 1)) // P
    GT = 4
    NT += -NT % (4 * GT)
    NG_B = NT // GT
    HB0 = H0 // 2
    VW0 = DH0 + 1
    VW1 = DH1 + 1
    GH = 4
    NG = H1 // GH
    HH = H1 // 2
    KEYS = P // GH
    NKB = J // KEYS
    JR = J - NKB * KEYS
    RR = 2 * JR * GH
    NP = NG // 2
    assert NKB == 2 and RR <= P
    SETUP_STEPS = 23
    KT_AT = (NKB + 1) * D
    LOOP0 = 8
    LAST_LAG_A, LAST_LAG_B, LAST_LAG_C = 7, 6, 11
    LOOPB = 32
    LOOPC = 16
    TURN = 8
    ROUTE0 = CB + LAST_LAG_A
    ROUTE0 += -ROUTE0 % TURN

    ctx = ExitStack()
    with ctx:
        def sb(name, shape, dt=F32):
            return ctx.enter_context(nc.sbuf_tensor(name, shape, dt))

        def sem(name):
            return ctx.enter_context(nc.semaphore(name))

        XR = sb("residual", [P, NB, D])
        XN = sb("moe_in", [P, NB, D])
        W1s = sb("w1", [P, NE, EH])
        W2s = sb("w2", [P, NE, 2, D])
        b1s = sb("b1_rows", [P, NE, EH])
        b2s = sb("b2_rows", [P, NE, D])
        LG = sb("logits", [P, NB, NE])
        WT = [sb(f"gate_w{k}", [P, NB]) for k in range(2)]
        POS = [sb(f"slot{k}", [P, NB], I32) for k in range(2)]
        ETI = sb("tile_experts", [1, NCH * NT // 4], I32)
        ident = sb("ident", [P, P])
        identb = sb("identb", [P, P], BF16)
        ltri = sb("before", [P, P], BF16)
        onesb = sb("onesb", [P, P], BF16)
        iotaD = sb("rank_of_expert", [P, NE])
        tau = sb("tile_start", [P, 1])
        nfirst = sb("not_first", [P, NE, CB])
        mask4 = sb("head_of_row", [P, GH])
        mhalf = sb("minus_half", [P, 1])
        tg = sb("tanh_gates", [P, 4])
        gamma = sb("gamma", [P, 1])
        beta = sb("beta", [P, 1])
        wgs = sb("wg", [P, NE])
        lbias = sb("logit_bias", [P, 2, NE])
        T0 = sb("wk_wq", [P, H0, D])
        wv0 = sb("wv0", [P, HD0])
        wo0 = sb("wo0", [P, HD0 // P, D])
        wq1 = sb("wq1", [P, D])
        wk1 = sb("wk1", [P, D])
        wv1 = sb("wv1", [P, D])
        wo1 = sb("wo1", [P, D])
        bq1 = sb("bq1", [P, 1])
        bk1 = sb("bk1", [P, 1])
        bv1 = sb("bv1", [P, 1])
        bv1b = sb("bv1_columns", [P, D])
        maskv = sb("head_of_block_row", [P, GH])
        maskr = sb("group_and_head_of_shared_row", [P, 2 * GH])
        maski = sb("row_less_head", [P, GH], I32)
        rlow = sb("row_of_first_group", [P, 1])
        bo1 = sb("bo1", [P, D])
        kf = sb("ffn_kernel", [P, D], BF16)
        kq = sb("ffn_kernel_q", [P, D], BF16)
        sc = sb("ffn_scales", [P, 2])
        scr = sb("ffn_rscales", [P, 2])
        scm = sb("ffn_scale_product", [P, 1])
        fbias = sb("ffn_bias", [P, D], BF16)
        ZR, ZP = NT * P // CB, P // 2
        zt = sb("zeros", [ZP, ZR // ZP * D])

        PS = ctx.enter_context(nc.psum_tensor("PS", [P, 8, 512], F32))

        AW = 14700
        arena = sb("arena", [P, AW])

        class Carver:
            def __init__(self):
                self.at = 0

            def __call__(self, width, parts=P):
                v = arena[0:parts, self.at:self.at + width]
                self.at += width
                assert self.at <= AW, self.at
                return v

        ca = Carver()
        one16 = ca(NE)
        scat = [ca(D) for _ in range(2)]
        si = [ca(1).bitcast(I32) for _ in range(4)]
        after_scatter = ca.at
        ctxa = [ca(2 * J) for _ in range(2)]
        mv1 = [ca(2) for _ in range(2)]
        st1 = ca(6)
        rs1 = [ca(2) for _ in range(2)]
        xn1 = [ca(D) for _ in range(2)]
        xT1 = [ca(D) for _ in range(2)]
        KA = [ca(H0 * 2 * J) for _ in range(2)]
        V0 = [ca(H0 * VW0, J) for _ in range(2)]
        S0 = [ca(H0 * J) for _ in range(2)]
        P0 = [ca(H0 * J) for _ in range(2)]
        mx0 = ca(H0)
        PT0 = [ca(H0 * P, J) for _ in range(2)]
        rd0 = ca(H0)
        O0 = [ca(HD0) for _ in range(2)]
        OT0 = [ca(HD0) for _ in range(2)]
        mv2 = [ca(2) for _ in range(2)]
        st2 = ca(6)
        rs2 = [ca(2) for _ in range(2)]
        xn2 = [ca(D) for _ in range(2)]
        xT2 = [ca(D) for _ in range(2)]
        after_a = ca.at
        rt = {}
        for name, width in (("v0", CB), ("v1", CB), ("m", CB), ("oh0", CB * NE),
                            ("oh1", CB * NE), ("e", CB), ("s", CB), ("cum", NE * CB),
                            ("pos", NE * CB), ("tot", NE), ("pad", NE), ("inc", NE), ("base", NE),
                            ("et", 1), ("le", NE), ("pk", P), ("pk2", P // 2),
                            ("pick_eq", 4 * NE), ("pick_second", 4 * NE), ("pick_m", 4)):
            rt[name] = ca(width)
        rtM = ca(NE * CB // 2).bitcast(BF16)
        rti = ca(NE).bitcast(I32)
        cb = Carver()
        cb.at = after_scatter
        xsb = [cb(GT * D).rearrange("p (k d) -> p k d", d=D) for _ in range(2)]
        xsT = [cb(D) for _ in range(2)]
        hb = [cb(EH) for _ in range(2)]
        hT = [cb(EH) for _ in range(2)]
        yb = [cb(GT * D).rearrange("p (k d) -> p k d", d=D) for _ in range(2)]
        cc = Carver()
        S1 = cc(H1 * J)
        P1 = [cc(H1 * J) for _ in range(2)]
        PT1 = cc((NG * NKB + NP) * P)
        assert cc.at >= cb.at
        gy = [[cc(D) for _ in range(2)] for _ in range(2)]
        gi = [[cc(1).bitcast(I32) for _ in range(2)] for _ in range(2)]
        ctxc = [cc(J) for _ in range(2)]
        ctxr = [cc(NKB * P + RR) for _ in range(2)]
        uc = cc(D)
        mv3 = [cc(2) for _ in range(2)]
        st3 = cc(6)
        rs3 = [cc(2) for _ in range(2)]
        xn3 = [cc(D) for _ in range(2)]
        xT3 = [cc(D) for _ in range(2)]
        QT1 = [cc(NG * D) for _ in range(2)]
        KB1 = [cc(GH * J) for _ in range(2)]
        V1 = [cc((NKB + 1) * H1 * VW1) for _ in range(2)]
        mx1 = cc(H1)
        rd1 = cc(H1)
        O1 = [cc(D) for _ in range(2)]
        OT1 = [cc(D) for _ in range(2)]
        mv4 = [cc(2) for _ in range(2)]
        st4 = cc(6)
        rs4 = [cc(2) for _ in range(2)]
        xb4 = cc(D // 2).bitcast(BF16)
        z4 = [cc(D) for _ in range(2)]
        c4 = [cc(D) for _ in range(2)]
        q4 = cc(D)
        n4 = cc(D)
        t4 = cc(D)
        xq4 = [cc(D // 2).bitcast(BF16) for _ in range(2)]
        xqT4 = [cc(D // 2).bitcast(BF16) for _ in range(2)]
        y4 = [cc(D // 2).bitcast(BF16) for _ in range(2)]
        y4b = [cc(D // 2).bitcast(BF16) for _ in range(2)]
        ob = [cc(D) for _ in range(2)]
        cs = Carver()
        cs.at = after_a
        wqT = cs(H0 * D, DH0)
        wkT = cs(H0 * D, DH0)
        ksz = cs(D)
        ksc = cs(D)
        ksq = cs(D)

        names = """w_loaded w1_loaded moe_loaded ms consts mask_made
            t0_mm t0_cp tanh_made kq_step bv_mm lb_made xs_zeroed0 xs_zeroed1
            x_loaded ctx_loaded stats1 agg1 rst1 rs1_made xn1_made xT1_mm xT1_cp KA_mm KA_cp V0_mm V0_cp S0_mm mx0_made
            S0_sub exp0 PT0_mm PT0_cp O0_mm rd0_made O0_cp OT0_mm OT0_cp Y0_mm x1_made
            stats2 agg2 rst2 rs2_made xn2_made XN_kept xT2_mm xT2_cp lg_mm lg_made
            ro pick ro_e ro_cnt ro_et ro_done ro_exp idx_made scat_made0 scat_made1
            xs_loaded0 xs_loaded1 xsT_mm xsT_cp h_mm h_made hT_mm hT_cp y_mm y_made ys_stored0 ys_stored1
            gi_made gy_made0 gy_made1 ctxc_loaded ctxr_made u_made x2_made x2b_made stats3 agg3 rst3 rs3_made xn3_made xT3_mm xT3_cp
            QT_mm QT_cp KT_mm KB_made V1_mm V1_cp S1_mm mx1_made S1_sub exp1
            PT1_mm PT1_cp O1_mm rd1_made O1_cp OT1_mm OT1_cp Y1_mm x3_made stats4 agg4 rst4 rs4_made xb4_made
            m4_made c4_made t4_made q4_made n4_made xq4_made xqT_mm xqT_cp y4_mm y4_made y4b_made ob_made out_stored0 out_stored1""".split()
        s = {n: sem(n) for n in names}

        block = ctx.enter_context(nc.Block())

        xs_flat = [xs_dram[c] for c in range(NCH)]
        ys_flat = [ys_dram[c] for c in range(NCH)]
        x_rows = a["x"].rearrange("b n d -> (b n) d")
        out_rows = out.rearrange("b n d -> (b n) d")
        w1_rows = a["W1"].rearrange("e d h -> (e d) h")
        w2_rows = a["W2"].rearrange("e h d -> (e h) d")
        ctx_rows = a["ctxT"].rearrange("b d j -> (b d) j")

        def apart(engine):
            engine.nop(nofuse=True)

        def row(ap, parts=P):
            return ap.rearrange("(o n) -> o n", o=1).to_broadcast([parts, ap.shape[0]])

        def col(ap):
            return ap.rearrange("(n o) -> n o", o=1)

        def route_spans():
            return [(0, LOOP0, True), (LOOP0, ROUTE0, False), None,
                    (ROUTE0, ROUTE0 + TURN, True), (ROUTE0 + TURN, NB, False),
                    (NB, NB + LAST_LAG_A, True)]

        def spans(count, lead, lag):
            return [(0, lead, True), (lead, count, False), (count, count + lag, True)]

        def c_spans():
            return [(0, LOOPC, True), (LOOPC, CB, False), (CB, NB, False), (NB, NB + LAST_LAG_C, True)]

        loads = [(wqT, a["WqT"]), (wkT, a["WkT"]), (gamma[:, :], col(a["gamma"])), (beta[:, :], col(a["beta"])),
                 (wv0[:, :], a["Wv"]), (wo0[:, :, :], a["Wout"].rearrange("(c p) n -> p c n", p=P)),
                 (tg[:, 0:2], row(a["g_xattn"])), (tg[:, 2:4], row(a["g_ffn"])),
                 (wgs[:, :], a["Wg"]), (lbias[:, 0, :], row(a["bg"])), (lbias[:, 1, :], row(a["bias"])),
                 ]
        loads1 = [(wq1[:, :], a["Wq1"]), (wk1[:, :], a["Wk1"]), (wv1[:, :], a["Wv1"]), (wo1[:, :], a["Wo1"]),
                 (bq1[:, :], col(a["bq1"])), (bk1[:, :], col(a["bk1"])), (bv1[:, :], col(a["bv1"])),
                 (bo1[:, :], row(a["bo1"])), (kf[:, :], a["kernel"]), (sc[:, 0:1], row(a["input_scale"])),
                 (sc[:, 1:2], row(a["kernel_scale"])), (fbias[:, :], row(a["ffn_bias"]))]

        @block.sync
        def _(sp):
            def load_x(b):
                wait_free(sp, s["x_loaded"], b * 16)
                sp.dma_start(XR[:, bass.ds(b, 1), :].rearrange("p o d -> p (o d)"),
                             x_rows[bass.ds(b * N, N), :]).then_inc(s["x_loaded"], 16)

            def load_ctx_pair(k, p):
                wait_free(sp, s["ctx_loaded"], k * 16)
                apart(sp)
                wait_free(sp, s["V0_mm"], 2 * k - 2)
                sp.dma_start(ctxa[p].rearrange("p (i j) -> p i j", i=2),
                             ctx_rows[bass.ds(k * 2 * D, 2 * D), :].rearrange("(i p) j -> p i j", i=2)).then_inc(s["ctx_loaded"], 16)

            def load_ctx(b, dst, loaded, free):
                wait_free(sp, s[loaded], b * 16)
                apart(sp)
                wait_free(sp, s[free], b - 1)
                sp.dma_start(dst, ctx_rows[bass.ds(b * D, D), :]).then_inc(s[loaded], 16)

            load_x(0)
            load_x(1)
            load_ctx_pair(0, 0)
            for dst, src in loads:
                sp.dma_start(dst, src).then_inc(s["w_loaded"], 16)
            load_ctx_pair(1, 1)

            def clear(c, b):
                sp.dma_start(xs_flat[c][bass.ds(b * ZR, ZR), :].rearrange("(p r) d -> p (r d)", p=ZP),
                             zt[:, :]).then_inc(s[f"xs_zeroed{c}"], 16)

            sp.wait_ge(s["ms"], 11)
            for dst, src in loads1:
                sp.dma_start(dst, src).then_inc(s["w1_loaded"], 16)
            load_x(2)
            load_x(3)
            for b in range(4):
                clear(0, b)
            with sp.Fori(1, CB // 4) as turn:
                for p in range(4):
                    if p % 2 == 0:
                        load_ctx_pair(turn * 2 + p // 2, p // 2)
                    load_x(turn * 4 + p)
                    clear(0, turn * 4 + p)
            with sp.Fori(CB // 4, NB // 4) as turn:
                for p in range(4):
                    if p % 2 == 0:
                        load_ctx_pair(turn * 2 + p // 2, p // 2)
                    load_x(turn * 4 + p)
                    clear(1, turn * 4 + (p - CB))
                    e = turn * 2 + (p // 2 - CB // 2)
                    if p % 2 == 0:
                        sp.dma_start(W1s[:, bass.ds(e, 1), :].rearrange("p o h -> p (o h)"),
                                     w1_rows[bass.ds(e * D, D), :]).then_inc(s["moe_loaded"], 16)
                        sp.dma_start(W2s[:, bass.ds(e, 1), :, :].rearrange("p o c d -> p (o c) d"),
                                     w2_rows[bass.ds(e * EH, EH), :].rearrange("(c p) d -> p c d", p=P)).then_inc(s["moe_loaded"], 16)
                    else:
                        sp.dma_start(b1s[:, bass.ds(e, 1), :].rearrange("p o h -> p (o h)"),
                                     a["b1"][bass.ds(e, 1), :].to_broadcast([P, EH])).then_inc(s["moe_loaded"], 16)
                        sp.dma_start(b2s[:, bass.ds(e, 1), :].rearrange("p o h -> p (o h)"),
                                     a["b2"][bass.ds(e, 1), :].to_broadcast([P, D])).then_inc(s["moe_loaded"], 16)
            def scattered(c):
                sp.wait_ge(s[f"xs_zeroed{c}"], 16 * CB)
                for p in range(2):
                    sp.wait_ge(s[f"scat_made{p}"], 16 * CB * (c + 1))

            def load_group(c, g, p):
                wait_free(sp, s[f"xs_loaded{p}"], (g - p) * 8)
                apart(sp)
                wait_free(sp, s["xsT_mm"], (g - 1) * GT)
                sp.dma_start(xsb[p], xs_flat[c][bass.ds((g - c * NG_B) * (GT * P), GT * P), :].rearrange(
                    "(k p) d -> p k d", p=P)).then_inc(s[f"xs_loaded{p}"], 16)

            def store_group(c, g, p):
                sp.wait_ge(s["y_made"], g * GT + GT)
                apart(sp)
                wait_free(sp, s[f"ys_stored{p}"], (g - p) * 8)
                sp.dma_start(ys_flat[c][bass.ds((g - c * NG_B) * (GT * P), GT * P), :].rearrange("(k p) d -> p k d", p=P),
                             yb[p]).then_inc(s[f"ys_stored{p}"], 16)

            for c in range(NCH):
                scattered(c)
                for g in range(c * NG_B, c * NG_B + 4):
                    load_group(c, g, g % 2)
                    if g >= 2:
                        store_group((g - 2) // NG_B, g - 2, g % 2)
                with sp.Fori(c * NG_B // 2 + 2, (c + 1) * NG_B // 2) as turn:
                    for p in range(2):
                        load_group(c, turn * 2 + p, p)
                        store_group(c, turn * 2 + (p - 2), p)
            for g in range(NCH * NG_B - 2, NCH * NG_B):
                store_group(NCH - 1, g, g % 2)
            sp.wait_ge(s["lg_made"], NB)
            load_ctx(0, ctxc[0], "ctxc_loaded", "V1_mm")
            load_ctx(1, ctxc[1], "ctxc_loaded", "V1_mm")

            def store_out(b, p):
                sp.wait_ge(s["ob_made"], b + 1)
                wait_free(sp, s[f"out_stored{p}"], (b - p) * 8)
                sp.dma_start(out_rows[bass.ds(b * N, N), :], ob[p]).then_inc(s[f"out_stored{p}"], 16)

            for b in range(2, 10):
                load_ctx(b, ctxc[b % 2], "ctxc_loaded", "V1_mm")
            with sp.Fori(5, NB // 2) as turn:
                for p in range(2):
                    load_ctx(turn * 2 + p, ctxc[p], "ctxc_loaded", "V1_mm")
                    store_out(turn * 2 + (p - 10), p)
            for b in range(NB - 10, NB):
                store_out(b, b % 2)
            for p in range(2):
                sp.wait_ge(s[f"out_stored{p}"], NB // 2 * 16)

        @block.gpsimd
        def _(pool):
            g = nc.gpsimd
            g.memset(ident[:, :], 0.0).then_inc(s["ms"], 1)
            g.memset(identb[:, :], 0.0).then_inc(s["ms"], 1)
            g.memset(ltri[:, :], 0.0).then_inc(s["ms"], 1)
            g.memset(onesb[:, :], 1.0).then_inc(s["ms"], 1)
            g.memset(nfirst[:, :, :], 1.0).then_inc(s["ms"], 1)
            g.memset(mask4[:, :], 1.0).then_inc(s["ms"], 1)
            g.memset(zt[:, :], 0.0).then_inc(s["ms"], 1)
            g.memset(one16, 1.0).then_inc(s["ms"], 1)
            g.memset(mhalf[:, :], -0.5).then_inc(s["ms"], 1)
            pool.wait_ge(s["ms"], 9)
            for p in range(2):
                vv = V0[p].rearrange("j (h w) -> j h w", h=H0)
                g.memset(vv[:, :, VW0 - 1:VW0], 1.0).then_inc(s["ms"], 1)
            pool.wait_ge(s["ms"], 11)
            for m in (ident, identb):
                g.affine_select(out=m[:, :], in_=m[:, :], compare_op=ALU.not_equal, fill=1.0, base=0,
                                pattern=[[-1, P]], channel_multiplier=1).then_inc(s["consts"], 1)
            g.affine_select(out=ltri[:, :], in_=ltri[:, :], compare_op=ALU.is_ge, fill=-1.0, base=-1,
                            pattern=[[1, P]], channel_multiplier=-1).then_inc(s["consts"], 1)
            g.iota(iotaD[:, :], pattern=[[-1, NE]], base=NE, channel_multiplier=0,
                   allow_small_or_imprecise_dtypes=True).then_inc(s["consts"], 1)
            g.iota(tau[:, :], pattern=[[0, 1]], base=0, channel_multiplier=P,
                   allow_small_or_imprecise_dtypes=True).then_inc(s["consts"], 1)
            g.iota(maski[:, :], pattern=[[-1, GH]], base=GH, channel_multiplier=1).then_inc(s["consts"], 1)
            g.memset(nfirst[:, :, 0:1], 0.0).then_inc(s["consts"], 1)
            for q in range(P // 32):
                m = mask4[32 * q:32 * q + 32, :]
                wait_free(pool, s["mask_made"], 2 * q)
                g.affine_select(out=m, in_=m, compare_op=ALU.is_ge, fill=0.0, base=0,
                                pattern=[[-DH1, GH]], channel_multiplier=1).then_inc(s["mask_made"], 1)
                pool.wait_ge(s["mask_made"], 2 * q + 1)
                g.affine_select(out=m, in_=m, compare_op=ALU.is_ge, fill=0.0, base=DH1 - 1,
                                pattern=[[DH1, GH]], channel_multiplier=-1).then_inc(s["mask_made"], 1)
            pool.wait_ge(s["mask_made"], 2 * P // 32)
            def rstd(mv, rs, agg, mid, made, b, scale, shift, last_use):
                pool.wait_ge(s[agg], b + 1)
                wait_free(pool, s[last_use], b - 1)
                apart(pool)
                g.tensor_scalar(rs[:, 0:1], mv[:, 1:2], scale, shift, ALU.mult, ALU.add).then_inc(s[mid], 1)
                pool.wait_ge(s[mid], b + 1)
                g.tensor_tensor(rs[:, 1:2], rs[:, 0:1], mhalf[:, :], ALU.pow).then_inc(s[made], 1)

            def scatter(c, b, p):
                bb = b + c * CB
                wait_free(pool, s[f"scat_made{p}"], (bb - p) * 16)
                g.tensor_copy(scat[p], XN[:, bass.ds(bb, 1), :].rearrange("q o d -> q (o d)")).then_inc(s["idx_made"], 1)
                for k in range(2):
                    g.tensor_copy(si[2 * p + k], POS[k][:, bass.ds(bb, 1)]).then_inc(s["idx_made"], 1)
                pool.wait_ge(s["idx_made"], bb * 3 + 3)
                apart(pool)
                for k in range(2):
                    g.indirect_dma_start(out=xs_flat[c][:, :], out_offset=bass.IndirectOffsetOnAxis(ap=si[2 * p + k], axis=0),
                                         in_=scat[p], in_offset=None).then_inc(s[f"scat_made{p}"], 16)

            def step_a(t):
                if (b := t.at(4)) is not None:
                    p = t.par(4)
                    rstd(mv2[p], rs2[p], "agg2", "rst2", "rs2_made", b, 1.0, EPS, "xn2_made")
                if (b := t.at(0)) is not None:
                    p = t.par(0)
                    rstd(mv1[p], rs1[p], "agg1", "rst1", "rs1_made", b, 1.0 + EPS, EPS * EPS, "xn1_made")
                if (b := t.at(5)) is not None:
                    pool.wait_ge(s["xn2_made"], b + 1)
                    g.tensor_copy(XN[:, bass.ds(b, 1), :].rearrange("q o d -> q (o d)"), xn2[t.par(5)]).then_inc(s["XN_kept"], 1)

            for span in route_spans():
                if span is None:
                    pool.wait_ge(s["ro_done"], 1)
                    pool.wait_ge(s["xs_zeroed0"], 16 * CB)
                    continue
                first, last, peeled = span

                def step(t):
                    step_a(t)
                    if first >= ROUTE0:
                        v = t.value - ROUTE0
                        scatter(0, v, t.par(ROUTE0))
                run_steps(pool, NB, first, last, peeled, step, TURN)
            for b in range(NB + LAST_LAG_A - ROUTE0, CB):
                scatter(0, b, b % 2)
            pool.wait_ge(s["ro_done"], 2)
            pool.wait_ge(s["xs_zeroed1"], 16 * CB)
            pool.wait_ge(s["XN_kept"], NB)
            with pool.Fori(0, CB // 2) as turn:
                for p in range(2):
                    scatter(1, turn * 2 + p, p)
            pool.wait_ge(s["w1_loaded"], 16 * len(loads1))
            pool.wait_ge(s["kq_step"], SETUP_STEPS)
            for p in range(2):
                g.memset(QT1[p], 0.0).then_inc(s["ms"], 1)
            pool.wait_ge(s["ms"], 13)

            def gather(b, p, c):
                wait_free(pool, s["x2_made"], b - 1)
                for k in range(2):
                    g.tensor_copy(gi[k][p], POS[k][:, bass.ds(b, 1)]).then_inc(s["gi_made"], 1)
                pool.wait_ge(s["gi_made"], b * 2 + 2)
                apart(pool)
                for k in range(2):
                    g.indirect_dma_start(out=gy[k][p], out_offset=None, in_=ys_flat[c][:, :],
                                         in_offset=bass.IndirectOffsetOnAxis(ap=gi[k][p], axis=0)).then_inc(s[f"gy_made{p}"], 16)

            def step_c(t):
                if (b := t.at(2)) is not None:
                    p = t.par(2)
                    rstd(mv3[p], rs3[p], "agg3", "rst3", "rs3_made", b, 1.0, EPS, "xn3_made")
                if (b := t.at(3)) is not None:
                    pool.wait_ge(s["xn3_made"], b + 1)
                    g.tensor_tensor(XR[:, bass.ds(b, 1), :].rearrange("q o d -> q (o d)"),
                                    XR[:, bass.ds(b, 1), :].rearrange("q o d -> q (o d)"), bo1[:, :], ALU.add).then_inc(s["x2b_made"], 1)
                if (b := t.at(10)) is not None:
                    p = t.par(10)
                    pool.wait_ge(s["y4_made"], b + 1)
                    wait_free(pool, s["ob_made"], b - 1)
                    g.tensor_tensor(y4b[p], y4[p], fbias[:, :], ALU.add).then_inc(s["y4b_made"], 1)
                if (b := t.at(7)) is not None:
                    p = t.par(7)
                    rstd(mv4[p], rs4[p], "agg4", "rst4", "rs4_made", b, 1.0, EPS, "xb4_made")
                if (b := t.at(0)) is not None:
                    gather(b, t.par(0), t.chunk)
                if (b := t.at(8)) is not None:
                    p = t.par(8)
                    pool.wait_ge(s["c4_made"], b + 1)
                    wait_free(pool, s["xq4_made"], b)
                    g.tensor_tensor(t4, z4[p], c4[p], ALU.add).then_inc(s["t4_made"], 1)
                    apart(pool)
                    g.tensor_scalar(n4, z4[p], FP8_TOP, 0.0, ALU.mult, ALU.mult).then_inc(s["n4_made"], 1)
                    pool.wait_ge(s["t4_made"], b + 1)
                    g.tensor_tensor(q4, t4, c4[p], ALU.subtract).then_inc(s["q4_made"], 1)
                    pool.wait_ge(s["n4_made"], b + 1)
                    pool.wait_ge(s["q4_made"], b + 1)
                    wait_free(pool, s["xqT_mm"], b - 1)
                    g.tensor_tensor(xq4[p], q4, n4, ALU.add).then_inc(s["xq4_made"], 1)

            for first, last, peeled in c_spans():
                if first in (0, CB):
                    for p in range(2):
                        pool.wait_ge(s[f"ys_stored{p}"], (NCH if first else 1) * NG_B // 2 * 16)

                def step(t):
                    t.chunk = 0 if first < CB else 1
                    step_c(t)
                run_steps(pool, NB, first, last, peeled, step, TURN)

        @block.scalar
        def _(act):
            A = nc.scalar

            def cp(o, i, done):
                A.activation(o, i, ACT.Copy).then_inc(s[done], 1)

            act.wait_ge(s["w_loaded"], 16 * len(loads))
            A.activation(tg[:, :], tg[:, :], ACT.Tanh).then_inc(s["tanh_made"], 1)
            for k in range(2):
                act.wait_ge(s["t0_mm"], k + 1)
                cp(T0[:, 4 * k:4 * k + 4, :].rearrange("p h d -> p (h d)"), PS[:, k, :], "t0_cp")

            def step_a(t):
                if (b := t.at(3)) is not None:
                    for q in range(2):
                        act.wait_ge(s["PT0_mm"], 2 * b + q + 1)
                        cp(PT0[t.par(3)][:, q * HB0 * P:(q + 1) * HB0 * P], PS[0:J, 2 + q, :], "PT0_cp")
                if (b := t.at(6)) is not None:
                    act.wait_ge(s["xT2_mm"], b + 1)
                    wait_edge(act, t, s["lg_mm"], b - 1)
                    cp(xT2[t.par(6)], PS[:, 6, 0:D], "xT2_cp")
                if (b := t.at(2)) is not None:
                    act.wait_ge(s["S0_sub"], b + 1)
                    A.activation(P0[t.par(2)], S0[t.par(2)], ACT.Exp, scale=DH0 ** -0.5).then_inc(s["exp0"], 1)
                if (b := t.at(1)) is not None:
                    p = t.par(1)
                    act.wait_ge(s["V0_mm"], b + 1)
                    wait_edge(act, t, s["O0_mm"], b - 1)
                    cp(V0[p].rearrange("j (h w) -> j h w", h=H0)[:, :, 0:DH0],
                       PS[0:J, 2, :].rearrange("j (h w) -> j h w", h=H0), "V0_cp")
                if (b := t.at(3)) is not None:
                    act.wait_ge(s["OT0_mm"], b + 1)
                    wait_free(act, s["Y0_mm"], b - 1)
                    cp(OT0[t.par(3)], PS[:, 3, :], "OT0_cp")
                if (b := t.at(0)) is not None:
                    half, width = t.ring(0, 2), H0 // 2 * 2 * J
                    act.wait_ge(s["KA_mm"], b + 1)
                    wait_free(act, s["S0_mm"], b - half - 2)
                    cp(KA[t.ring(0, 4) // 2][:, half * width:(half + 1) * width].rearrange("p (k w) -> p k w", k=2),
                       PS[:, 6:8, 0:HB0 * J], "KA_cp")
                if (b := t.at(1)) is not None:
                    p = t.par(1)
                    act.wait_ge(s["xT1_mm"], b + 1)
                    A.activation(xT1[p], PS[:, 5, 0:D], ACT.Identity, bias=beta[:, 0:1],
                                 scale=gamma[:, 0:1]).then_inc(s["xT1_cp"], 1)

            def route(c):
                act.wait_ge(s["ro_e"], c + 1)
                A.activation(rt["e"], rt["s"], ACT.Exp).then_inc(s["ro_exp"], 1)

            for span in route_spans():
                if span is None:
                    route(0)
                else:
                    run_steps(act, NB, *span, step_a, TURN)
            route(1)

            def step_b(t):
                if (b := t.at(4)) is not None:
                    p = t.par(4)
                    act.wait_ge(s["hT_mm"], b + 1)
                    wait_edge(act, t, s["y_mm"], b - 1)
                    A.activation(hT[p], PS[:, 4 + p, 0:EH], ACT.Relu).then_inc(s["hT_cp"], 1)
                if (b := t.at(0)) is not None:
                    act.wait_ge(s["xsT_mm"], b + 1)
                    wait_edge(act, t, s["h_mm"], b - 1)
                    cp(xsT[t.par(0)], PS[:, t.par(0), 0:D], "xsT_cp")

            for span in spans(NCH * NT, LOOPB, LAST_LAG_B):
                run_steps(act, NCH * NT, *span, step_b, LOOPB)
            act.wait_ge(s["w1_loaded"], 16 * len(loads1))
            act.wait_ge(s["ms"], 13)

            def step_c(t):
                def take_p(b, k):
                    width = 2 * NKB * P
                    act.wait_ge(s["PT1_mm"], 3 * b + k + 1)
                    if k < NP:
                        cp(PT1[:, k * width:(k + 1) * width], PS[:, 4 + k, 0:width], "PT1_cp")
                    else:
                        cp(PT1[0:RR, NP * width:], PS[0:RR, 6, 0:NP * P], "PT1_cp")

                def take_exp(b, p, i):
                    half = slice(i * HH * J, (i + 1) * HH * J)
                    act.wait_ge(s["S1_sub"], 2 * b + i + 1)
                    src = S1[:, half].rearrange("q (g w) -> q g w", g=2)
                    whole, n = NKB * P, 2 * NKB * P
                    A.activation(P1[p][:, half][:, 0:n].rearrange("q (g w) -> q g w", g=2), src[:, :, 0:whole],
                                 ACT.Exp, scale=DH1 ** -0.5).then_inc(s["exp1"], 1)
                    A.activation(P1[p][:, half][:, n:].rearrange("q (g w) -> q g w", g=2), src[:, :, whole:],
                                 ACT.Exp, scale=DH1 ** -0.5).then_inc(s["exp1"], 1)

                if (b := t.at(5)) is not None:
                    wait_free(act, s["O1_mm"], b)
                    take_p(b, 0)
                if (b := t.at(6)) is not None:
                    act.wait_ge(s["OT1_mm"], b + 1)
                    wait_free(act, s["xqT_mm"], t.seen(9, 1))
                    wait_free(act, s["Y1_mm"], b - 1)
                    cp(OT1[t.par(6)], PS[:, 6, 0:D], "OT1_cp")
                if (b := t.at(9)) is not None:
                    act.wait_ge(s["xqT_mm"], b + 1)
                    wait_free(act, s["y4_mm"], b - 1)
                    cp(xqT4[t.par(9)], PS[:, 6, D:D + D // 2].bitcast(BF16), "xqT_cp")
                if (b := t.at(5)) is not None:
                    take_p(b, 1)
                if (b := t.at(4)) is not None:
                    take_exp(b, t.par(4), 0)
                if (b := t.at(5)) is not None:
                    take_p(b, 2)
                if (b := t.at(3)) is not None:
                    act.wait_ge(s["QT_mm"], b + 1)
                    wait_free(act, s["S1_mm"], 2 * (b - 1))
                    for q in range(NG):
                        strip = slice(32 * q, 32 * q + 32)
                        A.activation(QT1[t.par(3)][strip, q * D:(q + 1) * D], PS[strip, 6, 0:D], ACT.Identity,
                                     bias=bq1[strip, 0:1]).then_inc(s["QT_cp"], 1)
                if (b := t.at(4)) is not None:
                    take_exp(b, t.par(4), 1)
                if (b := t.at(2)) is not None:
                    act.wait_ge(s["xT3_mm"], b + 1)
                    wait_free(act, s["QT_mm"], b - 1)
                    cp(xT3[t.par(2)], PS[:, 6, 0:D], "xT3_cp")
                if (b := t.at(3)) is not None:
                    p = t.par(3)
                    act.wait_ge(s["ctxc_loaded"], b * 16 + 16)
                    wait_edge(act, t, s["V1_mm"], b - 1)
                    cp(ctxr[p][:, 0:NKB * P].rearrange("p (j h) -> p j h", h=GH),
                       ctxc[p][:, 0:NKB * KEYS].rearrange("p (j o) -> p j o", o=1).to_broadcast([P, NKB * KEYS, GH]), "ctxr_made")
                    cp(ctxr[p][:, NKB * P:].rearrange("p (g j h) -> p g j h", g=2, h=GH),
                       ctxc[p][:, NKB * KEYS:J].rearrange("p (o j u) -> p o j u", o=1, u=1).to_broadcast([P, 2, JR, GH]), "ctxr_made")

            for span in c_spans():
                run_steps(act, NB, *span, step_c, TURN)

        @block.vector
        def _(dve):
            V = nc.vector
            chain = {"kq_step": 0, "ro": 0}

            def link(ins, name):
                chain[name] += 1
                ins.then_inc(s[name], 1)
                dve.wait_ge(s[name], chain[name])

            def res(b):
                return XR[:, bass.ds(b, 1), :].rearrange("q o d -> q (o d)")

            dve.wait_ge(s["w_loaded"], 16 * len(loads))
            V.tensor_tensor(lbias[:, 0, :], lbias[:, 0, :], lbias[:, 1, :], ALU.add).then_inc(s["lb_made"], 1)
            dve.wait_ge(s["lb_made"], 1)
            dve.wait_ge(s["tanh_made"], 1)

            def stats(src, st, mv, sname, aname, b, last_use):
                wait_free(dve, s[aname], b)
                apart(dve)
                V.bn_stats(st, src).then_inc(s[sname], 1)
                dve.wait_ge(s[sname], b + 1)
                wait_free(dve, s[last_use], b - 1)
                apart(dve)
                V.bn_aggr(mv, st).then_inc(s[aname], 1)

            def normed(o, src, mv, rs, done):
                V.tensor_scalar(o, src, mv[:, 0:1], rs[:, 1:2], ALU.subtract, ALU.mult).then_inc(s[done], 1)

            def step_a(t):
                if (b := t.at(4)) is not None:
                    dve.wait_ge(s["Y0_mm"], b + 1)
                    V.scalar_tensor_tensor(res(b), PS[:, 4, 0:D], tg[:, 0:1], res(b), ALU.mult,
                                           ALU.add).then_inc(s["x1_made"], 1)
                    dve.wait_ge(s["x1_made"], b + 1)
                    stats(res(b), st2, mv2[t.par(4)], "stats2", "agg2", b, "xn2_made")
                if (b := t.at(0)) is not None:
                    dve.wait_ge(s["x_loaded"], b * 16 + 16)
                    stats(res(b), st1, mv1[t.par(0)], "stats1", "agg1", b, "xn1_made")
                if (b := t.at(7)) is not None:
                    dve.wait_ge(s["lg_mm"], b + 1)
                    V.tensor_tensor(LG[:, bass.ds(b, 1), :].rearrange("q o e -> q (o e)"), PS[:, 7, 0:NE],
                                    lbias[:, 0, :], ALU.add).then_inc(s["lg_made"], 1)
                if (b := t.at(5)) is not None:
                    p = t.par(5)
                    dve.wait_ge(s["rs2_made"], b + 1)
                    wait_free(dve, s["xT2_mm"], b - 1)
                    wait_free(dve, s["XN_kept"], b - 1)
                    normed(xn2[p], res(b), mv2[p], rs2[p], "xn2_made")
                if (b := t.at(2)) is not None:
                    p = t.par(2)
                    sv = PS[:, 0:2, 0:HB0 * J].rearrange("q k (h j) -> q k h j", j=J)
                    dve.wait_ge(s["S0_mm"], b + 1)
                    wait_free(dve, s["S0_sub"], b)
                    V.tensor_reduce(mx0.rearrange("q (k h) -> q k h", k=2), sv, X, ALU.max).then_inc(s["mx0_made"], 1)
                    dve.wait_ge(s["mx0_made"], b + 1)
                    wait_free(dve, s["exp0"], b - 1)
                    V.tensor_tensor(S0[p].rearrange("q (k h j) -> q k h j", k=2, j=J), sv,
                                    mx0.rearrange("q (k h o) -> q k h o", k=2, o=1).to_broadcast([P, 2, HB0, J]),
                                    ALU.subtract).then_inc(s["S0_sub"], 1)
                if (b := t.at(3)) is not None:
                    p = t.par(3)
                    ov = PS[:, 4:6, 0:HB0 * VW0].rearrange("q k (h w) -> q k h w", w=VW0)
                    dve.wait_ge(s["O0_mm"], b + 1)
                    wait_free(dve, s["O0_cp"], b)
                    V.reciprocal(rd0.rearrange("q (k h o) -> q k h o", k=2, o=1), ov[:, :, :, DH0:VW0]).then_inc(s["rd0_made"], 1)
                    dve.wait_ge(s["rd0_made"], b + 1)
                    wait_free(dve, s["OT0_mm"], b - 1)
                    V.tensor_tensor(O0[p].rearrange("q (k h w) -> q k h w", k=2, w=DH0), ov[:, :, :, 0:DH0],
                                    rd0.rearrange("q (k h o) -> q k h o", k=2, o=1).to_broadcast([P, 2, HB0, DH0]),
                                    ALU.mult).then_inc(s["O0_cp"], 1)
                if (b := t.at(1)) is not None:
                    p = t.par(1)
                    dve.wait_ge(s["rs1_made"], b + 1)
                    wait_free(dve, s["xT1_mm"], b - 1)
                    normed(xn1[p], res(b), mv1[p], rs1[p], "xn1_made")
                if t.place % 4 >= 2:
                    b = t.value - t.place % 4 - 8
                    if not isinstance(b, int) or 0 <= b < NB:
                        pick(t.chunk, b, t.place % 4 - 2)

            be = lambda v: v.rearrange("q (b e) -> q b e", e=NE)
            eb = lambda v: v.rearrange("q (e b) -> q e b", e=NE)

            def pick(c, b, k):
                lb = b - c * CB
                n = b * 3 + 6 * k
                v, oh = rt[f"v{k}"][:, bass.ds(lb, 4)], be(rt[f"oh{k}"])[:, bass.ds(lb, 4), :]
                oh0 = be(rt["oh0"])[:, bass.ds(lb, 4), :]
                lg = LG[:, bass.ds(b, 4), :]
                ranks = iotaD[:, :].rearrange("q (o e) -> q o e", o=1).to_broadcast([P, 4, NE])
                per_b = lambda w: w.rearrange("q (b o) -> q b o", o=1).to_broadcast([P, 4, NE])
                eq, second, m = be(rt["pick_eq"]), be(rt["pick_second"]), rt["pick_m"]

                def then(ins, i):
                    ins.then_inc(s["pick"], 1)
                    dve.wait_ge(s["pick"], n + i)

                if k == 0:
                    dve.wait_ge(s["lg_made"], b + 4)
                else:
                    lg = second
                then(V.tensor_reduce(v, lg, X, ALU.max), 1)
                then(V.tensor_tensor(eq, lg, per_b(v), ALU.is_equal), 2)
                then(V.tensor_tensor(eq, eq, ranks, ALU.mult), 3)
                then(V.tensor_reduce(m, eq, X, ALU.max), 4)
                then(V.tensor_tensor(oh, ranks, per_b(m), ALU.is_equal), 5)
                if k == 0:
                    then(V.scalar_tensor_tensor(second, oh, -3.0e38, lg, ALU.mult, ALU.add), 6)
                else:
                    then(V.tensor_tensor(rtM.rearrange("q (e b) -> q b e", e=NE)[:, bass.ds(lb, 4), :], oh0, oh, ALU.add), 6)

            def route(c):
                lo = c * CB
                eq = LG[:, lo:lo + CB, :]
                dve.wait_ge(s["pick"], 3 * (lo + CB))
                V.tensor_tensor(rt["s"], rt["v1"], rt["v0"], ALU.subtract).then_inc(s["ro_e"], 1)
                dve.wait_ge(s["ro_cnt"], c + 1)
                link(V.tensor_tensor_scan(rt["cum"], nfirst[:, :, :].rearrange("q e b -> q (e b)"), PS[:, 1, :],
                                          0.0, ALU.mult, ALU.add), "ro")
                link(V.tensor_scalar(rti, eb(rt["cum"])[:, :, CB - 1], float(P - 1), None, ALU.add), "ro")
                link(V.tensor_scalar(rti, rti, -P, None, ALU.bitwise_and), "ro")
                link(V.tensor_copy(rt["pad"], rti), "ro")
                link(V.tensor_tensor_scan(rt["inc"], one16, rt["pad"], 0.0, ALU.mult, ALU.add), "ro")
                link(V.tensor_tensor(rt["base"], rt["inc"], rt["pad"], ALU.subtract), "ro")
                link(V.tensor_scalar(rt["le"], rt["inc"], tau[:, 0:1], None, ALU.is_le), "ro")
                link(V.tensor_reduce(rt["et"], rt["le"], X, ALU.add), "ro")
                V.tensor_scalar(rt["et"], rt["et"], float(NE - 1), None, ALU.min).then_inc(s["ro_et"], 1)
                link(V.tensor_tensor(rt["pos"], rt["cum"], PS[:, 0, :], ALU.add), "ro")
                link(V.tensor_tensor(eb(rt["pos"]), eb(rt["pos"]),
                                     rt["base"].rearrange("q (e o) -> q e o", o=1).to_broadcast([P, NE, CB]), ALU.add), "ro")
                for k in range(2):
                    link(V.tensor_tensor(eq, be(rt[f"oh{k}"]), rt["pos"].rearrange("q (e b) -> q b e", e=NE),
                                         ALU.mult), "ro")
                    link(V.tensor_reduce(rt["m"], eq, X, ALU.add), "ro")
                    link(V.tensor_copy(POS[k][:, lo:lo + CB], rt["m"]), "ro")
                dve.wait_ge(s["ro_exp"], c + 1)
                link(V.tensor_scalar(rt["s"], rt["e"], 1.0, None, ALU.add), "ro")
                link(V.reciprocal(rt["s"], rt["s"]), "ro")
                link(V.tensor_scalar(WT[0][:, lo:lo + CB], rt["s"], tg[:, 2:3], None, ALU.mult), "ro")
                link(V.tensor_tensor(WT[1][:, lo:lo + CB], WT[0][:, lo:lo + CB], rt["e"], ALU.mult), "ro")
                dve.wait_ge(s["ro_et"], 2 * c + 2)
                e4 = PS[0:1, 2, 0:P].rearrange("o (w k) -> o w k", k=4)
                link(V.tensor_copy(rt["pk"][0:1, :].rearrange("o (w k) -> o w k", k=4), e4), "ro")
                pk = rt["pk"][0:1, :].rearrange("o (w h k) -> o (w h) k", h=2, k=2)
                pairs = rt["pk2"][0:1, :]
                link(V.scalar_tensor_tensor(pairs, pk[:, :, 1], 16.0, pk[:, :, 0], ALU.mult, ALU.add), "ro")
                pq = pairs.rearrange("o (w h) -> o w h", h=2)
                words = NT // 4
                V.scalar_tensor_tensor(ETI[:, c * words:(c + 1) * words], pq[:, 0:words, 1], 256.0, pq[:, 0:words, 0],
                                       ALU.mult, ALU.add).then_inc(s["ro_done"], 1)

            for span in route_spans():
                if span is None:
                    route(0)
                    continue
                first, last, peeled = span
                if last == NB + LAST_LAG_A:
                    last += -last % 4

                def step(t):
                    t.chunk = 0 if first < ROUTE0 else 1
                    step_a(t)
                run_steps(dve, NB, first, last, peeled, step, TURN)
            route(1)

            dve.wait_ge(s["w1_loaded"], 16 * len(loads1))
            dve.wait_ge(s["consts"], 7)
            link(V.tensor_scalar(bv1b[:, :], ident[:, :], 0.0, bv1[:, 0:1], ALU.mult, ALU.add), "kq_step")
            dve.wait_ge(s["bv_mm"], 1)
            link(V.tensor_tensor(bo1[:, :], bo1[:, :], PS[:, 3, 0:D], ALU.add), "kq_step")
            link(V.tensor_scalar(bo1[:, :], bo1[:, :], tg[:, 1:2], None, ALU.mult), "kq_step")
            link(V.tensor_scalar(maski[:, :], maski[:, :], GH - 1, None, ALU.bitwise_and), "kq_step")
            link(V.tensor_scalar(maskv[:, :], maski[:, :], 0.0, None, ALU.is_equal), "kq_step")
            link(V.tensor_scalar(rlow[:, :], tau[:, :], float(JR * GH * P), None, ALU.is_lt), "kq_step")
            link(V.tensor_scalar(maskr[:, 0:GH], maskv[:, :], rlow[:, 0:1], None, ALU.mult), "kq_step")
            link(V.tensor_tensor(maskr[:, GH:2 * GH], maskv[:, :], maskr[:, 0:GH], ALU.subtract), "kq_step")
            for p in range(2):
                vv = V1[p].rearrange("q (c h w) -> q c h w", c=NKB + 1, w=VW1)
                for c in range(NKB):
                    link(V.tensor_copy(vv[:, c, :, VW1 - 1].rearrange("q (g h) -> q g h", h=GH),
                                       maskv[:, :].rearrange("q (o h) -> q o h", o=1).to_broadcast([P, NG, GH])), "kq_step")
                link(V.tensor_copy(vv[:, NKB, :, VW1 - 1].rearrange("q (g h) -> q g h", h=2 * GH),
                                   maskr[:, :].rearrange("q (o h) -> q o h", o=1).to_broadcast([P, NP, 2 * GH])), "kq_step")
            link(V.reciprocal(scr[:, :], sc[:, :]), "kq_step")
            link(V.tensor_tensor(scm[:, :], sc[:, 0:1], sc[:, 1:2], ALU.mult), "kq_step")
            link(V.tensor_scalar(ksz, kf[:, :], scr[:, 1:2], None, ALU.mult), "kq_step")
            link(V.tensor_scalar(ksc.bitcast(I32), ksz.bitcast(I32), EXP_BITS, None, ALU.bitwise_and), "kq_step")
            link(V.tensor_scalar(ksc, ksc, FP8_LEAST, FP8_ROUND, ALU.max, ALU.mult), "kq_step")
            link(V.tensor_tensor(ksq, ksz, ksc, ALU.add), "kq_step")
            link(V.tensor_tensor(ksq, ksq, ksc, ALU.subtract), "kq_step")
            link(V.tensor_scalar(ksz, ksz, FP8_TOP, 0.0, ALU.mult, ALU.mult), "kq_step")
            link(V.tensor_tensor(kq[:, :], ksq, ksz, ALU.add), "kq_step")
            assert chain["kq_step"] == SETUP_STEPS

            dve.wait_ge(s["moe_loaded"], 4 * 16 * NE)
            dve.wait_ge(s["ro_done"], NCH)

            experts = Experts(dve, ETI)

            def step_b(t):
                if (b := t.at(6)) is not None:
                    p = t.par(6)
                    e = experts.of(t, 6)
                    dve.wait_ge(s["y_mm"], b + 1)
                    k = t.ring(6, 2 * GT)
                    if k % GT == 0:
                        wait_free(dve, s[f"ys_stored{k // GT}"], (b - k) * 2)
                        apart(dve)
                    V.tensor_tensor(yb[k // GT][:, k % GT, :], PS[:, 6 + p, 0:D],
                                    b2s[:, bass.ds(e, 1), :].rearrange("q o h -> q (o h)"), ALU.add).then_inc(s["y_made"], 1)
                if (b := t.at(2)) is not None:
                    p = t.par(2)
                    e = experts.of(t, 2)
                    dve.wait_ge(s["h_mm"], b + 1)
                    wait_edge(dve, t, s["hT_mm"], b - 1)
                    V.tensor_tensor(hb[p], PS[:, 2 + p, 0:EH],
                                    b1s[:, bass.ds(e, 1), :].rearrange("q o h -> q (o h)"), ALU.add).then_inc(s["h_made"], 1)

            for span in spans(NCH * NT, LOOPB, LAST_LAG_B):
                run_steps(dve, NCH * NT, *span, step_b, LOOPB)

            def gather_stats(src, st, sname, aname, b):
                wait_free(dve, s[aname], b)
                apart(dve)
                V.bn_stats(st, src).then_inc(s[sname], 1)

            def join_stats(st, mv, sname, aname, b, last_use):
                dve.wait_ge(s[sname], b + 1)
                wait_free(dve, s[last_use], b - 1)
                apart(dve)
                V.bn_aggr(mv, st).then_inc(s[aname], 1)

            def step_c(t):
                gh = NG // 2

                def largest(i):
                    if (b := t.at(4)) is not None:
                        sv = PS[:, gh * i:gh * (i + 1), 0:GH * J].rearrange("q g (j h) -> q g h j", j=J)
                        dve.wait_ge(s["S1_mm"], 2 * b + i + 1)
                        wait_free(dve, s["S1_sub"], 2 * b + i - 1)
                        V.tensor_reduce(mx1[:, HH * i:HH * (i + 1)].rearrange("q (g h) -> q g h", g=gh), sv, X,
                                        ALU.max).then_inc(s["mx1_made"], 1)

                def less_largest(i):
                    if (b := t.at(4)) is not None:
                        sv = PS[:, gh * i:gh * (i + 1), 0:GH * J].rearrange("q g (j h) -> q g j h", j=J)
                        dve.wait_ge(s["mx1_made"], 2 * b + i + 1)
                        wait_free(dve, s["exp1"], 2 * (2 * b + i - 1))
                        V.tensor_tensor(S1[:, HH * J * i:HH * J * (i + 1)].rearrange("q (g j h) -> q g j h", g=gh, j=J), sv,
                                        mx1[:, HH * i:HH * (i + 1)].rearrange("q (g o h) -> q g o h", g=gh, o=1).to_broadcast(
                                            [P, gh, J, GH]), ALU.subtract).then_inc(s["S1_sub"], 1)

                ov = PS[:, 7, 0:H1 * VW1].rearrange("q (h w) -> q h w", w=VW1)
                if (b := t.at(6)) is not None:
                    dve.wait_ge(s["O1_mm"], b + 1)
                    wait_free(dve, s["O1_cp"], b)
                    V.reciprocal(rd1.rearrange("q (h o) -> q h o", o=1), ov[:, :, DH1:VW1]).then_inc(s["rd1_made"], 1)
                if (b := t.at(2)) is not None:
                    join_stats(st3, mv3[t.par(2)], "stats3", "agg3", b, "xn3_made")
                if (b := t.at(7)) is not None:
                    dve.wait_ge(s["Y1_mm"], b + 1)
                    wait_free(dve, s["y4_mm"], t.seen(9))
                    dve.wait_ge(s["x2b_made"], b + 1)
                    V.scalar_tensor_tensor(res(b), PS[:, 5, 0:D], tg[:, 1:2], res(b), ALU.mult,
                                           ALU.add).then_inc(s["x3_made"], 1)
                if (b := t.at(6)) is not None:
                    p = t.par(6)
                    dve.wait_ge(s["rd1_made"], b + 1)
                    wait_free(dve, s["OT1_mm"], b - 1)
                    V.tensor_tensor(O1[p].rearrange("q (h w) -> q h w", w=DH1), ov[:, :, 0:DH1],
                                    rd1.rearrange("q (h o) -> q h o", o=1).to_broadcast([P, H1, DH1]),
                                    ALU.mult).then_inc(s["O1_cp"], 1)
                if (b := t.at(10)) is not None:
                    p = t.par(10)
                    dve.wait_ge(s["y4_mm"], b + 1)
                    wait_free(dve, s["y4b_made"], b - 1)
                    V.tensor_scalar(y4[p], PS[:, 5, D:2 * D], scm[:, 0:1], None, ALU.mult).then_inc(s["y4_made"], 1)
                if (b := t.at(7)) is not None:
                    dve.wait_ge(s["x3_made"], b + 1)
                    gather_stats(res(b), st4, "stats4", "agg4", b)
                largest(0)
                if (b := t.at(7)) is not None:
                    join_stats(st4, mv4[t.par(7)], "stats4", "agg4", b, "xb4_made")
                if (b := t.at(2)) is not None:
                    p = t.par(2)
                    dve.wait_ge(s["rs3_made"], b + 1)
                    wait_free(dve, s["xT3_mm"], b - 1)
                    normed(xn3[p], res(b), mv3[p], rs3[p], "xn3_made")
                less_largest(0)
                if (b := t.at(8)) is not None:
                    p = t.par(8)
                    dve.wait_ge(s["rs4_made"], b + 1)
                    wait_free(dve, s["m4_made"], 2 * b)
                    normed(xb4, res(b), mv4[p], rs4[p], "xb4_made")
                if (b := t.at(8)) is not None:
                    p = t.par(8)
                    dve.wait_ge(s["xb4_made"], b + 1)
                    wait_free(dve, s["xq4_made"], b - 1)
                    V.tensor_scalar(z4[p], xb4, scr[:, 0:1], None, ALU.mult).then_inc(s["m4_made"], 1)
                if (b := t.at(3)) is not None:
                    p = t.par(3)
                    dve.wait_ge(s["KT_mm"], b + 1)
                    wait_free(dve, s["V1_mm"], t.seen(4, 1))
                    wait_free(dve, s["S1_mm"], 2 * (b - 1))
                    V.scalar_tensor_tensor(KB1[p].rearrange("q (j h) -> q j h", h=GH),
                                           PS[:, 5, KT_AT:KT_AT + J].rearrange("q (j o) -> q j o", o=1).to_broadcast([P, J, GH]),
                                           bk1[:, 0:1],
                                           mask4[:, :].rearrange("q (o h) -> q o h", o=1).to_broadcast([P, J, GH]),
                                           ALU.add, ALU.mult).then_inc(s["KB_made"], 1)
                if (b := t.at(4)) is not None:
                    p = t.par(4)
                    n = NKB * H1 * VW1
                    dve.wait_ge(s["V1_mm"], b + 1)
                    wait_free(dve, s["O1_mm"], b - 1)
                    V.tensor_tensor(V1[p][:, 0:n].rearrange("q (g h w) -> q g h w", h=GH, w=VW1)[:, :, :, 0:DH1],
                                    PS[:, 5, 0:NKB * D].rearrange("q (g h w) -> q g h w", h=GH, w=DH1),
                                    maskv[:, :].rearrange("q (o h u) -> q o h u", o=1, u=1).to_broadcast([P, NKB * NG, GH, DH1]),
                                    ALU.mult).then_inc(s["V1_cp"], 1)
                    V.tensor_tensor(V1[p][0:RR, n:].rearrange("q (g h w) -> q g h w", h=2 * GH, w=VW1)[:, :, :, 0:DH1],
                                    PS[0:RR, 5, NKB * D:(NKB + 1) * D].rearrange("q (g h w) -> q g h w", h=2 * GH, w=DH1),
                                    maskr[0:RR, :].rearrange("q (o h u) -> q o h u", o=1, u=1).to_broadcast([RR, NP, 2 * GH, DH1]),
                                    ALU.mult).then_inc(s["V1_cp"], 1)
                if (b := t.at(8)) is not None:
                    p = t.par(8)
                    dve.wait_ge(s["m4_made"], 2 * b + 1)
                    V.tensor_scalar(c4[p].bitcast(I32), z4[p].bitcast(I32), EXP_BITS, None, ALU.bitwise_and).then_inc(s["m4_made"], 1)
                if (b := t.at(8)) is not None:
                    p = t.par(8)
                    dve.wait_ge(s["m4_made"], 2 * b + 2)
                    V.tensor_scalar(c4[p], c4[p], FP8_LEAST, FP8_ROUND, ALU.max, ALU.mult).then_inc(s["c4_made"], 1)
                largest(1)
                if (b := t.at(1)) is not None:
                    p = t.par(1)
                    dve.wait_ge(s[f"gy_made{p}"], (b - p) * 16 + 32)
                    wait_free(dve, s["x2_made"], b)
                    V.scalar_tensor_tensor(uc, gy[0][p], WT[0][:, bass.ds(b, 1)], res(b), ALU.mult, ALU.add).then_inc(s["u_made"], 1)
                less_largest(1)
                if (b := t.at(1)) is not None:
                    p = t.par(1)
                    dve.wait_ge(s["u_made"], b + 1)
                    V.scalar_tensor_tensor(res(b), gy[1][p], WT[1][:, bass.ds(b, 1)], uc, ALU.mult, ALU.add).then_inc(s["x2_made"], 1)
                if (b := t.at(11)) is not None:
                    p = t.par(11)
                    dve.wait_ge(s["y4b_made"], b + 1)
                    wait_free(dve, s[f"out_stored{p}"], (b - p) * 8)
                    V.scalar_tensor_tensor(ob[p], y4b[p], tg[:, 3:4], res(b), ALU.mult, ALU.add).then_inc(s["ob_made"], 1)
                if (b := t.at(1)) is not None:
                    dve.wait_ge(s["x2_made"], b + 1)
                    gather_stats(res(b), st3, "stats3", "agg3", b)

            for span in c_spans():
                run_steps(dve, NB, *span, step_c, TURN)

        @block.tensor
        def _(pe):
            T = nc.tensor

            def mm(o, l, r, start=True, stop=True):
                return T.matmul(o, l, r, start=start, stop=stop)

            pe.wait_ge(s["w_loaded"], 16 * len(loads))
            for h in range(H0):
                last = mm(PS[:, h // 4, (h % 4) * D:(h % 4 + 1) * D], wkT[:, h * D:(h + 1) * D], wqT[:, h * D:(h + 1) * D])
                if h % 4 == 3:
                    last.then_inc(s["t0_mm"], 1)
            pe.wait_ge(s["t0_cp"], 2)
            pe.wait_ge(s["consts"], 7)

            def step_a(t):
                if (b := t.at(3)) is not None:
                    p = t.par(3)
                    wait_edge(pe, t, s["exp0"], b + 1)
                    wait_edge(pe, t, s["OT0_cp"], t.seen(3))
                    wait_edge(pe, t, s["V0_cp"], t.seen(1))
                    for h in range(H0):
                        last = T.transpose(PS[0:J, 2 + h // HB0, (h % HB0) * P:(h % HB0 + 1) * P],
                                           P0[p][:, h * J:(h + 1) * J], ident[:, :])
                        if h % HB0 == HB0 - 1:
                            last.then_inc(s["PT0_mm"], 1)
                if (b := t.at(6)) is not None:
                    p = t.par(6)
                    pe.wait_ge(s["xn2_made"], b + 1)
                    wait_free(pe, s["KA_cp"], t.seen(0))
                    wait_edge(pe, t, s["xT2_cp"], b)
                    T.transpose(PS[:, 6, 0:D], xn2[p], ident[:, :]).then_inc(s["xT2_mm"], 1)
                if (b := t.at(7)) is not None:
                    p = t.par(7)
                    wait_edge(pe, t, s["KA_cp"], t.seen(0))
                    wait_edge(pe, t, s["xT2_cp"], b + 1)
                    wait_edge(pe, t, s["lg_made"], b)
                    mm(PS[:, 7, 0:NE], xT2[p], wgs[:, :]).then_inc(s["lg_mm"], 1)
                if (b := t.at(2)) is not None:
                    p = t.par(2)
                    pe.wait_ge(s["xT1_cp"], b + 1)
                    wait_edge(pe, t, s["KA_cp"], b + 2 - t.ring(2, 2))
                    wait_free(pe, s["S0_sub"], b)
                    keys = KA[t.ring(2, 4) // 2].rearrange("p (h i j) -> p h i j", h=H0, i=2)
                    for k in range(2):
                        last = mm(PS[:, k, 0:HB0 * J], xT1[p], keys[:, k * HB0:(k + 1) * HB0, t.ring(2, 2), :])
                    last.then_inc(s["S0_mm"], 1)
                if (b := t.at(3)) is not None:
                    p = t.par(3)
                    pe.wait_ge(s["PT0_cp"], 2 * b + 2)
                    wait_free(pe, s["x1_made"], t.seen(3))
                    wait_edge(pe, t, s["xT1_cp"], t.seen(1))
                    for h in range(H0):
                        last = mm(PS[:, 4 + h // HB0, (h % HB0) * VW0:(h % HB0 + 1) * VW0],
                                  PT0[p][:, h * P:(h + 1) * P], V0[p][:, h * VW0:(h + 1) * VW0])
                    last.then_inc(s["O0_mm"], 1)
                def keys_through(bank):
                    if (b := t.at(0)) is not None:
                        half = t.ring(0, 2)
                        if bank == 0:
                            if half == 0:
                                pe.wait_ge(s["ctx_loaded"], b * 8 + 16)
                            wait_edge(pe, t, s["KA_cp"], b)
                            wait_free(pe, s["xT2_cp"], t.seen(6, 1))
                        else:
                            wait_edge(pe, t, s["lg_made"], t.seen(7, 1))
                        for h in range(2 * bank, 2 * bank + 2):
                            last = mm(PS[:, 6 + bank, (h % 2) * 2 * J:(h % 2 + 1) * 2 * J],
                                      T0[:, half * (H0 // 2) + h, :], ctxa[t.ring(0, 4) // 2])
                        if bank == 1:
                            last.then_inc(s["KA_mm"], 1)

                keys_through(0)
                if (b := t.at(1)) is not None:
                    i = t.ring(1, 2)
                    wait_edge(pe, t, s["V0_cp"], b)
                    wait_edge(pe, t, s["PT0_cp"], 2 * t.seen(3, 1))
                    mm(PS[0:J, 2, :], ctxa[t.ring(1, 4) // 2][:, i * J:(i + 1) * J], wv0[:, :]).then_inc(s["V0_mm"], 1)
                if (b := t.at(3)) is not None:
                    p = t.par(3)
                    pe.wait_ge(s["O0_cp"], b + 1)
                    for q in range(HD0 // P):
                        last = T.transpose(PS[:, 3, q * P:(q + 1) * P], O0[p][:, q * P:(q + 1) * P], ident[:, :])
                    last.then_inc(s["OT0_mm"], 1)
                keys_through(1)
                if (b := t.at(1)) is not None:
                    p = t.par(1)
                    pe.wait_ge(s["xn1_made"], b + 1)
                    wait_edge(pe, t, s["xT1_cp"], b)
                    wait_edge(pe, t, s["O0_cp"], t.seen(3, 1))
                    T.transpose(PS[:, 5, 0:D], xn1[p], ident[:, :]).then_inc(s["xT1_mm"], 1)
                if (b := t.at(3)) is not None:
                    p = t.par(3)
                    pe.wait_ge(s["OT0_cp"], b + 1)
                    for q in range(HD0 // P):
                        last = mm(PS[:, 4, 0:D], OT0[p][:, q * P:(q + 1) * P], wo0[:, q, :],
                                  start=(q == 0), stop=(q == HD0 // P - 1))
                    last.then_inc(s["Y0_mm"], 1)

            def route(c):
                pe.wait_ge(s["pick"], 3 * CB * (c + 1))
                pe.wait_ge(s["S0_sub"], ROUTE0 - 2 if c == 0 else NB)
                pe.wait_ge(s["xT2_cp"], ROUTE0 - 6 if c == 0 else NB)
                pe.wait_ge(s["lg_made"], ROUTE0 - 7 if c == 0 else NB)
                pe.wait_ge(s["V0_cp"], ROUTE0 - 1 if c == 0 else NB)
                pe.wait_ge(s["PT0_cp"], 2 * (ROUTE0 - 3 if c == 0 else NB))
                mm(PS[:, 0, :], ltri[:, :], rtM)
                mm(PS[:, 1, :], onesb[:, :], rtM).then_inc(s["ro_cnt"], 1)
                pe.wait_ge(s["ro_et"], 2 * c + 1)
                mm(PS[0:1, 2, 0:P], rt["et"], ident[:, :]).then_inc(s["ro_et"], 1)
                pe.wait_ge(s["ro_done"], c + 1)

            for span in route_spans():
                if span is None:
                    route(0)
                else:
                    run_steps(pe, NB, *span, step_a, TURN)
            route(1)

            pe.wait_ge(s["w1_loaded"], 16 * len(loads1))
            pe.wait_ge(s["kq_step"], 1)
            pe.wait_ge(s["OT0_cp"], NB)
            pe.wait_ge(s["PT0_cp"], 2 * NB)
            mm(PS[:, 3, 0:D], bv1b[:, :], wo1[:, :]).then_inc(s["bv_mm"], 1)
            pe.wait_ge(s["kq_step"], 2)
            pe.wait_ge(s["moe_loaded"], 4 * 16 * NE)
            for last in ("OT0_cp", "KA_cp", "xT1_cp", "O0_cp", "x1_made", "xT2_cp", "lg_made"):
                pe.wait_ge(s[last], NB)

            experts = Experts(pe, ETI)

            def step_b(t):
                if (b := t.at(6)) is not None:
                    p = t.par(6)
                    e = experts.of(t, 6)
                    pe.wait_ge(s["hT_cp"], b + 1)
                    wait_free(pe, s["y_made"], b - 1)
                    for q in range(2):
                        last = mm(PS[:, 6 + p, 0:D], hT[p][:, q * P:(q + 1) * P],
                                  W2s[:, bass.ds(e, 1), q, :].rearrange("q o d -> q (o d)"), start=(q == 0), stop=(q == 1))
                    last.then_inc(s["y_mm"], 1)
                if (b := t.at(4)) is not None:
                    p = t.par(4)
                    pe.wait_ge(s["h_made"], b + 1)
                    wait_edge(pe, t, s["hT_cp"], b - 1)
                    for q in range(2):
                        last = T.transpose(PS[:, 4 + p, q * P:(q + 1) * P], hb[p][:, q * P:(q + 1) * P], ident[:, :])
                    last.then_inc(s["hT_mm"], 1)
                if (b := t.at(2)) is not None:
                    p = t.par(2)
                    e = experts.of(t, 2)
                    pe.wait_ge(s["xsT_cp"], b + 1)
                    wait_edge(pe, t, s["h_made"], b - 1)
                    mm(PS[:, 2 + p, 0:EH], xsT[p], W1s[:, bass.ds(e, 1), :].rearrange("q o h -> q (o h)")).then_inc(s["h_mm"], 1)
                if (b := t.at(0)) is not None:
                    p = t.par(0)
                    k = t.ring(0, 2 * GT)
                    if k % GT == 0:
                        pe.wait_ge(s[f"xs_loaded{k // GT}"], (b - k) * 2 + 16)
                    wait_edge(pe, t, s["xsT_cp"], b - 1)
                    T.transpose(PS[:, p, 0:D], xsb[k // GT][:, k % GT, :], ident[:, :]).then_inc(s["xsT_mm"], 1)

            for span in spans(NCH * NT, LOOPB, LAST_LAG_B):
                run_steps(pe, NCH * NT, *span, step_b, LOOPB)
            pe.wait_ge(s["y_made"], NCH * NT)
            pe.wait_ge(s["ms"], 13)
            pe.wait_ge(s["kq_step"], SETUP_STEPS)
            pe.wait_ge(s["w1_loaded"], 16 * len(loads1))

            def step_c(t):
                def scores(q):
                    if (b := t.at(4)) is not None:
                        p = t.par(4)
                        if q == 0:
                            pe.wait_ge(s["QT_cp"], NG * b + NG)
                            pe.wait_ge(s["KB_made"], b + 1)
                        if q % 2 == 0:
                            wait_edge(pe, t, s["S1_sub"], 2 * b + q // 2 - 1)
                        ins = mm(PS[:, q, 0:GH * J], QT1[p][:, q * D:(q + 1) * D], KB1[p])
                        if q % 2 == 1:
                            ins.then_inc(s["S1_mm"], 1)

                def transpose_whole(k):
                    if (b := t.at(5)) is not None:
                        if k == 0:
                            pe.wait_ge(s["exp1"], 4 * b + 2)
                        else:
                            wait_edge(pe, t, s["exp1"], 4 * b + 4)
                        for i in range(2 * NKB):
                            at = k * HH * J + i * P
                            last = T.transpose(PS[:, 4 + k, i * P:(i + 1) * P], P1[t.par(5)][:, at:at + P], ident[:, :])
                        last.then_inc(s["PT1_mm"], 1)

                def transpose_shared():
                    if (b := t.at(5)) is not None:
                        for k in range(NP):
                            last = T.transpose(PS[0:RR, 6, k * P:(k + 1) * P],
                                               P1[t.par(5)][:, (k + 1) * HH * J - RR:(k + 1) * HH * J], ident[:, :])
                        last.then_inc(s["PT1_mm"], 1)

                def attend(k):
                    if (b := t.at(5)) is not None:
                        if k == 0:
                            pe.wait_ge(s["PT1_cp"], 3 * b + k + 1)
                        else:
                            wait_edge(pe, t, s["PT1_cp"], 3 * b + k + 1)
                        gw = GH * VW1
                        v = V1[t.par(5)].rearrange("q (c w) -> q c w", c=NKB + 1)
                        for i in range(2 * NKB if k < NP else NP):
                            if k < NP:
                                g, c = 2 * k + i // NKB, i % NKB
                                at = (g * NKB + c) * P
                                last = mm(PS[:, 7, g * gw:(g + 1) * gw], PT1[:, at:at + P], v[:, c, g * gw:(g + 1) * gw],
                                          start=(k == 0 and i == 0), stop=False)
                            else:
                                at = (NG * NKB + i) * P
                                last = mm(PS[:, 7, 2 * i * gw:2 * (i + 1) * gw], PT1[0:RR, at:at + P],
                                          v[0:RR, NKB, 2 * i * gw:2 * (i + 1) * gw], start=False, stop=(i == NP - 1))
                        if k == NP:
                            last.then_inc(s["O1_mm"], 1)

                def bank5_free(now):
                    wait_edge(pe, t, s["x3_made"], t.seen(6))
                    wait_edge(pe, t, s["y4_made"], t.seen(9))
                    wait_edge(pe, t, s["KB_made"], t.seen(3, now))
                    if now:
                        wait_free(pe, s["V1_cp"], 2 * t.seen(4, 1))
                    else:
                        wait_edge(pe, t, s["V1_cp"], 2 * t.seen(4))

                def bank6_free(now):
                    wait_edge(pe, t, s["OT1_cp"], t.seen(6, now))
                    wait_edge(pe, t, s["xqT_cp"], t.seen(9, now))

                scores(0)
                wait_edge(pe, t, s["PT1_cp"], 3 * t.seen(5))
                transpose_whole(0)
                scores(1)
                if t.at(6) is not None or t.at(9) is not None:
                    bank6_free(0)
                    wait_edge(pe, t, s["QT_cp"], NG * t.seen(3))
                    wait_free(pe, s["xT3_cp"], t.seen(2))
                if (b := t.at(6)) is not None:
                    pe.wait_ge(s["O1_cp"], b + 1)
                    T.transpose(PS[:, 6, 0:D], O1[t.par(6)], ident[:, :]).then_inc(s["OT1_mm"], 1)
                if (b := t.at(9)) is not None:
                    pe.wait_ge(s["xq4_made"], b + 1)
                    T.transpose(PS[:, 6, D:D + D // 2].bitcast(BF16), xq4[t.par(9)], identb[:, :]).then_inc(s["xqT_mm"], 1)
                if t.at(5) is not None:
                    bank5_free(0)
                    wait_free(pe, s["y4_made"], t.seen(9))
                transpose_whole(1)
                if t.at(5) is not None:
                    wait_edge(pe, t, s["O1_cp"], t.seen(5))
                attend(0)
                if t.at(4) is not None or t.at(3) is not None:
                    wait_free(pe, s["PT1_cp"], 3 * t.seen(5, 1) - 1)
                    bank5_free(0)
                if (b := t.at(4)) is not None:
                    wait_edge(pe, t, s["ctxc_loaded"], b * 16 + 16)
                    pe.wait_ge(s["ctxr_made"], 2 * b + 2)
                    cx = ctxr[t.par(4)]
                    for c in range(NKB):
                        mm(PS[:, 5, c * D:(c + 1) * D], cx[:, c * P:(c + 1) * P], wv1[:, :])
                    mm(PS[0:RR, 5, NKB * D:(NKB + 1) * D], cx[:, NKB * P:NKB * P + RR], wv1[:, :]).then_inc(s["V1_mm"], 1)
                if (b := t.at(3)) is not None:
                    pe.wait_ge(s["ctxc_loaded"], b * 16 + 16)
                    mm(PS[:, 5, KT_AT:KT_AT + J], wk1[:, :], ctxc[t.par(3)]).then_inc(s["KT_mm"], 1)
                scores(2)
                if t.at(5) is not None:
                    bank6_free(1)
                    wait_free(pe, s["xqT_cp"], t.seen(9, 1))
                    wait_edge(pe, t, s["QT_cp"], NG * t.seen(3))
                    wait_edge(pe, t, s["xT3_cp"], t.seen(2))
                transpose_shared()
                scores(3)
                if (b := t.at(3)) is not None:
                    wait_edge(pe, t, s["xT3_cp"], b + 1)
                    wait_free(pe, s["PT1_cp"], 3 * t.seen(5, 1))
                    bank6_free(1)
                    mm(PS[:, 6, 0:D], wq1[:, :], xT3[t.par(3)]).then_inc(s["QT_mm"], 1)
                attend(1)
                attend(2)
                if t.at(6) is not None or t.at(9) is not None:
                    wait_edge(pe, t, s["PT1_cp"], 3 * t.seen(5, 1) - 1)
                    bank5_free(1)
                if (b := t.at(6)) is not None:
                    wait_edge(pe, t, s["OT1_cp"], b + 1)
                    mm(PS[:, 5, 0:D], OT1[t.par(6)], wo1[:, :]).then_inc(s["Y1_mm"], 1)
                if (b := t.at(9)) is not None:
                    wait_edge(pe, t, s["xqT_cp"], b + 1)
                    mm(PS[:, 5, D:2 * D], xqT4[t.par(9)], kq[:, :]).then_inc(s["y4_mm"], 1)
                if (b := t.at(2)) is not None:
                    pe.wait_ge(s["xn3_made"], b + 1)
                    wait_edge(pe, t, s["PT1_cp"], 3 * t.seen(5, 1))
                    bank6_free(1)
                    wait_free(pe, s["QT_cp"], NG * t.seen(3, 1))
                    wait_edge(pe, t, s["xT3_cp"], b)
                    T.transpose(PS[:, 6, 0:D], xn3[t.par(2)], ident[:, :]).then_inc(s["xT3_mm"], 1)

            for span in c_spans():
                run_steps(pe, NB, *span, step_c, TURN)


EXP_BITS = 0x7F800000
FP8_LEAST = 2.0 ** -6
FP8_ROUND = 1.5 * 2.0 ** 20
FP8_TOP = 3.4028234e38 / 464.5


_INS = {"x": "x", "g_xattn": "g_xattn", "g_ffn": "g_ffn", "gamma": "L0_xattn_gamma", "beta": "L0_xattn_beta",
        "Wout": "L0_xattn_Wout", "Wg": "L0_ffn_Wg", "bg": "L0_ffn_bg", "bias": "L0_ffn_bias",
        "W1": "L0_ffn_W1", "b1": "L0_ffn_b1", "W2": "L0_ffn_W2", "b2": "L0_ffn_b2",
        "Wq1": "L1_xattn_Wq", "bq1": "L1_xattn_bq", "Wk1": "L1_xattn_Wk", "bk1": "L1_xattn_bk",
        "Wv1": "L1_xattn_Wv", "bv1": "L1_xattn_bv", "Wo1": "L1_xattn_Wo", "bo1": "L1_xattn_bo",
        "kernel": "L1_ffn_kernel", "input_scale": "L1_ffn_input_scale", "kernel_scale": "L1_ffn_kernel_scale",
        "ffn_bias": "L1_ffn_bias"}


def kernel(**inputs):
    import numpy as np
    import concourse.bacc as bacc
    from concourse.bass_utils import run_bass_kernel_spmd

    data = {name: np.ascontiguousarray(inputs[full]) for name, full in _INS.items()}
    heads, dh = 8, 64
    wq, wkv = np.asarray(inputs["L0_xattn_Wq"]), np.asarray(inputs["L0_xattn_Wkv"])
    d, inner = wq.shape
    data["WqT"] = np.ascontiguousarray(wq.reshape(d, heads, dh).transpose(2, 1, 0)).reshape(dh, heads * d)
    data["WkT"] = np.ascontiguousarray(wkv[:, :inner].reshape(d, heads, dh).transpose(2, 1, 0)).reshape(dh, heads * d)
    data["Wv"] = np.ascontiguousarray(wkv[:, inner:])
    data["ctxT"] = np.ascontiguousarray(np.asarray(inputs["ctx_1024"]).transpose(0, 2, 1))

    nc = bacc.Bacc("TRN2", target_bir_lowering=False, num_devices=1)
    aps, arrays = {}, {}
    for name, v in data.items():
        arrays[f"in_{name}"] = v
        aps[name] = nc.dram_tensor(f"in_{name}", v.shape, mybir.dt.from_np(v.dtype), kind="ExternalInput").ap()
    out = nc.dram_tensor("out", data["x"].shape, F32, kind="ExternalOutput").ap()
    nb, n, dd = data["x"].shape
    nt = (nb * n + 16 * 127) // 128
    nt += -nt % 16
    xs = [nc.dram_tensor(f"moe_rows{c}", (nt * 128, dd), F32, kind="Internal").ap() for c in range(2)]
    ys = [nc.dram_tensor(f"moe_results{c}", (nt * 128, dd), F32, kind="Internal").ap() for c in range(2)]
    flamingo_two_layers(nc, aps, out, xs, ys)
    r = run_bass_kernel_spmd(nc, [arrays], core_ids=[0])
    return r.results[0]["out"]
```
